# Optimizing a Trainium2 kernel written in Bass

```python
import numpy as np
import jax
import jax.numpy as jnp

def _softmax(x, axis=-1):
    return jax.nn.softmax(x, axis=axis)

def _gelu(x):
    return jax.nn.gelu(x, approximate=True)

def _silu(x):
    return jax.nn.silu(x)

def _sigmoid(x):
    return jax.nn.sigmoid(x)

def _layernorm(x, axis=-1, eps=1e-05):
    m = jnp.mean(x, axis=axis, keepdims=True)
    v = jnp.var(x, axis=axis, keepdims=True)
    return (x - m) / jnp.sqrt(v + eps)

def _scatter_add(tgt, idx, src, axis=0):
    return tgt.at[idx].add(src)

def _segment_sum(src, seg, n):
    return jax.ops.segment_sum(src, seg, n)
kernel_name = 'mk_early_fusion_d1_tok_img768_r4_d27c3e'

def setup_inputs(seed: int=0):
    np.random.seed(seed)
    _w = jnp.asarray

    def _rec_inputs():
        import jax
        import jax.numpy as jnp
        _rk = jax.random.key(seed)
        x = -0.000356955 + 1 * jax.random.normal(jax.random.fold_in(_rk, 1), (32, 3, 224, 224), jnp.float32)
        txt = -6.28402e-05 + 0.577654 * jax.random.normal(jax.random.fold_in(_rk, 2), (32, 128, 192), jnp.float32)
        return (x, txt)
    x, txt = _rec_inputs()

    def _L0_tok_setup():
        import jax, jax.numpy as jnp
        import numpy as np
        PATCH = 16
        EMBED = 192
        IN_DIM = PATCH * PATCH * 3

        def extract_patches(x, p):
            B, C, H, Wd = x.shape
            h, w = (H // p, Wd // p)
            xr = x.reshape(B, C, h, p, w, p)
            xr = xr.transpose(0, 2, 4, 3, 5, 1)
            return xr.reshape(B, h * w, p * p * C)
        key = jax.random.key(seed)
        kx, kw, kb = jax.random.split(key, 3)
        x = jax.random.normal(kx, (128, 3, 224, 224), dtype=jnp.float32)
        bound = 1.0 / np.sqrt(IN_DIM)
        W = jax.random.uniform(kw, (EMBED, IN_DIM), jnp.float32, -bound, bound)
        b = jax.random.uniform(kb, (EMBED,), jnp.float32, -bound, bound)
        return {'x': x, 'W': W, 'b': b}
    _L0_tok_all = _L0_tok_setup()
    _L0_tok_in = {k: v for k, v in _L0_tok_all.items() if k in ('W', 'b')}
    del _L0_tok_all

    def _L0_attn_setup():
        import jax, jax.numpy as jnp
        import numpy as np
        BLOCK_SIZE = 64
        N_EMBD = 192
        HEAD_SIZE = 192

        def _rope_tables(T, dim, theta0=10000.0):
            j = jnp.arange(dim // 2, dtype=jnp.float32)
            theta = jnp.float32(theta0) ** (-2.0 * j / jnp.float32(dim))
            ang = jnp.arange(T, dtype=jnp.float32)[:, None] * theta[None, :]
            return (jnp.cos(ang), jnp.sin(ang))

        def _apply_rope(t, cos, sin):
            B, T, D = t.shape
            tr = t.reshape(B, T, D // 2, 2)
            re, im = (tr[..., 0], tr[..., 1])
            out_re = re * cos[None] - im * sin[None]
            out_im = re * sin[None] + im * cos[None]
            return jnp.stack([out_re, out_im], axis=-1).reshape(B, T, D)
        key = jax.random.key(seed)
        k1, k2, k3, k4 = jax.random.split(key, 4)
        B, T = (128, BLOCK_SIZE)
        x = jax.random.normal(k1, (B, T, N_EMBD), dtype=jnp.float32)
        Wq = jax.random.normal(k2, (N_EMBD, HEAD_SIZE), dtype=jnp.float32) * 0.02
        Wk = jax.random.normal(k3, (N_EMBD, HEAD_SIZE), dtype=jnp.float32) * 0.02
        Wv = jax.random.normal(k4, (N_EMBD, HEAD_SIZE), dtype=jnp.float32) * 0.02
        return {'x': x, 'Wq': Wq, 'Wk': Wk, 'Wv': Wv}
    _L0_attn_all = _L0_attn_setup()
    _L0_attn_in = {k: v for k, v in _L0_attn_all.items() if k in ('Wq', 'Wk', 'Wv')}
    del _L0_attn_all

    def _L0_ffn_setup():
        import jax, jax.numpy as jnp
        import numpy as np
        B, N, D, H, E, HID, TOPK = (8, 197, 192, 12, 8, 768, 2)

        def _layernorm(x, w, b, eps=1e-05):
            mu = jnp.mean(x, axis=-1, keepdims=True)
            var = jnp.mean((x - mu) ** 2, axis=-1, keepdims=True)
            return (x - mu) * jax.lax.rsqrt(var + eps) * w + b
        key = jax.random.key(seed)
        ks = jax.random.split(key, 8)
        s = 0.02
        return {'x': jax.random.normal(ks[0], (B, N, D), jnp.float32), 'norm1_w': jnp.ones((D,), jnp.float32), 'norm1_b': jnp.zeros((D,), jnp.float32), 'qkv_w': jax.random.normal(ks[1], (3 * D, D), jnp.float32) * s, 'qkv_b': jnp.zeros((3 * D,), jnp.float32), 'proj_w': jax.random.normal(ks[2], (D, D), jnp.float32) * s, 'proj_b': jnp.zeros((D,), jnp.float32), 'norm2_w': jnp.ones((D,), jnp.float32), 'norm2_b': jnp.zeros((D,), jnp.float32), 'w_gate': jax.random.normal(ks[3], (D, E), jnp.float32) * s, 'W1': jax.random.normal(ks[4], (E, D, HID), jnp.float32) * s, 'b1': jnp.zeros((E, HID), jnp.float32), 'W2': jax.random.normal(ks[5], (E, HID, D), jnp.float32) * s, 'b2': jnp.zeros((E, D), jnp.float32)}
    _L0_ffn_all = _L0_ffn_setup()
    _L0_ffn_in = {k: v for k, v in _L0_ffn_all.items() if k in ('norm1_w', 'norm1_b', 'qkv_w', 'qkv_b', 'proj_w', 'proj_b', 'norm2_w', 'norm2_b', 'w_gate', 'W1', 'b1', 'W2', 'b2')}
    del _L0_ffn_all
    return {'x': x, 'txt': txt, 'L0_tok_W': _L0_tok_in['W'], 'L0_tok_b': _L0_tok_in['b'], 'L0_attn_Wq': _L0_attn_in['Wq'], 'L0_attn_Wk': _L0_attn_in['Wk'], 'L0_attn_Wv': _L0_attn_in['Wv'], 'L0_ffn_norm1_w': _L0_ffn_in['norm1_w'], 'L0_ffn_norm1_b': _L0_ffn_in['norm1_b'], 'L0_ffn_qkv_w': _L0_ffn_in['qkv_w'], 'L0_ffn_qkv_b': _L0_ffn_in['qkv_b'], 'L0_ffn_proj_w': _L0_ffn_in['proj_w'], 'L0_ffn_proj_b': _L0_ffn_in['proj_b'], 'L0_ffn_norm2_w': _L0_ffn_in['norm2_w'], 'L0_ffn_norm2_b': _L0_ffn_in['norm2_b'], 'L0_ffn_w_gate': _L0_ffn_in['w_gate'], 'L0_ffn_W1': _L0_ffn_in['W1'], 'L0_ffn_b1': _L0_ffn_in['b1'], 'L0_ffn_W2': _L0_ffn_in['W2'], 'L0_ffn_b2': _L0_ffn_in['b2']}

def reference(x, txt, L0_tok_W, L0_tok_b, L0_attn_Wq, L0_attn_Wk, L0_attn_Wv, L0_ffn_norm1_w, L0_ffn_norm1_b, L0_ffn_qkv_w, L0_ffn_qkv_b, L0_ffn_proj_w, L0_ffn_proj_b, L0_ffn_norm2_w, L0_ffn_norm2_b, L0_ffn_w_gate, L0_ffn_W1, L0_ffn_b1, L0_ffn_W2, L0_ffn_b2):
    import jax
    import jax.numpy as jnp

    def _L0_tok_ref(x, W, b):
        import jax, jax.numpy as jnp
        import numpy as np
        PATCH = 16
        EMBED = 192
        IN_DIM = PATCH * PATCH * 3

        def extract_patches(x, p):
            B, C, H, Wd = x.shape
            h, w = (H // p, Wd // p)
            xr = x.reshape(B, C, h, p, w, p)
            xr = xr.transpose(0, 2, 4, 3, 5, 1)
            return xr.reshape(B, h * w, p * p * C)
        patches = extract_patches(x, PATCH)
        return jnp.einsum('bnd,ed->bne', patches, W) + b

    def _L0_attn_ref(x, Wq, Wk, Wv):
        import jax, jax.numpy as jnp
        import numpy as np
        BLOCK_SIZE = 64
        N_EMBD = 192
        HEAD_SIZE = 192

        def _rope_tables(T, dim, theta0=10000.0):
            j = jnp.arange(dim // 2, dtype=jnp.float32)
            theta = jnp.float32(theta0) ** (-2.0 * j / jnp.float32(dim))
            ang = jnp.arange(T, dtype=jnp.float32)[:, None] * theta[None, :]
            return (jnp.cos(ang), jnp.sin(ang))

        def _apply_rope(t, cos, sin):
            B, T, D = t.shape
            tr = t.reshape(B, T, D // 2, 2)
            re, im = (tr[..., 0], tr[..., 1])
            out_re = re * cos[None] - im * sin[None]
            out_im = re * sin[None] + im * cos[None]
            return jnp.stack([out_re, out_im], axis=-1).reshape(B, T, D)
        B, T, C = x.shape
        q = x @ Wq
        k = x @ Wk
        v = x @ Wv
        cos, sin = _rope_tables(T, HEAD_SIZE)
        q = _apply_rope(q, cos, sin)
        k = _apply_rope(k, cos, sin)
        scale = jnp.float32(HEAD_SIZE) ** (-0.5)
        wei = jnp.einsum('bqd,bkd->bqk', q, k) * scale
        causal = jnp.tril(jnp.ones((T, T), dtype=bool))
        wei = jnp.where(causal[None], wei, -jnp.inf)
        wei = jax.nn.softmax(wei, axis=-1)
        out = jnp.einsum('bqk,bkd->bqd', wei, v)
        return out

    def _L0_ffn_ref(x, norm1_w, norm1_b, qkv_w, qkv_b, proj_w, proj_b, norm2_w, norm2_b, w_gate, W1, b1, W2, b2):
        import jax, jax.numpy as jnp
        import numpy as np
        B, N, D, H, E, HID, TOPK = (8, 197, 192, 12, 8, 768, 2)

        def _layernorm(x, w, b, eps=1e-05):
            mu = jnp.mean(x, axis=-1, keepdims=True)
            var = jnp.mean((x - mu) ** 2, axis=-1, keepdims=True)
            return (x - mu) * jax.lax.rsqrt(var + eps) * w + b
        Bx, Nx, C = x.shape
        hd = C // H
        scale = hd ** (-0.5)
        xn = _layernorm(x, norm1_w, norm1_b)
        qkv = (xn @ qkv_w.T + qkv_b).reshape(Bx, Nx, 3, H, hd).transpose(2, 0, 3, 1, 4)
        q, k, v = (qkv[0], qkv[1], qkv[2])
        attn = jax.nn.softmax(jnp.einsum('bhqd,bhkd->bhqk', q, k) * scale, axis=-1)
        o = jnp.einsum('bhqk,bhkd->bqhd', attn, v).reshape(Bx, Nx, C)
        x = x + (o @ proj_w.T + proj_b)
        xn2 = _layernorm(x, norm2_w, norm2_b).reshape(-1, C)
        T = xn2.shape[0]
        logits = xn2 @ w_gate
        top_vals, top_idx = jax.lax.top_k(logits, TOPK)
        gates = jax.nn.softmax(top_vals, axis=-1)
        gates_full = jnp.zeros((T, E), xn2.dtype).at[jnp.arange(T)[:, None], top_idx].add(gates)

        def body(acc, p):
            w1, bb1, w2, bb2, g = p
            h = jax.nn.gelu(xn2 @ w1 + bb1, approximate=False)
            return (acc + g[:, None] * (h @ w2 + bb2), None)
        moe_out, _ = jax.lax.scan(body, jnp.zeros_like(xn2), (W1, b1, W2, b2, gates_full.T))
        return x + moe_out.reshape(Bx, Nx, C)
    h = _L0_tok_ref(x, L0_tok_W, L0_tok_b)
    h = jnp.concatenate([h, txt], axis=1)
    h = h + _L0_attn_ref(_layernorm(h, axis=-1), L0_attn_Wq, L0_attn_Wk, L0_attn_Wv)
    h = h + _L0_ffn_ref(_layernorm(h, axis=-1), L0_ffn_norm1_w, L0_ffn_norm1_b, L0_ffn_qkv_w, L0_ffn_qkv_b, L0_ffn_proj_w, L0_ffn_proj_b, L0_ffn_norm2_w, L0_ffn_norm2_b, L0_ffn_w_gate, L0_ffn_W1, L0_ffn_b1, L0_ffn_W2, L0_ffn_b2)
    return h

_drawn_inputs = setup_inputs


def setup_inputs(seed=0):
    import zlib

    import numpy as np

    out = dict(_drawn_inputs(seed))
    spreads = {'L0_ffn_norm1_w': (1.0, 0.6),
     'L0_ffn_norm1_b': (0.0, 0.8),
     'L0_ffn_qkv_b': (0.0, 0.389),
     'L0_ffn_proj_b': (0.0, 0.1),
     'L0_ffn_norm2_w': (1.0, 0.573),
     'L0_ffn_norm2_b': (0.0, 0.43),
     'L0_ffn_b1': (0.0, 0.576),
     'L0_ffn_b2': (0.0, 0.1)}
    factors = {'L0_attn_Wq': 8.0, 'L0_attn_Wk': 8.0, 'L0_ffn_qkv_w': 7.56}
    for name, (base, spread) in spreads.items():
        noise = np.random.default_rng([zlib.crc32(name.encode()), seed]).standard_normal(out[name].shape)
        drawn = base * np.exp(spread * noise) if base else spread * noise
        out[name] = jnp.asarray(drawn.astype(out[name].dtype))
    for name, factor in factors.items():
        out[name] = (out[name] * factor).astype(out[name].dtype)
    return out
```

```python
from contextlib import ExitStack

import concourse.bass as bass
from concourse import mybir

ALU = mybir.AluOpType
ACT = mybir.ActivationFunctionType
F32 = mybir.dt.float32
F16 = mybir.dt.float16
BF16 = mybir.dt.bfloat16
AX = mybir.AxisListType

B, CH, IMG, PATCH = 32, 3, 224, 16
D, HID, E, HEADS = 192, 768, 8, 12
HD = D // HEADS
GRID = IMG // PATCH
NPATCH = GRID * GRID
NTEXT = 128
T = NPATCH + NTEXT
TP = 108
NT = T // TP
PT1 = NPATCH - TP
KA, KB = 128, D - 128
RH = D // 2
NC = HID // 128
IMROWS = CH * PATCH
CHUNKS = 7
CW = GRID * IMG // CHUNKS
WSC = 64.0
EPS = 1e-5
SCALE1 = float(D) ** -0.5
SCALE2 = float(HD) ** -0.5

C_ID, C_M64, C_MQ, C_MK, C_M48 = 0, 128, 129, 130, 131
C_COS, C_SIN = 132, 132 + T
C_CAP = C_SIN + T
C_REV = C_CAP + TP
C_POW = C_REV + NT * E
C_EPS = C_POW + NT
C_N = C_EPS + NT

XIN = 96
DVE_STEPS = 43
SP_SIGNALS = dict(xin0=4 * XIN, xin1=3 * XIN, txt_in=32, out_done=16)
PE_SIGNALS = dict(emb_full=2, tr_full=6, qk1_full=4, v1_full=3, s1_full=3, p1t_full=3, pv1_full=3, qk2_full=12,
                  v2_full=3, s_full=36, mt_full=1, st_full=36, pv_done=12, pj_full=3, gate_full=1, gt_full=1,
                  b2_full=3, w1_full=48, o_full=24)
ACT_SIGNALS = dict(img_hi=7, tr_hi=6, rope_hi=4, v1_hi=3, p1_ready=3, p1t_hi=3, qk2_m=12, v2_hi=3, st_exp=36, o_hi=3,
                   gate_tanh=1, gelu=48)
DVE_SIGNALS = dict(img_split=7, emb_evac=2, n_ready=3, tr_lo=6, rope_re=2, rope_mul=2, v1_lo=3, s1_evac=3, m1_ready=1,
                   p1t_lo=3, pv1_evac=3, xf_ready=1, qk2_done=12, v2_lo=3, s_max=36, mt_done=1, pt_lo=36, pv_norm=3,
                   o_lo=3, x1_done=3, gate_evac=1, gate_tanh_in=1, g_ready=1, gt_done=1, r_ready=3, h_lo=48, acc=24,
                   ln_var=4, dve_step=DVE_STEPS)
POOL_SIGNALS = dict(rope_sum=4, rope_lo=4, xfb_ready=1, pt_hi=36, r_sum=1, ln_eps=4, ln_rstd=4, h_hi=48)
PER = SP_SIGNALS | PE_SIGNALS | ACT_SIGNALS | DVE_SIGNALS | POOL_SIGNALS

USES = []


def plan_uses():
    turn = [0]

    def use(step, i, sem, k, bank=None):
        if bank is None:
            bank = turn[0] % 3
            turn[0] += 1
        USES.append(((step, i), bank, sem, k))

    use("emb", 0, "emb_evac", 1)
    use("emb", 1, "emb_evac", 2)
    use("tr", 0, "tr_lo", 1)
    use("tr", 1, "tr_lo", 2)
    for i in range(4):
        use("qk1", i, "rope_mul" if i % 2 else "rope_re", i // 2 + 1)
    for i in range(3):
        use("v1", i, "v1_lo", i + 1)
    for i in range(3):
        use("s1", i, "s1_evac", i + 1)
    for i in range(3):
        use("p1t", i, "p1t_lo", i + 1)
    for i in range(3):
        use("pv1", i, "pv1_evac", i + 1)
    use("tr", 2, "tr_lo", 3)
    use("tr", 3, "tr_lo", 4)
    for i in range(12):
        use("qk2", i, "qk2_done", i + 1)
    for i in range(3):
        use("v2", i, "v2_lo", i + 1)
    for i in range(36):
        use("s", i, "s_max", i + 1)
    use("mt", 0, "mt_done", 1)
    for h in range(HEADS):
        for kt in range(3):
            use("st", 3 * h + kt, "st_exp", 3 * h + kt + 1, bank=(3 * h + kt) % 2)
        if h >= 1 and (h - 1) % 4 == 0:
            use("pv", (h - 1) // 4, "pv_norm", (h - 1) // 4 + 1, bank=2)
    for i in range(3):
        use("pj", i, "x1_done", i + 1)
    use("tr", 4, "tr_lo", 5)
    use("tr", 5, "tr_lo", 6)
    use("gate", 0, "gate_evac", 1)
    use("gt", 0, "gt_done", 1)
    for i in range(3):
        use("b2", i, "r_ready", i + 1)


plan_uses()
BANK = {key: bank for key, bank, _, _ in USES}
LAST = {bank: (sem, k) for _, bank, sem, k in USES}
BEFORE = {}
_seen = {}
for _key, _bank, _sem, _k in USES:
    BEFORE[_key] = _seen.get(_bank)
    _seen[_bank] = (_sem, _k)

PIECES = ([("img", k) for k in range(CHUNKS)] + [("emb", 0), None, None, ("tr", 0), None, ("qk1", 0), ("qk1", 1),
          ("v1", 0), ("s1", 0), None, None, ("p1t", 0), None, ("pv1", 0), None, None, None, ("tr", 1), None]
          + [("qk2", i) for i in range(6)] + [("v2", 0)] + [("s", h) for h in range(HEADS)] + [None, ("mt", 0), None,
          ("att2", 0), ("pj", 0)])
MAIN = [("W1", e, c) for e in range(1) for c in range(NC)]
for _e in range(1, E):
    MAIN += [("W1", _e, c) for c in range(NC)]
    if _e < E - 1:
        MAIN += [("W2", _e - 1, t) for t in range(NT)]
TAIL = [("W2", E - 2, 0), ("tr", 2), ("W2", E - 2, 1), ("W2", E - 2, 2), ("gate", 0), ("W2", E - 1, 0), ("W2", E - 1, 1),
        ("gt", 0), ("W2", E - 1, 2), ("b2", 0)]


def order(experts, attention):
    out, at = [], 0
    for n, unit in enumerate(MAIN):
        if experts:
            out.append(unit)
        upto = (n + 1) * len(PIECES) // len(MAIN)
        if attention:
            out += [p for p in PIECES[at:upto] if p]
        at = upto
    for step in TAIL:
        if experts if step[0][0] == "W" else attention:
            out.append(step)
    return out


def build_program(nc, x, txt, tok_w, tok_b, wq, wk, wv, n1w, n1b, qkv_w, qkv_b, proj_w, proj_b, n2w, n2b,
                  w_gate, w1, b1, w2, b2, const, out):
    with ExitStack() as ctx:
        def sb(name, shape, dt):
            return ctx.enter_context(nc.sbuf_tensor(name, shape, dt))

        def sem(name):
            return ctx.enter_context(nc.semaphore(name))

        W1a = sb("W1a", [128, E, 2, HID], F16)
        W1b = sb("W1b", [128, E, 2, HID], F16)
        W2s = sb("W2s", [128, E, NC, 2, D], F16)
        tokW = sb("tokW", [128, 2, PATCH, D], F16)
        attWa = sb("attWa", [128, 2, 3 * D], F16)
        attWb = sb("attWb", [128, 2, 3 * D], F16)
        qkvWa = sb("qkvWa", [128, 2, 12 * 128 + D], F16)
        qkvWb = sb("qkvWb", [128, 2, 12 * 128 + D], F16)
        projW = sb("projW", [128, 2, 3, D], F16)
        gateWa = sb("gateWa", [128, 2, E], F16)
        gateWb = sb("gateWb", [128, 2, E], F16)
        b2s = sb("b2s", [E, D], F32)
        b1s = sb("b1s", [128, E, NC], F32)
        tokb = sb("tokb", [TP, D], F32)
        projb = sb("projb", [TP, D], F32)
        norms = sb("norms", [TP, 4, D], F32)
        qkb = sb("qkb", [128, 12], F32)
        qkmb = sb("qkmb", [128, 12], F32)
        vb = sb("vb", [128, 3], F32)
        cst = sb("cst", [128, C_N], F32)
        identb = sb("identb", [HEADS, HEADS], BF16)
        ident = cst[:, C_ID:C_ID + 128]
        m64, mq, mk, m48 = (cst[:, c:c + 1] for c in (C_M64, C_MQ, C_MK, C_M48))
        cos, sin = cst[0:RH, C_COS:C_COS + T], cst[0:RH, C_SIN:C_SIN + T]
        cap = cst[0:TP, C_CAP:C_CAP + TP]
        rev = cst[0:TP, C_REV:C_REV + NT * E].rearrange("p (t e) -> p t e", t=NT)

        ximg = sb("ximg", [128, 2, CW], F32)
        xmask = sb("xmask", [128, CW], F16)
        XS = sb("XS", [128, CHUNKS * CW], F16)
        Hres = sb("Hres", [TP, NT, D], F32)
        Nrm = sb("Nrm", [TP, NT, D], F32)
        XF = sb("XF", [TP, NT, D], F32)
        R = sb("R", [TP, NT, D], F32)
        ACC = sb("ACC", [TP, NT, D], F32)
        XT = sb("XT", [128, 3, T], F16)
        XM = sb("XM", [128, 3, T], F16)
        QK = sb("QK", [128, 12, T], F16)
        QK1 = QK[0:RH, 0:8, :].rearrange("p (i s) t -> p i s t", s=2)
        V1 = sb("V1", [TP, 2, NT, D], F16)
        WS = sb("WS", [128, 4 * T + 6 * T], F32)
        tmp = WS[0:RH, 0:8 * T].rearrange("p (i t) -> p i t", t=T)
        S1 = WS[0:TP, 0:3 * T].rearrange("p (i t) -> p i t", t=T)
        Pr = WS[0:TP, 0:4 * T].rearrange("p (i t) -> p i t", t=T)
        PT = WS[0:TP, 4 * T:10 * T].bitcast(F16).rearrange("p (a s k t) -> p a s k t", a=2, s=2, k=3)
        qm = sb("qm", [128, 2, T], F16)
        trm = qm[:, 0, :]
        Vp = sb("Vp", [TP, 2, NT, HEADS, 32], F16)
        mx = sb("mx", [TP, NT, HEADS], F32)
        nmT = sb("nmT", [HEADS, T], BF16)
        rsq = sb("rsq", [128, T], F32)
        rsi = sb("rsi", [128, T], F32)
        Os = sb("Os", [128, 2, 3, T], F16)
        st6 = sb("st6", [TP, NT, 6], F32)
        mv = sb("mv", [TP, NT, 2], F32)
        rstd = sb("rstd", [TP, NT], F32)
        veps = sb("veps", [TP, NT], F32)
        nm1 = sb("nm1", [TP, 4, NT], F32)
        rt = sb("rt", [TP, 8, NT, E], F32)
        rs = sb("rs", [TP, 8, NT], F32)
        G = sb("G", [TP, NT, E], F32)
        Gs = sb("Gs", [TP, NT, E], F32)
        GT = rsi[0:E, :]

        h32 = sb("h32", [128, 3, T], F32)
        Hs = sb("Hs", [128, 2, 2, NC, T], F16)

        M = [ctx.enter_context(nc.psum_tensor(f"M{i}", [128, 512], F32)) for i in range(3)]
        O = [ctx.enter_context(nc.psum_tensor(f"O{i}", [128, 512], F32)) for i in range(2)]
        TB = [ctx.enter_context(nc.psum_tensor(f"TB{i}", [128, 512], F32)) for i in range(3)]

        S = {name: sem(name) for name in PER}
        c_in, c_set = sem("c_in"), sem("c_set")
        stg_in = [sem(f"stg_in{i}") for i in range(4)]
        stg_hi, stg_lo = sem("stg_hi"), sem("stg_lo")
        big_in, prep_full, prep_hi, prep_lo = sem("big_in"), sem("prep_full"), sem("prep_hi"), sem("prep_lo")
        passed = sem("passed")
        pad_set, tok_dup = sem("pad_set"), sem("tok_dup")

        def due(name, b, k):
            return (b + 1) * PER[name] + k

        def one_ahead(eng, signals):
            for name, count in signals.items():
                eng.sem_inc(S[name], count)

        def apart(eng):
            eng.sem_inc(passed, 1)

        def bank_read(b, step, i):
            before = BEFORE[(step, i)]
            if before:
                return S[before[0]], due(before[0], b, before[1])
            last, k = LAST[BANK[(step, i)]]
            return S[last], due(last, b - 1, k)

        def bank(step, i):
            return TB[BANK[(step, i)]]

        big = Hs[:, :, :, :, :].rearrange("p a s c t -> p (a s c t)").bitcast(F32)
        tokS = big[0:96, 0:2 * 768].rearrange("p (a n) -> p a n", a=2)
        qkvS = big[0:96, 1536:1536 + 6 * D].rearrange("p (a n) -> p a n", a=6)
        projS = big[0:96, 2688:2688 + 768].rearrange("p (a g n) -> p a g n", a=2, g=3)
        tokD = XS[:, :].bitcast(F32)[0:96, 0:768].rearrange("p (s n m) -> p s n m", s=2, n=4)
        slot = [WS[:, 768 * i:768 * (i + 1)] for i in range(4)]
        stages = []

        def flat(ap):
            return ap

        for name, w, c0 in (("q", wq, 0), ("k", wk, D)):
            for half in range(2):
                for dst, rows in ((attWa, None), (attWb, 64)):
                    stages.append((w, rows, D, dst, c0 + half * RH, half, 1.0))
        for dst, rows in ((attWa, None), (attWb, 64)):
            stages.append((wv, rows, D, dst, 2 * D, None, 1.0))
        for dst, rows in ((gateWa, None), (gateWb, 64)):
            stages.append((w_gate, rows, E, dst, 0, None, WSC))
        for e in range(E):
            stages.append((w1[e], None, HID, W1a[:, e], 0, None, WSC))
            stages.append((w1[e], 64, HID, W1b[:, e], 0, None, WSC))
            for c in range(0, NC, 3):
                stages.append((w2[e], ("w2", c), 3 * D, W2s[:, e, c:c + 3], 0, "w2", WSC))

        def stage_views(i):
            src, rows, cols, dst, c0, pick, scale = stages[i]
            s = slot[i % 4]
            if pick == "w2":
                v = s[:, 0:cols].rearrange("p (c n) -> p c n", c=3)
                return v, dst[:, :, 0, :], dst[:, :, 1, :], scale
            if pick is None:
                return s[:, 0:cols], dst[:, 0, c0:c0 + cols], dst[:, 1, c0:c0 + cols], scale
            v = s[:, 0:cols].rearrange("p (j r) -> p j r", r=2)[:, :, pick]
            return v, dst[:, 0, c0:c0 + RH], dst[:, 1, c0:c0 + RH], scale

        preps = []
        for pw in range(0, PATCH, 2):
            preps.append(("tok", pw, 96, 2 * D, tokW[0:96, 0, pw:pw + 2, :], tokW[0:96, 1, pw:pw + 2, :], WSC))
        def four(w, sel, i):
            return w[:, sel, 768 * i:768 * i + 768].rearrange("p (h a d) -> p h a d", h=HEADS, a=4)

        for part, dst in (("a", qkvWa), ("b", qkvWb)):
            for i in range(2):
                preps.append(("qkv" + part, i, 128, D, four(dst, 0, i), four(dst, 1, i), 1.0))
            preps.append(("qkv" + part, 2, 128, D, dst[:, 0, 1536:], dst[:, 1, 1536:], 1.0))
        for half in range(2):
            cols = slice(96 * half, 96 * half + 96)
            preps.append(("proj", half, 128, 288, projW[:, 0, :, cols], projW[:, 1, :, cols], WSC))

        def prep_view(i):
            kind, at, rows, cols, hi, lo, scale = preps[i]
            v = TB[i % 3][0:rows, 0:cols]
            if kind == "tok":
                v = v.rearrange("p (w n) -> p w n", w=2)
            if kind == "proj":
                v = v.rearrange("p (g n) -> p g n", g=3)
            if kind[:3] == "qkv" and at < 2:
                v = v.rearrange("p (h a d) -> p h a d", h=HEADS, a=1).to_broadcast([128, HEADS, 4, HD])
            return v, hi, lo, scale

        N_C = [0]
        block = ctx.enter_context(nc.Block())

        @block.sync
        def _(sp):
            def const_in(dst, src):
                sp.dma_start(dst, src, allow_slow_non_contiguous=True).then_inc(c_in, 16)
                N_C[0] += 16

            const_in(cst[:, :], const)
            sp.wait_ge(pad_set, 2)
            sp.dma_start(tokS, tok_w.rearrange("(a p) n -> p a n", p=96)).then_inc(big_in, 16)
            sp.dma_start(qkvS, qkv_w.rearrange("(a p) n -> p a n", p=96)).then_inc(big_in, 16)
            for a in range(2):
                for g in range(3):
                    sp.dma_start(projS[:, a, g, :].rearrange("p (j r) -> p j r", r=32)[:, :, 0:HD],
                                 proj_w[96 * a:96 * a + 96, 64 * g:64 * g + 64].rearrange("p (j r) -> p j r", r=HD)
                                 ).then_inc(big_in, 16)
            const_in(tokb[:, :], tok_b.rearrange("(a n) -> a n", a=1).to_broadcast([TP, D]))
            const_in(projb[:, :], proj_b.rearrange("(a n) -> a n", a=1).to_broadcast([TP, D]))
            for i, v in enumerate((n1w, n1b, n2w, n2b)):
                const_in(norms[:, i, :], v.rearrange("(a n) -> a n", a=1).to_broadcast([TP, D]))
            for hh in range(2):
                for c in range(4):
                    const_in(qkb[64 * hh + 16 * c:64 * hh + 16 * c + 16, :],
                             qkv_b[0:2 * D].rearrange("(i h d) -> h d i", h=2, d=HD)[hh])
            for j in range(4):
                const_in(vb[32 * j:32 * j + HD, :], qkv_b[2 * D:3 * D].rearrange("(g j d) -> j d g", j=4, d=HD)[j])
            const_in(b2s[:, :], b2)
            for e in range(E):
                const_in(b1s[:, e, :], b1[e].rearrange("(c p) -> p c", p=128))
            for i, (src, rows, cols, dst, c0, pick, scale) in enumerate(stages):
                if i >= 4:
                    sp.wait_ge(stg_lo, i - 3)
                s = slot[i % 4]
                if pick == "w2":
                    c = rows[1]
                    sp.dma_start(s[:, 0:cols].rearrange("p (c n) -> p c n", c=3),
                                 src[128 * c:128 * (c + 3), :].rearrange("(c p) n -> p c n", p=128)
                                 ).then_inc(stg_in[i % 4], 32)
                elif rows is None:
                    sp.dma_start(s[:, 0:cols], src[0:128, :]).then_inc(stg_in[i % 4], 32)
                else:
                    for r in range(2):
                        sp.dma_start(s[64 * r:64 * r + 64, 0:cols], src[128:D, :]).then_inc(stg_in[i % 4], 16)

            def image(b, k):
                name = f"xin{k % 2}"
                sp.wait_ge(S["img_split"], due("img_split", b, k - 1 if k >= 2 else 0))
                rows = x[b].rearrange("c (h r) w -> c r h w", r=PATCH)
                for s in range(2):
                    for c in range(CH):
                        p = IMROWS * s + PATCH * c
                        sp.dma_start(ximg[p:p + PATCH, k % 2, :].rearrange("r (h w) -> r h w", h=2),
                                     rows[c, :, 2 * k:2 * k + 2, :]).then_inc(S[name], 16)

            def text(b):
                sp.wait_ge(S["r_sum"], due("r_sum", b - 1, 1))
                sp.dma_start(Hres[PT1:TP, 1, :], txt[b, 0:TP - PT1, :]).then_inc(S["txt_in"], 16)
                sp.dma_start(Hres[:, 2, :], txt[b, TP - PT1:NTEXT, :]).then_inc(S["txt_in"], 16)

            def store(m):
                sp.wait_ge(S["acc"], due("acc", m, 24))
                sp.dma_start(out[m].rearrange("(t p) d -> p t d", p=TP), ACC[:, :, :]).then_inc(S["out_done"], 16)

            def turn(b, m):
                image(b, 0)
                image(b, 1)
                text(b)
                for k in range(2, CHUNKS):
                    image(b, k)
                if m is not None:
                    store(m)

            one_ahead(sp, SP_SIGNALS)
            turn(0, None)
            with sp.Fori(1, B) as b:
                turn(b, b - 1)
            store(B - 1)
            sp.wait_ge(S["out_done"], due("out_done", B - 1, 16))

        @block.gpsimd
        def _(pool):
            nc.gpsimd.memset(big[0:96, 2688:3456], 0.0).then_inc(pad_set, 1)
            nc.gpsimd.memset(vb[:, :], 0.0).then_inc(pad_set, 1)
            nc.gpsimd.memset(Vp[:, 0, :, :, :], 1.0).then_inc(pad_set, 1)
            nc.gpsimd.memset(Vp[:, 1, :, :, :], 0.0).then_inc(pad_set, 1)
            one_ahead(pool, POOL_SIGNALS)
            pool.wait_ge(big_in, 128)
            for i in range(PATCH // 2):
                if i >= 2:
                    pool.wait_ge(prep_full, i - 1)
                for w in range(2):
                    for a in range(2):
                        src = tokS[:, a, :].rearrange("p (r w c) -> p w c r", r=PATCH, w=PATCH)[:, 2 * i + w]
                        src = src.rearrange("p (s c) r -> p s c r", s=1).to_broadcast([96, 2, CH, PATCH])
                        last = nc.gpsimd.tensor_copy(
                            tokD[:, i % 2, 2 * w + a, :].rearrange("p (s c r) -> p s c r", s=2, c=CH), src)
                last.then_inc(tok_dup, 1)

            def qk1(b, i):
                pool.wait_ge(S["rope_mul"], due("rope_mul", b, i + 1))
                t0, t1, t2, t3 = (tmp[:, 4 * i + j, :] for j in range(4))
                nc.gpsimd.tensor_tensor(t0, t0, t2, ALU.subtract).then_inc(S["rope_sum"], 1)
                nc.gpsimd.tensor_tensor(t1, t1, t3, ALU.add).then_inc(S["rope_sum"], 1)
                for j, t in enumerate((t0, t1)):
                    pool.wait_ge(S["rope_hi"], due("rope_hi", b, 2 * i + j + 1))
                    nc.gpsimd.tensor_tensor(QK1[:, 2 * i + j, 1, :], t, QK1[:, 2 * i + j, 0, :],
                                            ALU.subtract).then_inc(S["rope_lo"], 1)

            def inv_std(b, i):
                pool.wait_ge(S["ln_var"], due("ln_var", b, i + 1))
                nc.gpsimd.tensor_tensor(veps[:, :], mv[:, :, 1], cst[0:TP, C_EPS:C_EPS + NT],
                                        ALU.add).then_inc(S["ln_eps"], 1)
                pool.wait_ge(S["ln_eps"], due("ln_eps", b, i + 1))
                nc.gpsimd.tensor_tensor(rstd[:, :], veps[:, :], cst[0:TP, C_POW:C_POW + NT],
                                        ALU.pow).then_inc(S["ln_rstd"], 1)

            def pv1(b):
                inv_std(b, 1)
                pool.wait_ge(S["xf_ready"], due("xf_ready", b, 1))
                nc.gpsimd.tensor_tensor(R[:, :, :], XF[:, :, :],
                                        projb[:, :].rearrange("p (a n) -> p a n", a=1).to_broadcast([TP, NT, D]),
                                        ALU.add).then_inc(S["xfb_ready"], 1)
                inv_std(b, 2)

            def att2(b):
                for h in range(HEADS):
                    if h < 2:
                        pool.wait_ge(S["pv_done"], due("pv_done", b - 1, HEADS - 1 + h))
                    else:
                        pool.wait_ge(S["pv_done"], due("pv_done", b, h - 1))
                    for kt in range(3):
                        n = 3 * h + kt
                        pool.wait_ge(S["st_exp"], due("st_exp", b, n + 1))
                        apart(pool)
                        nc.gpsimd.tensor_copy(PT[:, h % 2, 0, kt, :], Pr[:, n % 4, :]).then_inc(S["pt_hi"], 1)

            def pj(b):
                inv_std(b, 3)
                pool.wait_ge(S["x1_done"], due("x1_done", b, 3))
                nc.gpsimd.tensor_tensor(R[:, :, :], Hres[:, :, :], XF[:, :, :], ALU.add).then_inc(S["r_sum"], 1)

            def w1_cast(m, e, c):
                n = NC * e + c
                if c == 0:
                    pool.wait_ge(S["o_full"], due("o_full", m, 3 * (e - 1)))
                pool.wait_ge(S["gelu"], due("gelu", m, n + 1))
                apart(pool)
                nc.gpsimd.tensor_copy(Hs[:, e % 2, 0, c, :], h32[:, n % 3, :]).then_inc(S["h_hi"], 1)

            def turn(b, m):
                for step in order(m is not None, b is not None):
                    if step[0] == "W1":
                        w1_cast(m, step[1], step[2])
                    elif step[0] == "emb":
                        inv_std(b, 0)
                    elif step[0] == "qk1":
                        qk1(b, step[1])
                    elif step[0] == "pv1":
                        pv1(b)
                    elif step[0] == "att2":
                        att2(b)
                    elif step[0] == "pj":
                        pj(b)

            turn(0, None)
            with pool.Fori(1, B) as b:
                turn(b, b - 1)
            turn(None, B - 1)

        @block.scalar
        def _(act):
            one_ahead(act, ACT_SIGNALS)
            act.wait_ge(c_in, 16)
            for i in range(len(preps)):
                v, hi, lo, scale = prep_view(i)
                act.wait_ge(prep_full, i + 1)
                nc.scalar.activation(hi, v, ACT.Copy, scale=scale).then_inc(prep_hi, 1)
            for i in range(len(stages)):
                v, hi, lo, scale = stage_views(i)
                act.wait_ge(stg_in[i % 4], 32 * (i // 4 + 1))
                nc.scalar.activation(hi, v, ACT.Copy, scale=scale).then_inc(stg_hi, 1)
            act.wait_ge(c_set, 1)

            def img(b, k):
                act.wait_ge(S[f"xin{k % 2}"], due(f"xin{k % 2}", b, (k // 2 + 1) * XIN))
                act.wait_ge(S["img_split"], due("img_split", b, k))
                nc.scalar.activation(xmask[0:96, :], ximg[0:96, k % 2, :], ACT.Identity,
                                     scale=m48[0:96, :]).then_inc(S["img_hi"], 1)

            def tr(b, i):
                dst = XM if i == 2 else XT
                act.wait_ge(S["tr_full"], due("tr_full", b, 2 * i + 1))
                nc.scalar.activation(dst[:, 0, :], bank("tr", 2 * i)[:, 0:T], ACT.Copy).then_inc(S["tr_hi"], 1)
                act.wait_ge(S["tr_full"], due("tr_full", b, 2 * i + 2))
                nc.scalar.activation(trm, bank("tr", 2 * i + 1)[:, 0:T], ACT.Identity,
                                     scale=m64).then_inc(S["tr_hi"], 1)

            def qk1(b, i):
                for j in range(2):
                    act.wait_ge(S["rope_sum"], due("rope_sum", b, 2 * i + j + 1))
                    nc.scalar.activation(QK1[:, 2 * i + j, 0, :], tmp[:, 4 * i + j, :],
                                         ACT.Copy).then_inc(S["rope_hi"], 1)

            def v1(b):
                for t in range(NT):
                    act.wait_ge(S["v1_full"], due("v1_full", b, t + 1))
                    nc.scalar.activation(V1[:, 0, t, :], bank("v1", t)[0:TP, 0:D], ACT.Copy).then_inc(S["v1_hi"], 1)

            def s1(b):
                act.wait_ge(S["m1_ready"], due("m1_ready", b, 1))
                for t in range(NT):
                    w = TP * (t + 1)
                    nc.scalar.activation(S1[:, t, 0:w], S1[:, t, 0:w], ACT.Exp, bias=nm1[:, 1, t:t + 1], scale=SCALE1,
                                         accum_out=nm1[:, 2, t:t + 1]).then_inc(S["p1_ready"], 1)

            def p1t(b):
                for kt in range(NT):
                    act.wait_ge(S["p1t_full"], due("p1t_full", b, kt + 1))
                    nc.scalar.activation(PT[:, 0, 0, kt, TP * kt:T], bank("p1t", kt)[0:TP, TP * kt:T],
                                         ACT.Copy).then_inc(S["p1t_hi"], 1)

            def qk2(b, i):
                for j in (2 * i, 2 * i + 1):
                    mask = mq if j < 6 else mk
                    act.wait_ge(S["qk2_full"], due("qk2_full", b, j + 1))
                    act.wait_ge(S["qk2_done"], due("qk2_done", b, j - 1))
                    nc.scalar.activation(qm[:, j % 2, :], bank("qk2", j)[:, 0:T], ACT.Identity, scale=mask,
                                         bias=qkmb[:, j:j + 1]).then_inc(S["qk2_m"], 1)

            def v2(b):
                for t in range(NT):
                    act.wait_ge(S["v2_full"], due("v2_full", b, t + 1))
                    nc.scalar.activation(Vp[:, 0, t, :, 0:HD],
                                         bank("v2", t)[0:TP, 0:D].rearrange("p (h d) -> p h d", h=HEADS),
                                         ACT.Copy).then_inc(S["v2_hi"], 1)

            def o_norm(b, g):
                act.wait_ge(S["pv_norm"], due("pv_norm", b, g + 1))
                nc.scalar.activation(Os[:, 0, g, :], rsq[:, :], ACT.Identity,
                                     bias=vb[:, g:g + 1]).then_inc(S["o_hi"], 1)

            def att2(b):
                for h in range(HEADS):
                    for kt in range(3):
                        n = 3 * h + kt
                        act.wait_ge(S["st_full"], due("st_full", b, n + 1))
                        act.wait_ge(S["pt_lo"], due("pt_lo", b, n - 3))
                        nc.scalar.activation(Pr[:, n % 4, :], bank("st", n)[0:TP, 0:T], ACT.Exp,
                                             scale=SCALE2).then_inc(S["st_exp"], 1)
                    if h in (5, 9):
                        o_norm(b, (h - 5) // 4)
                o_norm(b, 2)

            def gate(b):
                act.wait_ge(S["gate_tanh_in"], due("gate_tanh_in", b, 1))
                nc.scalar.activation(rs[:, 6, :], rs[:, 5, :], ACT.Tanh, scale=0.5).then_inc(S["gate_tanh"], 1)

            def w1_gelu(m, e, c):
                n = NC * e + c
                act.wait_ge(S["w1_full"], due("w1_full", m, n + 1))
                act.wait_ge(S["h_lo"], due("h_lo", m, n - 2))
                nc.scalar.activation(h32[:, n % 3, :], M[n % 3][:, 0:T], ACT.Gelu, bias=b1s[:, e, c:c + 1],
                                     scale=1.0 / WSC).then_inc(S["gelu"], 1)

            def turn(b, m):
                for step in order(m is not None, b is not None):
                    kind = step[0]
                    if kind == "W1":
                        w1_gelu(m, step[1], step[2])
                    elif kind == "img":
                        img(b, step[1])
                    elif kind == "tr":
                        tr(b, step[1])
                    elif kind == "qk1":
                        qk1(b, step[1])
                    elif kind == "v1":
                        v1(b)
                    elif kind == "s1":
                        s1(b)
                    elif kind == "p1t":
                        p1t(b)
                    elif kind == "qk2":
                        qk2(b, step[1])
                    elif kind == "v2":
                        v2(b)
                    elif kind == "att2":
                        att2(b)
                    elif kind == "gate":
                        gate(b)

            turn(0, None)
            with act.Fori(1, B) as b:
                turn(b, b - 1)
            turn(None, B - 1)

        @block.vector
        def _(dve):
            one_ahead(dve, DVE_SIGNALS)
            for i in range(len(preps)):
                v, hi, lo, scale = prep_view(i)
                dve.wait_ge(prep_hi, i + 1)
                if scale == 1.0:
                    nc.vector.tensor_tensor(lo, v, hi, ALU.subtract).then_inc(prep_lo, 1)
                else:
                    nc.vector.scalar_tensor_tensor(lo, v, scale, hi, ALU.mult, ALU.subtract).then_inc(prep_lo, 1)
            for i in range(len(stages)):
                v, hi, lo, scale = stage_views(i)
                dve.wait_ge(stg_hi, i + 1)
                nc.vector.scalar_tensor_tensor(lo, v, scale, hi, ALU.mult, ALU.subtract).then_inc(stg_lo, 1)
            dve.wait_ge(c_in, N_C[0])
            nc.vector.tensor_copy(identb[:, :], cst[0:HEADS, 0:HEADS])
            nc.vector.tensor_scalar(qkmb[:, 0:6], qkb[:, 0:6], mq, None, ALU.mult)
            nc.vector.tensor_scalar(qkmb[:, 6:12], qkb[:, 6:12], mk, None, ALU.mult).then_inc(c_set, 1)

            steps = [0]

            def step_done(b, ins):
                ins.then_inc(S["dve_step"], 1)
                steps[0] += 1

            def stats(b, i, src):
                for t in range(NT):
                    step_done(b, nc.vector.bn_stats(st6[:, t, :], src[:, t, :]))
                dve.wait_ge(S["dve_step"], due("dve_step", b, steps[0]))
                apart(dve)
                for t in range(NT):
                    last = nc.vector.bn_aggr(mv[:, t, :], st6[:, t, :])
                last.then_inc(S["ln_var"], 1)
                dve.wait_ge(S["ln_rstd"], due("ln_rstd", b, i + 1))

            def norm_affine(b, src, w):
                for t in range(NT):
                    step_done(b, nc.vector.scalar_tensor_tensor(Nrm[:, t, :], src[:, t, :], mv[:, t, 0:1],
                                                                norms[:, w, :], ALU.subtract, ALU.mult))
                dve.wait_ge(S["dve_step"], due("dve_step", b, steps[0]))
                for t in range(NT):
                    last = nc.vector.scalar_tensor_tensor(Nrm[:, t, :], Nrm[:, t, :], rstd[:, t:t + 1],
                                                          norms[:, w + 1, :], ALU.mult, ALU.add)
                last.then_inc(S["n_ready"], 1)

            def img(b, k):
                if k == 0:
                    dve.wait_ge(S["emb_full"], due("emb_full", b - 1, 2))
                dve.wait_ge(S["img_hi"], due("img_hi", b, k + 1))
                nc.vector.tensor_tensor(XS[0:96, CW * k:CW * (k + 1)], ximg[0:96, k % 2, :], xmask[0:96, :],
                                        ALU.subtract).then_inc(S["img_split"], 1)

            def emb(b):
                dve.wait_ge(S["r_sum"], due("r_sum", b - 1, 1))
                for t, rows in ((0, TP), (1, PT1)):
                    dve.wait_ge(S["emb_full"], due("emb_full", b, t + 1))
                    nc.vector.scalar_tensor_tensor(Hres[0:rows, t, :], bank("emb", t)[0:rows, 0:D], 1.0 / WSC,
                                                   tokb[0:rows, :], ALU.mult, ALU.add).then_inc(S["emb_evac"], 1)
                dve.wait_ge(S["emb_evac"], due("emb_evac", b, 2))
                dve.wait_ge(S["txt_in"], due("txt_in", b, 32))
                stats(b, 0, Hres)
                dve.wait_ge(S["tr_full"], due("tr_full", b - 1, 6))
                for t in range(NT):
                    last = nc.vector.tensor_scalar(Nrm[:, t, :], Hres[:, t, :], mv[:, t, 0:1], rstd[:, t:t + 1],
                                                   ALU.subtract, ALU.mult)
                last.then_inc(S["n_ready"], 1)

            def tr(b, i):
                dst = XM if i == 2 else XT
                dve.wait_ge(S["tr_hi"], due("tr_hi", b, 2 * i + 1))
                nc.vector.tensor_tensor(dst[:, 1, :], bank("tr", 2 * i)[:, 0:T], dst[:, 0, :],
                                        ALU.subtract).then_inc(S["tr_lo"], 1)
                dve.wait_ge(S["tr_hi"], due("tr_hi", b, 2 * i + 2))
                nc.vector.tensor_tensor(dst[:, 2, :], bank("tr", 2 * i + 1)[:, 0:T], trm,
                                        ALU.subtract).then_inc(S["tr_lo"], 1)

            def qk1(b, i):
                re, im = bank("qk1", 2 * i)[0:RH, 0:T], bank("qk1", 2 * i + 1)[0:RH, 0:T]
                dve.wait_ge(S["qk1_full"], due("qk1_full", b, 2 * i + 1))
                nc.vector.tensor_tensor(tmp[:, 4 * i, :], re, cos, ALU.mult)
                nc.vector.tensor_tensor(tmp[:, 4 * i + 1, :], re, sin, ALU.mult).then_inc(S["rope_re"], 1)
                dve.wait_ge(S["qk1_full"], due("qk1_full", b, 2 * i + 2))
                nc.vector.tensor_tensor(tmp[:, 4 * i + 2, :], im, sin, ALU.mult)
                nc.vector.tensor_tensor(tmp[:, 4 * i + 3, :], im, cos, ALU.mult).then_inc(S["rope_mul"], 1)

            def v1(b):
                for t in range(NT):
                    dve.wait_ge(S["v1_hi"], due("v1_hi", b, t + 1))
                    nc.vector.tensor_tensor(V1[:, 1, t, :], bank("v1", t)[0:TP, 0:D], V1[:, 0, t, :],
                                            ALU.subtract).then_inc(S["v1_lo"], 1)

            def s1(b):
                for t in range(NT):
                    ps = bank("s1", t)
                    dve.wait_ge(S["s1_full"], due("s1_full", b, t + 1))
                    if t:
                        nc.vector.tensor_copy(S1[:, t, 0:TP * t], ps[0:TP, 0:TP * t])
                    nc.vector.tensor_tensor(S1[:, t, TP * t:TP * t + TP], ps[0:TP, TP * t:TP * t + TP], cap,
                                            ALU.min).then_inc(S["s1_evac"], 1)
                dve.wait_ge(S["s1_evac"], due("s1_evac", b, 3))
                for t in range(NT):
                    step_done(b, nc.vector.tensor_reduce(nm1[:, 0, t:t + 1], S1[:, t, 0:TP * (t + 1)], AX.X, ALU.max))
                dve.wait_ge(S["dve_step"], due("dve_step", b, steps[0]))
                nc.vector.tensor_scalar(nm1[:, 1, :], nm1[:, 0, :], -SCALE1, None, ALU.mult).then_inc(S["m1_ready"], 1)

            def p1t(b):
                for kt in range(NT):
                    dve.wait_ge(S["p1t_hi"], due("p1t_hi", b, kt + 1))
                    nc.vector.tensor_tensor(PT[:, 0, 1, kt, TP * kt:T], bank("p1t", kt)[0:TP, TP * kt:T],
                                            PT[:, 0, 0, kt, TP * kt:T], ALU.subtract).then_inc(S["p1t_lo"], 1)
                dve.wait_ge(S["p1_ready"], due("p1_ready", b, 3))
                step_done(b, nc.vector.reciprocal(nm1[:, 3, :], nm1[:, 2, :]))
                dve.wait_ge(S["dve_step"], due("dve_step", b, steps[0]))

            def pv1(b):
                for t in range(NT):
                    dve.wait_ge(S["pv1_full"], due("pv1_full", b, t + 1))
                    nc.vector.scalar_tensor_tensor(Hres[:, t, :], bank("pv1", t)[0:TP, 0:D], nm1[:, 3, t:t + 1],
                                                   Hres[:, t, :], ALU.mult, ALU.add).then_inc(S["pv1_evac"], 1)
                dve.wait_ge(S["pv1_evac"], due("pv1_evac", b, 3))
                stats(b, 1, Hres)
                for t in range(NT):
                    last = nc.vector.tensor_scalar(XF[:, t, :], Hres[:, t, :], mv[:, t, 0:1], rstd[:, t:t + 1],
                                                   ALU.subtract, ALU.mult)
                last.then_inc(S["xf_ready"], 1)
                dve.wait_ge(S["xf_ready"], due("xf_ready", b, 1))
                stats(b, 2, XF)
                norm_affine(b, XF, 0)

            def qk2(b, i):
                for j in (2 * i, 2 * i + 1):
                    dve.wait_ge(S["qk2_m"], due("qk2_m", b, j + 1))
                    nc.vector.scalar_tensor_tensor(QK[:, j, :], bank("qk2", j)[:, 0:T], qkb[:, j:j + 1], qm[:, j % 2, :],
                                                   ALU.add, ALU.subtract).then_inc(S["qk2_done"], 1)

            def v2(b):
                for t in range(NT):
                    dve.wait_ge(S["v2_hi"], due("v2_hi", b, t + 1))
                    nc.vector.tensor_tensor(Vp[:, 1, t, :, 0:HD],
                                            bank("v2", t)[0:TP, 0:D].rearrange("p (h d) -> p h d", h=HEADS),
                                            Vp[:, 0, t, :, 0:HD], ALU.subtract).then_inc(S["v2_lo"], 1)

            def s(b, h):
                for qt in range(NT):
                    n = 3 * h + qt
                    dve.wait_ge(S["s_full"], due("s_full", b, n + 1))
                    nc.vector.tensor_reduce(mx[:, qt, h:h + 1], bank("s", n)[0:TP, 0:T], AX.X,
                                            ALU.max).then_inc(S["s_max"], 1)

            def mt(b):
                dve.wait_ge(S["mt_full"], due("mt_full", b, 1))
                nc.vector.tensor_scalar(nmT[:, :], bank("mt", 0)[0:HEADS, 0:T], -1.0, None,
                                        ALU.mult).then_inc(S["mt_done"], 1)

            def o_norm(b, g):
                ps = TB[2][:, 0:T]
                dve.wait_ge(S["pv_done"], due("pv_done", b, 4 * g + 4))
                apart(dve)
                step_done(b, nc.vector.stream_shuffle(rsi[:, :], ps, [16 + i % 16 for i in range(32)]))
                dve.wait_ge(S["dve_step"], due("dve_step", b, steps[0]))
                step_done(b, nc.vector.reciprocal(rsi[:, :], rsi[:, :]))
                dve.wait_ge(S["dve_step"], due("dve_step", b, steps[0]))
                dve.wait_ge(S["o_lo"], due("o_lo", b, g))
                nc.vector.tensor_tensor(rsq[:, :], ps, rsi[:, :], ALU.mult).then_inc(S["pv_norm"], 1)

            def o_split(b, g):
                dve.wait_ge(S["o_hi"], due("o_hi", b, g + 1))
                nc.vector.scalar_tensor_tensor(Os[:, 1, g, :], rsq[:, :], vb[:, g:g + 1], Os[:, 0, g, :],
                                               ALU.add, ALU.subtract).then_inc(S["o_lo"], 1)

            def att2(b):
                for h in range(HEADS):
                    for kt in range(3):
                        n = 3 * h + kt
                        dve.wait_ge(S["pt_hi"], due("pt_hi", b, n + 1))
                        nc.vector.tensor_tensor(PT[:, h % 2, 1, kt, :], Pr[:, n % 4, :], PT[:, h % 2, 0, kt, :],
                                                ALU.subtract).then_inc(S["pt_lo"], 1)
                    if h in (4, 8):
                        o_norm(b, h // 4 - 1)
                    if h in (6, 10):
                        o_split(b, (h - 6) // 4)
                o_norm(b, 2)
                o_split(b, 2)

            def pj(b):
                dve.wait_ge(S["xfb_ready"], due("xfb_ready", b, 1))
                for t in range(NT):
                    dve.wait_ge(S["pj_full"], due("pj_full", b, t + 1))
                    nc.vector.scalar_tensor_tensor(XF[:, t, :], bank("pj", t)[0:TP, 0:D], 1.0 / WSC, R[:, t, :],
                                                   ALU.mult, ALU.add).then_inc(S["x1_done"], 1)
                dve.wait_ge(S["x1_done"], due("x1_done", b, 3))
                stats(b, 3, XF)
                norm_affine(b, XF, 2)

            def gate(b):
                def wide(ap):
                    return ap.rearrange("p (t a) -> p t a", a=1).to_broadcast([TP, NT, E])

                L, eq, c1, one1, L2, one2 = (rt[:, i] for i in range(6))
                top1, first1, top2, first2 = (rs[:, i, :] for i in range(4))
                dve.wait_ge(S["gate_full"], due("gate_full", b, 1))
                nc.vector.tensor_scalar(L, bank("gate", 0)[0:TP, 0:NT * E].rearrange("p (t e) -> p t e", e=E),
                                        1.0 / WSC, None, ALU.mult).then_inc(S["gate_evac"], 1)
                dve.wait_ge(S["gate_evac"], due("gate_evac", b, 1))
                for src, top, first, one in ((L, top1, first1, one1), (L2, top2, first2, one2)):
                    step_done(b, nc.vector.tensor_reduce(top, src, AX.X, ALU.max))
                    dve.wait_ge(S["dve_step"], due("dve_step", b, steps[0]))
                    step_done(b, nc.vector.tensor_tensor(eq, src, wide(top), ALU.is_ge))
                    dve.wait_ge(S["dve_step"], due("dve_step", b, steps[0]))
                    step_done(b, nc.vector.tensor_tensor(c1, eq, rev, ALU.mult))
                    dve.wait_ge(S["dve_step"], due("dve_step", b, steps[0]))
                    step_done(b, nc.vector.tensor_reduce(first, c1, AX.X, ALU.max))
                    dve.wait_ge(S["dve_step"], due("dve_step", b, steps[0]))
                    step_done(b, nc.vector.tensor_tensor(one, c1, wide(first), ALU.is_equal))
                    dve.wait_ge(S["dve_step"], due("dve_step", b, steps[0]))
                    if one is one1:
                        step_done(b, nc.vector.scalar_tensor_tensor(L2, one1, -3.0e38, L, ALU.mult, ALU.add))
                        dve.wait_ge(S["dve_step"], due("dve_step", b, steps[0]))
                nc.vector.tensor_tensor(rs[:, 5, :], top1, top2, ALU.subtract).then_inc(S["gate_tanh_in"], 1)
                dve.wait_ge(S["gate_tanh"], due("gate_tanh", b, 1))
                step_done(b, nc.vector.tensor_scalar(rs[:, 4, :], rs[:, 6, :], 0.5, 0.5, ALU.mult, ALU.add))
                step_done(b, nc.vector.tensor_scalar(rs[:, 7, :], rs[:, 6, :], -0.5, 0.5, ALU.mult, ALU.add))
                dve.wait_ge(S["dve_step"], due("dve_step", b, steps[0]))
                step_done(b, nc.vector.tensor_tensor(eq, one1, wide(rs[:, 4, :]), ALU.mult))
                step_done(b, nc.vector.tensor_tensor(c1, one2, wide(rs[:, 7, :]), ALU.mult))
                dve.wait_ge(S["dve_step"], due("dve_step", b, steps[0]))
                nc.vector.tensor_tensor(G[:, :, :], eq, c1, ALU.add).then_inc(S["g_ready"], 1)

            def gt(b):
                dve.wait_ge(S["gt_full"], due("gt_full", b, 1))
                nc.vector.tensor_copy(GT, bank("gt", 0)[0:E, 0:T]).then_inc(S["gt_done"], 1)

            def b2_step(b):
                dve.wait_ge(S["g_ready"], due("g_ready", b, 1))
                dve.wait_ge(S["acc"], due("acc", b - 1, 24))
                nc.vector.tensor_scalar(Gs[:, :, :], G[:, :, :], 1.0 / WSC, None, ALU.mult)
                dve.wait_ge(S["r_sum"], due("r_sum", b, 1))
                for t in range(NT):
                    dve.wait_ge(S["b2_full"], due("b2_full", b, t + 1))
                    nc.vector.tensor_tensor(R[:, t, :], bank("b2", t)[0:TP, 0:D], R[:, t, :],
                                            ALU.add).then_inc(S["r_ready"], 1)

            def h_low(m, n):
                e, c = n // NC, n % NC
                dve.wait_ge(S["h_hi"], due("h_hi", m, n + 1))
                nc.vector.tensor_tensor(Hs[:, e % 2, 1, c, :], h32[:, n % 3, :], Hs[:, e % 2, 0, c, :],
                                        ALU.subtract).then_inc(S["h_lo"], 1)

            def w2_acc(m, e, t):
                if t == 0:
                    return
                if e == 0 and t == 1:
                    dve.wait_ge(S["out_done"], due("out_done", m, 0))
                    dve.wait_ge(S["r_ready"], due("r_ready", m, 3))
                else:
                    dve.wait_ge(S["acc"], due("acc", m, 3 * e - 3 + (2 if t == 1 else 3)))
                dve.wait_ge(S["o_full"], due("o_full", m, 3 * e + t + 1))
                for u in ((0, 1) if t == 1 else (2,)):
                    ps = O[0][0:TP, D * u:D * u + D] if u < 2 else O[1][0:TP, 0:D]
                    nc.vector.scalar_tensor_tensor(ACC[:, u, :], ps, Gs[:, u, e:e + 1],
                                                   (R if e == 0 else ACC)[:, u, :], ALU.mult,
                                                   ALU.add).then_inc(S["acc"], 1)

            def turn(b, m):
                steps[0] = 0
                for step in order(m is not None, b is not None):
                    kind = step[0]
                    if kind == "W1":
                        n = NC * step[1] + step[2]
                        if n:
                            h_low(m, n - 1)
                    elif kind == "W2":
                        if step[1:] == (E - 2, 0):
                            h_low(m, NC * E - 1)
                        w2_acc(m, step[1], step[2])
                    elif kind == "img":
                        img(b, step[1])
                    elif kind == "emb":
                        emb(b)
                    elif kind == "tr":
                        tr(b, step[1])
                    elif kind == "qk1":
                        qk1(b, step[1])
                    elif kind == "v1":
                        v1(b)
                    elif kind == "s1":
                        s1(b)
                    elif kind == "p1t":
                        p1t(b)
                    elif kind == "pv1":
                        pv1(b)
                    elif kind == "qk2":
                        qk2(b, step[1])
                    elif kind == "v2":
                        v2(b)
                    elif kind == "s":
                        s(b, step[1])
                    elif kind == "mt":
                        mt(b)
                    elif kind == "att2":
                        att2(b)
                    elif kind == "pj":
                        pj(b)
                    elif kind == "gate":
                        gate(b)
                    elif kind == "gt":
                        gt(b)
                    elif kind == "b2":
                        b2_step(b)
                assert b is None or steps[0] == DVE_STEPS, steps[0]

            turn(0, None)
            with dve.Fori(1, B) as b:
                turn(b, b - 1)
            turn(None, B - 1)

        @block.tensor
        def _(pe):
            one_ahead(pe, PE_SIGNALS)
            pe.wait_ge(c_in, 16)
            pe.wait_ge(big_in, 128)

            def turn_twice(ps, c0, src, n):
                nc.tensor.transpose(ps[:, c0:c0 + n], src[:, D - 128:D], ident[0:n, 0:n])
                return nc.tensor.transpose(ps[0:KB, c0:c0 + n], src[:, KA:D], ident[0:n, 0:n])

            for i, (kind, at, rows, cols, _hi, _lo, _sc) in enumerate(preps):
                ps = TB[i % 3]
                if i >= 3:
                    pe.wait_ge(prep_lo, i - 2)
                if kind == "tok":
                    pe.wait_ge(tok_dup, i + 1)
                    for n in range(4):
                        last = nc.tensor.transpose(ps[0:96, 96 * n:96 * n + 96], tokD[:, i % 2, n, :], ident[0:96, 0:96])
                elif kind == "qkva":
                    for a in range(2):
                        last = nc.tensor.transpose(ps[:, 96 * a:96 * a + 96], qkvS[:, 2 * at + a, 0:KA], ident[0:96, 0:96])
                elif kind == "qkvb":
                    for a in range(2):
                        last = turn_twice(ps, 96 * a, qkvS[:, 2 * at + a, :], 96)
                else:
                    for g in range(3):
                        last = nc.tensor.transpose(ps[:, 96 * g:96 * g + 96], projS[:, at, g, :], ident[0:96, 0:96])
                last.then_inc(prep_full, 1)
            pe.wait_ge(c_set, 1)
            pe.wait_ge(pad_set, 4)

            def five(out_ap, pairs):
                for i, (lhsT, rhs) in enumerate(pairs):
                    last = nc.tensor.matmul(out_ap, lhsT, rhs, start=(i == 0), stop=(i == len(pairs) - 1))
                return last

            def emb(b):
                pe.wait_ge(S["img_split"], due("img_split", b, CHUNKS))
                xv = XS[0:96, :].rearrange("p (t w) -> p w t", w=PATCH)
                for t, n in ((0, TP), (1, PT1)):
                    pe.wait_ge(*bank_read(b, "emb", t))
                    five(bank("emb", t)[0:n, 0:D],
                         [(xv[:, w, TP * t:TP * t + n], tokW[0:96, s, w, :]) for w in range(PATCH) for s in range(2)]
                         ).then_inc(S["emb_full"], 1)

            def tr(b, i):
                pe.wait_ge(S["n_ready"], due("n_ready", b, i + 1))
                pe.wait_ge(*bank_read(b, "tr", 2 * i))
                for t in range(NT):
                    last = nc.tensor.transpose(bank("tr", 2 * i)[:, TP * t:TP * t + TP], Nrm[:, t, 0:KA],
                                               ident[0:TP, 0:TP])
                last.then_inc(S["tr_full"], 1)
                pe.wait_ge(*bank_read(b, "tr", 2 * i + 1))
                for t in range(NT):
                    last = turn_twice(bank("tr", 2 * i + 1), TP * t, Nrm[:, t, :], TP)
                last.then_inc(S["tr_full"], 1)

            def by_weight(wa, wb, pick, X):
                return [(pick(wa, 0), X[:, 0, :]), (pick(wa, 1), X[:, 0, :]), (pick(wa, 0), X[:, 1, :]),
                        (pick(wb, 0), X[:, 2, :]), (pick(wb, 1), X[:, 2, :])]

            def by_token(wa, wb, pick, X, t):
                c = slice(TP * t, TP * t + TP)
                return [(X[:, 0, c], pick(wa, 0)), (X[:, 0, c], pick(wa, 1)), (X[:, 1, c], pick(wa, 0)),
                        (X[:, 2, c], pick(wb, 0)), (X[:, 2, c], pick(wb, 1))]

            def qk1(b, i):
                pe.wait_ge(S["tr_lo"], due("tr_lo", b, 2))
                for j in (2 * i, 2 * i + 1):
                    pe.wait_ge(*bank_read(b, "qk1", j))
                    five(bank("qk1", j)[0:RH, 0:T],
                         by_weight(attWa, attWb, lambda w, s: w[:, s, RH * j:RH * j + RH], XT)
                         ).then_inc(S["qk1_full"], 1)

            def v1(b):
                for t in range(NT):
                    pe.wait_ge(*bank_read(b, "v1", t))
                    five(bank("v1", t)[0:TP, 0:D], by_token(attWa, attWb, lambda w, s: w[:, s, 2 * D:3 * D], XT, t)
                         ).then_inc(S["v1_full"], 1)

            def s1(b):
                pe.wait_ge(S["rope_lo"], due("rope_lo", b, 4))
                for t in range(NT):
                    w = TP * (t + 1)
                    pe.wait_ge(*bank_read(b, "s1", t))
                    five(bank("s1", t)[0:TP, 0:w],
                         [(QK1[:, j, qs, TP * t:w], QK1[:, 2 + j, ks, 0:w])
                          for j in range(2) for qs, ks in ((0, 0), (0, 1), (1, 0))]).then_inc(S["s1_full"], 1)

            def p1t(b):
                pe.wait_ge(S["p1_ready"], due("p1_ready", b, 3))
                for kt in range(NT):
                    pe.wait_ge(*bank_read(b, "p1t", kt))
                    for qt in range(kt, NT):
                        last = nc.tensor.transpose(bank("p1t", kt)[0:TP, TP * qt:TP * qt + TP],
                                                   S1[:, qt, TP * kt:TP * kt + TP], ident[0:TP, 0:TP])
                    last.then_inc(S["p1t_full"], 1)

            def pv1(b):
                pe.wait_ge(S["p1t_lo"], due("p1t_lo", b, 3))
                pe.wait_ge(S["v1_lo"], due("v1_lo", b, 3))
                for t in range(NT):
                    pe.wait_ge(*bank_read(b, "pv1", t))
                    five(bank("pv1", t)[0:TP, 0:D],
                         [(PT[:, 0, ps, kt, TP * t:TP * t + TP], V1[:, vs, kt, :])
                          for kt in range(t + 1) for ps, vs in ((0, 0), (0, 1), (1, 0))]).then_inc(S["pv1_full"], 1)

            def qk2(b, i):
                pe.wait_ge(S["tr_lo"], due("tr_lo", b, 4))
                for j in (2 * i, 2 * i + 1):
                    pe.wait_ge(*bank_read(b, "qk2", j))
                    five(bank("qk2", j)[:, 0:T],
                         by_weight(qkvWa, qkvWb, lambda w, s: w[:, s, 128 * j:128 * j + 128], XT)
                         ).then_inc(S["qk2_full"], 1)

            def v2(b):
                for t in range(NT):
                    pe.wait_ge(*bank_read(b, "v2", t))
                    five(bank("v2", t)[0:TP, 0:D], by_token(qkvWa, qkvWb, lambda w, s: w[:, s, 1536:1536 + D], XT, t)
                         ).then_inc(S["v2_full"], 1)

            def s(b, h):
                pe.wait_ge(S["qk2_done"], due("qk2_done", b, 12))
                r = slice(64 * (h % 2), 64 * (h % 2) + 64)
                for qt in range(NT):
                    pe.wait_ge(*bank_read(b, "s", 3 * h + qt))
                    nc.tensor.matmul(bank("s", 3 * h + qt)[0:TP, 0:T], QK[r, h // 2, TP * qt:TP * qt + TP],
                                     QK[r, 6 + h // 2, :], start=True, stop=True).then_inc(S["s_full"], 1)

            def mt(b):
                pe.wait_ge(S["s_max"], due("s_max", b, 36))
                pe.wait_ge(*bank_read(b, "mt", 0))
                for qt in range(NT):
                    last = nc.tensor.transpose(bank("mt", 0)[0:HEADS, TP * qt:TP * qt + TP], mx[:, qt, :],
                                               ident[0:TP, 0:TP])
                last.then_inc(S["mt_full"], 1)

            def st(b, h):
                r = slice(64 * (h % 2), 64 * (h % 2) + 64)
                for kt in range(3):
                    n = 3 * h + kt
                    pe.wait_ge(*bank_read(b, "st", n))
                    ps = bank("st", n)[0:TP, 0:T]
                    nc.tensor.matmul(ps, QK[r, 6 + h // 2, TP * kt:TP * kt + TP], QK[r, h // 2, :],
                                     start=True, stop=False)
                    nc.tensor.matmul(ps, identb[:, h:h + 1].to_broadcast([HEADS, TP]), nmT[:, :],
                                     start=False, stop=True).then_inc(S["st_full"], 1)

            def pv(b, h):
                j, g = h % 4, h // 4
                if j == 0:
                    pe.wait_ge(*bank_read(b, "pv", g))
                pe.wait_ge(S["pt_lo"], due("pt_lo", b, 3 * h + 3))
                ps = TB[2][32 * j:32 * j + 32, 0:T]
                for kt in range(3):
                    for p_, v_ in ((0, 0), (0, 1), (1, 0)):
                        last = nc.tensor.matmul(ps, Vp[:, v_, kt, h, :], PT[:, h % 2, p_, kt, :],
                                                start=(kt == 0 and (p_, v_) == (0, 0)),
                                                stop=(kt == 2 and (p_, v_) == (1, 0)))
                last.then_inc(S["pv_done"], 1)

            def att2(b):
                pe.wait_ge(S["mt_done"], due("mt_done", b, 1))
                pe.wait_ge(S["v2_lo"], due("v2_lo", b, 3))
                for h in range(HEADS):
                    st(b, h)
                    if h:
                        pv(b, h - 1)
                pv(b, HEADS - 1)

            def pj(b):
                pe.wait_ge(S["o_lo"], due("o_lo", b, 3))
                for t in range(NT):
                    c = slice(TP * t, TP * t + TP)
                    pe.wait_ge(*bank_read(b, "pj", t))
                    five(bank("pj", t)[0:TP, 0:D],
                         [(Os[:, s_, g, c], projW[:, w_, g, :]) for g in range(3) for s_, w_ in ((0, 0), (0, 1), (1, 0))]
                         ).then_inc(S["pj_full"], 1)

            def gate(b):
                pe.wait_ge(S["tr_lo"], due("tr_lo", b, 6))
                pe.wait_ge(*bank_read(b, "gate", 0))
                for t in range(NT):
                    last = five(bank("gate", 0)[0:TP, E * t:E * t + E],
                                by_token(gateWa, gateWb, lambda w, s: w[:, s, :], XM, t))
                last.then_inc(S["gate_full"], 1)

            def gt(b):
                pe.wait_ge(S["g_ready"], due("g_ready", b, 1))
                pe.wait_ge(*bank_read(b, "gt", 0))
                for t in range(NT):
                    last = nc.tensor.transpose(bank("gt", 0)[0:E, TP * t:TP * t + TP], G[:, t, :], ident[0:TP, 0:TP])
                last.then_inc(S["gt_full"], 1)

            def b2_step(b):
                pe.wait_ge(S["gt_done"], due("gt_done", b, 1))
                for t in range(NT):
                    pe.wait_ge(*bank_read(b, "b2", t))
                    nc.tensor.matmul(bank("b2", t)[0:TP, 0:D], GT[:, TP * t:TP * t + TP], b2s[:, :],
                                     start=True, stop=True).then_inc(S["b2_full"], 1)

            def w1_chunk(m, e, c):
                n = NC * e + c
                if n == 0:
                    pe.wait_ge(S["tr_lo"], due("tr_lo", m, 6))
                pe.wait_ge(S["gelu"], due("gelu", m, n - 2))
                cols = slice(128 * c, 128 * c + 128)
                five(M[n % 3][:, 0:T], by_weight(W1a[:, e], W1b[:, e], lambda w, s: w[:, s, cols], XM)
                     ).then_inc(S["w1_full"], 1)

            def w2_tile(m, e, t):
                if t == 0:
                    pe.wait_ge(S["h_lo"], due("h_lo", m, NC * (e + 1)))
                if t != 1:
                    pe.wait_ge(S["acc"], due("acc", m, 3 * (e - 1) + (2 if t == 0 else 3)))
                ps = O[0][0:TP, D * t:D * t + D] if t < 2 else O[1][0:TP, 0:D]
                rows = slice(TP * t, TP * t + TP)
                five(ps, [(Hs[:, e % 2, s_, c, rows], W2s[:, e, c, w_, :])
                          for c in range(NC) for s_, w_ in ((0, 0), (0, 1), (1, 0))]).then_inc(S["o_full"], 1)

            def turn(b, m):
                for step in order(m is not None, b is not None):
                    kind = step[0]
                    if kind == "W1":
                        w1_chunk(m, step[1], step[2])
                    elif kind == "W2":
                        w2_tile(m, step[1], step[2])
                    elif kind == "emb":
                        emb(b)
                    elif kind == "tr":
                        tr(b, step[1])
                    elif kind == "qk1":
                        qk1(b, step[1])
                    elif kind == "v1":
                        v1(b)
                    elif kind == "s1":
                        s1(b)
                    elif kind == "p1t":
                        p1t(b)
                    elif kind == "pv1":
                        pv1(b)
                    elif kind == "qk2":
                        qk2(b, step[1])
                    elif kind == "v2":
                        v2(b)
                    elif kind == "s":
                        s(b, step[1])
                    elif kind == "mt":
                        mt(b)
                    elif kind == "att2":
                        att2(b)
                    elif kind == "pj":
                        pj(b)
                    elif kind == "gate":
                        gate(b)
                    elif kind == "gt":
                        gt(b)
                    elif kind == "b2":
                        b2_step(b)

            turn(0, None)
            with pe.Fori(1, B) as b:
                turn(b, b - 1)
            turn(None, B - 1)


_INS = ["x", "txt", "L0_tok_W", "L0_tok_b", "L0_attn_Wq", "L0_attn_Wk", "L0_attn_Wv", "L0_ffn_norm1_w",
        "L0_ffn_norm1_b", "L0_ffn_qkv_w", "L0_ffn_qkv_b", "L0_ffn_proj_w", "L0_ffn_proj_b", "L0_ffn_norm2_w",
        "L0_ffn_norm2_b", "L0_ffn_w_gate", "L0_ffn_W1", "L0_ffn_b1", "L0_ffn_W2", "L0_ffn_b2"]


def shape_constants():
    import numpy as np
    c = np.zeros((128, C_N), np.float32)
    p = np.arange(128)
    c[:, C_ID:C_ID + 128] = np.eye(128, dtype=np.float32)
    c[:, C_M64] = p >= 64
    c[:, C_MQ] = p % 64 >= 32
    c[:, C_MK] = p % 32 >= 16
    c[:, C_M48] = p >= IMROWS
    j = np.arange(RH, dtype=np.float32)
    theta = np.power(np.float32(10000.0), np.float32(-2.0) * j / np.float32(D), dtype=np.float32)
    ang = np.arange(T, dtype=np.float32)[None, :] * theta[:, None]
    c[0:RH, C_COS:C_COS + T] = np.cos(ang)
    c[0:RH, C_SIN:C_SIN + T] = np.sin(ang)
    q, k = np.arange(TP)[:, None], np.arange(TP)[None, :]
    c[0:TP, C_CAP:C_CAP + TP] = np.where(k <= q, 3.0e38, -3.0e38)
    c[:, C_EPS:C_N] = EPS
    c[:, C_POW:C_EPS] = -0.5
    c[:, C_REV:C_POW] = np.tile(np.arange(E, 0, -1, dtype=np.float32), NT)[None, :]
    return c


def kernel(**inputs):
    import numpy as np
    import concourse.bacc as bacc
    from concourse.bass_utils import run_bass_kernel_spmd as run

    nc = bacc.Bacc("TRN2", target_bir_lowering=False, num_devices=1)
    arrays, args = {}, []
    for name in _INS:
        a = np.ascontiguousarray(inputs[name])
        arrays[f"in_{name}"] = a
        args.append(nc.dram_tensor(f"in_{name}", a.shape, mybir.dt.from_np(a.dtype), kind="ExternalInput").ap())
    arrays["in_const"] = shape_constants()
    args.append(nc.dram_tensor("in_const", (128, C_N), F32, kind="ExternalInput").ap())
    out = nc.dram_tensor("out", (B, T, D), F32, kind="ExternalOutput").ap()
    build_program(nc, *args, out)
    return run(nc, [arrays], core_ids=[0]).results[0]["out"]
```

```python
from contextlib import ExitStack

import concourse.bass as bass
from concourse import mybir

ALU = mybir.AluOpType
ACT = mybir.ActivationFunctionType
F32 = mybir.dt.float32
F16 = mybir.dt.float16
BF16 = mybir.dt.bfloat16
AX = mybir.AxisListType

B, CH, IMG, PATCH = 32, 3, 224, 16
D, HID, E, HEADS = 192, 768, 8, 12
HD = D // HEADS
GRID = IMG // PATCH
NPATCH = GRID * GRID
NTEXT = 128
T = NPATCH + NTEXT
TP = 108
NT = T // TP
PT1 = NPATCH - TP
KA, KB = 128, D - 128
RH = D // 2
NC = HID // 128
IMROWS = CH * PATCH
CHUNKS = 7
CW = GRID * IMG // CHUNKS
WSC = 64.0
EPS = 1e-5
SCALE1 = float(D) ** -0.5
SCALE2 = float(HD) ** -0.5

C_ID, C_M64, C_MQ, C_MK, C_M48 = 0, 128, 129, 130, 131
C_COS, C_SIN = 132, 132 + T
C_CAP = C_SIN + T
C_REV = C_CAP + TP
C_POW = C_REV + NT * E
C_EPS = C_POW + NT
C_N = C_EPS + NT

XIN = 96
DVE_STEPS = 37
SP_SIGNALS = dict(xin0=4 * XIN, xin1=3 * XIN, txt_in=32, out_done=16)
PE_SIGNALS = dict(emb_full=2, tr_full=6, qk1_full=4, v1_full=3, s1_full=3, p1t_full=3, pv1_full=3, qk2_full=12,
                  v2_full=3, s_full=36, mt_full=3, st_full=36, pv_done=12, pj_full=3, gate_full=1, gt_full=1,
                  b2_full=3, w1_full=48, o_full=24)
ACT_SIGNALS = dict(img_hi=7, tr_hi=6, rope_hi=4, v1_hi=3, p1_ready=3, p1t_hi=3, qk2_m=12, v2_hi=3, st_exp=36, o_hi=3,
                   gate_tanh=1, gelu=48, h_hi=48)
DVE_SIGNALS = dict(emb_evac=2, n_ready=3, tr_lo=6, rope_re=2, rope_mul=2, v1_lo=3, s1_evac=3, m1_ready=1,
                   p1t_lo=3, pv1_evac=3, xf_ready=1, qk2_done=12, v2_lo=3, s_max=36, mt_done=3, pt_hi=36, pt_lo=24, sum_out=3, sum_inv=3,
                   pv_norm=3, o_lo=3, x1_done=3, gate_evac=1, gate_tanh_in=1, g_ready=1, gt_done=1, r_ready=3, h_lo=32, acc=24,
                   ln_var=4, dve_step=DVE_STEPS)
POOL_SIGNALS = dict(img_split=7, h_lo2=16, rope_sum=4, rope_lo=4, xfb_ready=1, pt_lo2=12, r_sum=1, ln_eps=4, ln_rstd=4)
PER = SP_SIGNALS | PE_SIGNALS | ACT_SIGNALS | DVE_SIGNALS | POOL_SIGNALS

USES = []


def plan_uses():
    turn = [0]

    def use(step, i, sem, k, bank=None):
        if bank is None:
            bank = turn[0] % 4
            turn[0] += 1
        USES.append(((step, i), bank, sem, k))

    use("emb", 0, "emb_evac", 1)
    use("emb", 1, "emb_evac", 2)
    use("tr", 0, "tr_lo", 1)
    use("tr", 1, "tr_lo", 2)
    for i in range(4):
        use("qk1", i, "rope_mul" if i % 2 else "rope_re", i // 2 + 1)
    for i in range(3):
        use("v1", i, "v1_lo", i + 1)
    for i in range(3):
        use("s1", i, "s1_evac", i + 1)
    for i in range(3):
        use("p1t", i, "p1t_lo", i + 1)
    for i in range(3):
        use("pv1", i, "pv1_evac", i + 1)
    use("tr", 2, "tr_lo", 3)
    use("tr", 3, "tr_lo", 4)
    for i in range(12):
        use("qk2", i, "qk2_done", i + 1)
    for i in range(3):
        use("v2", i, "v2_lo", i + 1)
    for g in range(3):
        free = ((0, 1, 2, 3), (0, 1, 3), (0, 1, 2))[g]
        for i in range(12 * g, 12 * g + 12):
            use("s", i, "s_max", i + 1, bank=free[i % len(free)])
        use("mt", g, "mt_done", g + 1, bank=g % 2)
        for h in range(4 * g, 4 * g + 4):
            for kt in range(3):
                use("st", 3 * h + kt, "st_exp", 3 * h + kt + 1, bank=(0, 1, 3 - g % 2)[kt])
            if h == 4 * g + 1:
                use("pv", g, "pv_norm", g + 1, bank=2 + g % 2)
    for i in range(3):
        use("pj", i, "x1_done", i + 1)
    use("tr", 4, "tr_lo", 5)
    use("tr", 5, "tr_lo", 6)
    use("gate", 0, "gate_evac", 1)
    use("gt", 0, "gt_done", 1)
    for i in range(3):
        use("b2", i, "r_ready", i + 1)


plan_uses()
BANK = {key: bank for key, bank, _, _ in USES}
LAST = {bank: (sem, k) for _, bank, sem, k in USES}
BEFORE = {}
_seen = {}
for _key, _bank, _sem, _k in USES:
    BEFORE[_key] = _seen.get(_bank)
    _seen[_bank] = (_sem, _k)

FIRST = ([1, ("emb", 0), 2, ("ln", 0), 3, ("tr", 0), 2, ("qk1", 0), 1, ("qk1", 1), 1, ("v1", 0), 3, ("s1", 0), 3,
          ("p1t", 0), 1, ("img", 0), 1, ("img", 1), ("pv1", 0), 3, ("ln", 1), 2, ("ln", 2), 2, ("tr", 1), 1]
         + [p for i in range(6) for p in (("qk2", i), (0, 1, 1, 1, 1, 2)[i], ("img", i + 2)) if p != ("img", CHUNKS)]
         + [("v2", 0), 1])
SECOND = [("s", 0), 1]
for _g in range(3):
    _h = 4 * _g
    SECOND += [("s", _h + 1), 1, ("s", _h + 2), 1, ("s", _h + 3), 2, ("mt", _g), 1,
               ("att2", _h), 1, ("att2", _h + 1), 1, ("pv", _h), ("att2", _h + 2), ("pv", _h + 1), 1,
               ("att2", _h + 3), ("pv", _h + 2)]
    if _g < 2:
        SECOND += [("s", _h + 4), 1, ("pv", _h + 3), ("norm", _g), 1, ("scale", _g), ("osplit", _g)]
SECOND += [1, ("pv", HEADS - 1), ("norm", 2), 1, ("scale", 2), 1, ("osplit", 2), 1, ("pj", 0), 1, ("ln", 3), 1,
           ("tr", 2), 1, ("gate", 0), 2, ("gt", 0), 1, ("b2", 0)]
PIECES = FIRST + SECOND
MAIN = [("W1", 0, c) for c in range(NC)]
for _e in range(1, E // 2):
    for _t in range(NT):
        MAIN += [("W1", _e, 2 * _t), ("W1", _e, 2 * _t + 1), ("W2", _e - 1, _t)]
for _e in range(E // 2, E):
    MAIN += [("W1", _e, c) for c in range(NC)]
    MAIN += [("W2", _e - 1, _t) for _t in range(NT)]
MAIN += [("W2", E - 1, _t) for _t in range(NT)]


def order(experts, attention, image=True):
    out, at = [], 0
    for piece in PIECES:
        if isinstance(piece, int):
            out += MAIN[at:at + piece] if experts else []
            at += piece
        elif attention and (image or piece[0] != "img"):
            out.append(piece)
    assert at == len(MAIN), at
    return out


def build_program(nc, x, txt, tok_w, tok_b, wq, wk, wv, n1w, n1b, qkv_w, qkv_b, proj_w, proj_b, n2w, n2b,
                  w_gate, w1, b1, w2, b2, const, out):
    with ExitStack() as ctx:
        def sb(name, shape, dt):
            return ctx.enter_context(nc.sbuf_tensor(name, shape, dt))

        def sem(name):
            return ctx.enter_context(nc.semaphore(name))

        W1a = sb("W1a", [128, E, 2, HID], F16)
        W1b = sb("W1b", [128, E, 2, HID], F16)
        W2s = sb("W2s", [128, E, NC, 2, D], F16)
        tokW = sb("tokW", [128, 2, PATCH, D], F16)
        attWa = sb("attWa", [128, 2, 3 * D], F16)
        attWb = sb("attWb", [128, 2, 3 * D], F16)
        qkvWa = sb("qkvWa", [128, 2, 12 * 128 + D], F16)
        qkvWb = sb("qkvWb", [128, 2, 12 * 128 + D], F16)
        projW = sb("projW", [128, 2, 3, D], F16)
        gateWa = sb("gateWa", [128, 2, E], F16)
        gateWb = sb("gateWb", [128, 2, E], F16)
        b2s = sb("b2s", [E, D], F32)
        b1s = sb("b1s", [128, E, NC], F32)
        tokb = sb("tokb", [TP, D], F32)
        projb = sb("projb", [TP, D], F32)
        norms = sb("norms", [TP, 4, D], F32)
        qkb = sb("qkb", [128, 12], F32)
        qkmb = sb("qkmb", [128, 12], F32)
        vb = sb("vb", [128, 3], F32)
        cst = sb("cst", [128, C_N], F32)
        identb = sb("identb", [4, 4], BF16)
        ident = cst[:, C_ID:C_ID + 128]
        m64, mq, mk, m48 = (cst[:, c:c + 1] for c in (C_M64, C_MQ, C_MK, C_M48))
        cos, sin = cst[0:RH, C_COS:C_COS + T], cst[0:RH, C_SIN:C_SIN + T]
        cap = cst[0:TP, C_CAP:C_CAP + TP]
        rev = cst[0:TP, C_REV:C_REV + NT * E].rearrange("p (t e) -> p t e", t=NT)

        ximg = sb("ximg", [128, 2, CW], F32)
        xmask = sb("xmask", [128, CW], F16)
        XS = sb("XS", [128, CHUNKS * CW], F16)
        Hres = sb("Hres", [TP, NT, D], F32)
        Nrm = sb("Nrm", [TP, NT, D], F32)
        XF = sb("XF", [TP, NT, D], F32)
        R = sb("R", [TP, NT, D], F32)
        ACC = sb("ACC", [TP, NT, D], F32)
        XT = sb("XT", [128, 3, T], F16)
        XM = sb("XM", [128, 3, T], F16)
        QK = sb("QK", [128, 12, T], F16)
        QK1 = QK[0:RH, 0:8, :].rearrange("p (i s) t -> p i s t", s=2)
        V1 = sb("V1", [TP, 2, NT, D], F16)
        WS = sb("WS", [128, 4 * T + 6 * T], F32)
        tmp = WS[0:RH, 0:8 * T].rearrange("p (i t) -> p i t", t=T)
        S1 = WS[0:TP, 0:3 * T].rearrange("p (i t) -> p i t", t=T)
        Pr = WS[0:TP, 0:4 * T].rearrange("p (i t) -> p i t", t=T)
        PT = WS[0:TP, 4 * T:10 * T].bitcast(F16).rearrange("p (a s k t) -> p a s k t", a=2, s=2, k=3)
        qm = sb("qm", [128, 2, T], F16)
        trm = qm[:, 0, :]
        Vp = sb("Vp", [TP, 2, NT, HEADS, 32], F16)
        mx = sb("mx", [TP, NT, HEADS], F32)
        nmT = sb("nmT", [4, T], BF16)
        rsq = sb("rsq", [128, T], F32)
        rsi = sb("rsi", [128, T], F32)
        Os = sb("Os", [128, 2, 3, T], F16)
        st6 = sb("st6", [TP, NT, 6], F32)
        mv = sb("mv", [TP, NT, 2], F32)
        rstd = sb("rstd", [TP, NT], F32)
        veps = sb("veps", [TP, NT], F32)
        nm1 = sb("nm1", [TP, 4, NT], F32)
        rt = sb("rt", [TP, 8, NT, E], F32)
        rs = sb("rs", [TP, 8, NT], F32)
        G = sb("G", [TP, NT, E], F32)
        Gs = sb("Gs", [TP, NT, E], F32)
        GT = rsi[0:E, :]

        h32 = sb("h32", [128, 3, T], F32)
        Hs = sb("Hs", [128, 2, 2, NC, T], F16)

        M = [ctx.enter_context(nc.psum_tensor(f"M{i}", [128, 512], F32)) for i in range(2)]
        O = [ctx.enter_context(nc.psum_tensor(f"O{i}", [128, 512], F32)) for i in range(2)]
        TB = [ctx.enter_context(nc.psum_tensor(f"TB{i}", [128, 512], F32)) for i in range(4)]

        S = {name: sem(name) for name in PER}
        c_in, c_set = sem("c_in"), sem("c_set")
        stg_in = [sem(f"stg_in{i}") for i in range(4)]
        stg_hi, stg_lo = sem("stg_hi"), sem("stg_lo")
        big_in, prep_full, prep_hi, prep_lo = sem("big_in"), sem("prep_full"), sem("prep_hi"), sem("prep_lo")
        passed = sem("passed")
        pad_set, tok_dup = sem("pad_set"), sem("tok_dup")

        def due(name, b, k):
            return (b + 1) * PER[name] + k

        def one_ahead(eng, signals):
            for name, count in signals.items():
                eng.sem_inc(S[name], count)

        def dve_low(n):
            return 2 * (n // 3) + n % 3

        def apart(eng):
            eng.sem_inc(passed, 1)

        def bank_read(b, step, i):
            before = BEFORE[(step, i)]
            if before:
                return S[before[0]], due(before[0], b, before[1])
            last, k = LAST[BANK[(step, i)]]
            return S[last], due(last, b - 1, k)

        def bank(step, i):
            return TB[BANK[(step, i)]]

        big = Hs[:, :, :, :, :].rearrange("p a s c t -> p (a s c t)").bitcast(F32)
        tokS = big[0:96, 0:2 * 768].rearrange("p (a n) -> p a n", a=2)
        qkvS = big[0:96, 1536:1536 + 6 * D].rearrange("p (a n) -> p a n", a=6)
        projS = big[0:96, 2688:2688 + 768].rearrange("p (a g n) -> p a g n", a=2, g=3)
        tokD = XS[:, :].bitcast(F32)[0:96, 0:768].rearrange("p (s n m) -> p s n m", s=2, n=4)
        slot = [WS[:, 768 * i:768 * (i + 1)] for i in range(4)]
        stages = []

        def flat(ap):
            return ap

        for name, w, c0 in (("q", wq, 0), ("k", wk, D)):
            for half in range(2):
                for dst, rows in ((attWa, None), (attWb, 64)):
                    stages.append((w, rows, D, dst, c0 + half * RH, half, 1.0))
        for dst, rows in ((attWa, None), (attWb, 64)):
            stages.append((wv, rows, D, dst, 2 * D, None, 1.0))
        for dst, rows in ((gateWa, None), (gateWb, 64)):
            stages.append((w_gate, rows, E, dst, 0, None, WSC))
        for e in range(E):
            stages.append((w1[e], None, HID, W1a[:, e], 0, None, WSC))
            stages.append((w1[e], 64, HID, W1b[:, e], 0, None, WSC))
            for c in range(0, NC, 3):
                stages.append((w2[e], ("w2", c), 3 * D, W2s[:, e, c:c + 3], 0, "w2", WSC))

        def stage_views(i):
            src, rows, cols, dst, c0, pick, scale = stages[i]
            s = slot[i % 4]
            if pick == "w2":
                v = s[:, 0:cols].rearrange("p (c n) -> p c n", c=3)
                return v, dst[:, :, 0, :], dst[:, :, 1, :], scale
            if pick is None:
                return s[:, 0:cols], dst[:, 0, c0:c0 + cols], dst[:, 1, c0:c0 + cols], scale
            v = s[:, 0:cols].rearrange("p (j r) -> p j r", r=2)[:, :, pick]
            return v, dst[:, 0, c0:c0 + RH], dst[:, 1, c0:c0 + RH], scale

        preps = []
        for pw in range(0, PATCH, 2):
            preps.append(("tok", pw, 96, 2 * D, tokW[0:96, 0, pw:pw + 2, :], tokW[0:96, 1, pw:pw + 2, :], WSC))
        def four(w, sel, i):
            return w[:, sel, 768 * i:768 * i + 768].rearrange("p (h a d) -> p h a d", h=HEADS, a=4)

        for part, dst in (("a", qkvWa), ("b", qkvWb)):
            for i in range(2):
                preps.append(("qkv" + part, i, 128, D, four(dst, 0, i), four(dst, 1, i), 1.0))
            preps.append(("qkv" + part, 2, 128, D, dst[:, 0, 1536:], dst[:, 1, 1536:], 1.0))
        for half in range(2):
            cols = slice(96 * half, 96 * half + 96)
            preps.append(("proj", half, 128, 288, projW[:, 0, :, cols], projW[:, 1, :, cols], WSC))

        def prep_view(i):
            kind, at, rows, cols, hi, lo, scale = preps[i]
            v = TB[i % 3][0:rows, 0:cols]
            if kind == "tok":
                v = v.rearrange("p (w n) -> p w n", w=2)
            if kind == "proj":
                v = v.rearrange("p (g n) -> p g n", g=3)
            if kind[:3] == "qkv" and at < 2:
                v = v.rearrange("p (h a d) -> p h a d", h=HEADS, a=1).to_broadcast([128, HEADS, 4, HD])
            return v, hi, lo, scale

        N_C = [0]
        block = ctx.enter_context(nc.Block())

        @block.sync
        def _(sp):
            def const_in(dst, src):
                sp.dma_start(dst, src, allow_slow_non_contiguous=True).then_inc(c_in, 16)
                N_C[0] += 16

            const_in(cst[:, :], const)
            sp.wait_ge(pad_set, 2)
            sp.dma_start(tokS, tok_w.rearrange("(a p) n -> p a n", p=96)).then_inc(big_in, 16)
            sp.dma_start(qkvS, qkv_w.rearrange("(a p) n -> p a n", p=96)).then_inc(big_in, 16)
            for a in range(2):
                for g in range(3):
                    sp.dma_start(projS[:, a, g, :].rearrange("p (j r) -> p j r", r=32)[:, :, 0:HD],
                                 proj_w[96 * a:96 * a + 96, 64 * g:64 * g + 64].rearrange("p (j r) -> p j r", r=HD)
                                 ).then_inc(big_in, 16)
            const_in(tokb[:, :], tok_b.rearrange("(a n) -> a n", a=1).to_broadcast([TP, D]))
            const_in(projb[:, :], proj_b.rearrange("(a n) -> a n", a=1).to_broadcast([TP, D]))
            for i, v in enumerate((n1w, n1b, n2w, n2b)):
                const_in(norms[:, i, :], v.rearrange("(a n) -> a n", a=1).to_broadcast([TP, D]))
            for hh in range(2):
                for c in range(4):
                    const_in(qkb[64 * hh + 16 * c:64 * hh + 16 * c + 16, :],
                             qkv_b[0:2 * D].rearrange("(i h d) -> h d i", h=2, d=HD)[hh])
            for j in range(4):
                const_in(vb[32 * j:32 * j + HD, :], qkv_b[2 * D:3 * D].rearrange("(g j d) -> j d g", j=4, d=HD)[j])
            const_in(b2s[:, :], b2)
            for e in range(E):
                const_in(b1s[:, e, :], b1[e].rearrange("(c p) -> p c", p=128))
            for i, (src, rows, cols, dst, c0, pick, scale) in enumerate(stages):
                if i >= 4:
                    sp.wait_ge(stg_lo, i - 3)
                s = slot[i % 4]
                if pick == "w2":
                    c = rows[1]
                    sp.dma_start(s[:, 0:cols].rearrange("p (c n) -> p c n", c=3),
                                 src[128 * c:128 * (c + 3), :].rearrange("(c p) n -> p c n", p=128)
                                 ).then_inc(stg_in[i % 4], 32)
                elif rows is None:
                    sp.dma_start(s[:, 0:cols], src[0:128, :]).then_inc(stg_in[i % 4], 32)
                else:
                    for r in range(2):
                        sp.dma_start(s[64 * r:64 * r + 64, 0:cols], src[128:D, :]).then_inc(stg_in[i % 4], 16)

            def image(b, k):
                name = f"xin{k % 2}"
                sp.wait_ge(S["img_split"], due("img_split", b, k - 1 if k >= 2 else 0))
                rows = x[b].rearrange("c (h r) w -> c r h w", r=PATCH)
                for s in range(2):
                    for c in range(CH):
                        p = IMROWS * s + PATCH * c
                        sp.dma_start(ximg[p:p + PATCH, k % 2, :].rearrange("r (h w) -> r h w", h=2),
                                     rows[c, :, 2 * k:2 * k + 2, :]).then_inc(S[name], 16)

            def text(b):
                sp.wait_ge(S["r_sum"], due("r_sum", b - 1, 1))
                sp.dma_start(Hres[PT1:TP, 1, :], txt[b, 0:TP - PT1, :]).then_inc(S["txt_in"], 16)
                sp.dma_start(Hres[:, 2, :], txt[b, TP - PT1:NTEXT, :]).then_inc(S["txt_in"], 16)

            def store(m):
                sp.wait_ge(S["acc"], due("acc", m, 24))
                sp.dma_start(out[m].rearrange("(t p) d -> p t d", p=TP), ACC[:, :, :]).then_inc(S["out_done"], 16)

            def turn(b, m, ahead=True):
                text(b)
                if ahead:
                    for k in range(CHUNKS):
                        image(b + 1, k)
                if m is not None:
                    store(m)

            one_ahead(sp, SP_SIGNALS)
            for k in range(CHUNKS):
                image(0, k)
            turn(0, None)
            with sp.Fori(1, B - 1) as b:
                turn(b, b - 1)
            turn(B - 1, B - 2, False)
            store(B - 1)
            sp.wait_ge(S["out_done"], due("out_done", B - 1, 16))

        @block.gpsimd
        def _(pool):
            nc.gpsimd.memset(big[0:96, 2688:3456], 0.0).then_inc(pad_set, 1)
            nc.gpsimd.memset(vb[:, :], 0.0).then_inc(pad_set, 1)
            nc.gpsimd.memset(Vp[:, 0, :, :, :], 1.0).then_inc(pad_set, 1)
            nc.gpsimd.memset(Vp[:, 1, :, :, :], 0.0).then_inc(pad_set, 1)
            one_ahead(pool, POOL_SIGNALS)
            pool.wait_ge(big_in, 128)
            for i in range(PATCH // 2):
                if i >= 2:
                    pool.wait_ge(prep_full, i - 1)
                for w in range(2):
                    for a in range(2):
                        src = tokS[:, a, :].rearrange("p (r w c) -> p w c r", r=PATCH, w=PATCH)[:, 2 * i + w]
                        src = src.rearrange("p (s c) r -> p s c r", s=1).to_broadcast([96, 2, CH, PATCH])
                        last = nc.gpsimd.tensor_copy(
                            tokD[:, i % 2, 2 * w + a, :].rearrange("p (s c r) -> p s c r", s=2, c=CH), src)
                last.then_inc(tok_dup, 1)

            def qk1(b, i):
                pool.wait_ge(S["rope_mul"], due("rope_mul", b, i + 1))
                t0, t1, t2, t3 = (tmp[:, 4 * i + j, :] for j in range(4))
                nc.gpsimd.tensor_tensor(t0, t0, t2, ALU.subtract).then_inc(S["rope_sum"], 1)
                nc.gpsimd.tensor_tensor(t1, t1, t3, ALU.add).then_inc(S["rope_sum"], 1)
                for j, t in enumerate((t0, t1)):
                    pool.wait_ge(S["rope_hi"], due("rope_hi", b, 2 * i + j + 1))
                    nc.gpsimd.tensor_tensor(QK1[:, 2 * i + j, 1, :], t, QK1[:, 2 * i + j, 0, :],
                                            ALU.subtract).then_inc(S["rope_lo"], 1)

            def img(b, k):
                if k == 0:
                    pool.wait_ge(S["emb_full"], due("emb_full", b - 1, 2))
                pool.wait_ge(S["img_hi"], due("img_hi", b, k + 1))
                nc.gpsimd.tensor_tensor(XS[0:96, CW * k:CW * (k + 1)], ximg[0:96, k % 2, :], xmask[0:96, :],
                                        ALU.subtract).then_inc(S["img_split"], 1)

            def h_low(m, n):
                e, c = n // NC, n % NC
                pool.wait_ge(S["h_hi"], due("h_hi", m, n + 1))
                nc.gpsimd.tensor_tensor(Hs[:, e % 2, 1, c, :], h32[:, n % 3, :], Hs[:, e % 2, 0, c, :],
                                        ALU.subtract).then_inc(S["h_lo2"], 1)

            def inv_std(b, i):
                pool.wait_ge(S["ln_var"], due("ln_var", b, i + 1))
                nc.gpsimd.tensor_tensor(veps[:, :], mv[:, :, 1], cst[0:TP, C_EPS:C_EPS + NT],
                                        ALU.add).then_inc(S["ln_eps"], 1)
                pool.wait_ge(S["ln_eps"], due("ln_eps", b, i + 1))
                nc.gpsimd.tensor_tensor(rstd[:, :], veps[:, :], cst[0:TP, C_POW:C_POW + NT],
                                        ALU.pow).then_inc(S["ln_rstd"], 1)

            def pv1(b):
                inv_std(b, 1)
                pool.wait_ge(S["xf_ready"], due("xf_ready", b, 1))
                nc.gpsimd.tensor_tensor(R[:, :, :], XF[:, :, :],
                                        projb[:, :].rearrange("p (a n) -> p a n", a=1).to_broadcast([TP, NT, D]),
                                        ALU.add).then_inc(S["xfb_ready"], 1)
                inv_std(b, 2)

            def att2(b, h):
                pool.wait_ge(S["pt_hi"], due("pt_hi", b, 3 * h + 3))
                nc.gpsimd.tensor_tensor(PT[:, h % 2, 1, 2, :], Pr[:, (3 * h + 2) % 4, :], PT[:, h % 2, 0, 2, :],
                                        ALU.subtract).then_inc(S["pt_lo2"], 1)

            def pj(b):
                inv_std(b, 3)
                pool.wait_ge(S["x1_done"], due("x1_done", b, 3))
                nc.gpsimd.tensor_tensor(R[:, :, :], Hres[:, :, :], XF[:, :, :], ALU.add).then_inc(S["r_sum"], 1)

            def turn(b, m, ahead=True):
                for step in order(m is not None, b is not None, ahead):
                    if step[0] == "W1" and (NC * step[1] + step[2]) % 3 == 0 and step[1:] != (0, 0):
                        h_low(m, NC * step[1] + step[2] - 1)
                    elif step == ("W2", E - 2, 0):
                        h_low(m, NC * E - 1)
                    elif step[0] == "img":
                        img(b + 1, step[1])
                    elif step[0] == "emb":
                        inv_std(b, 0)
                    elif step[0] == "qk1":
                        qk1(b, step[1])
                    elif step[0] == "pv1":
                        pv1(b)
                    elif step[0] == "att2":
                        att2(b, step[1])
                    elif step[0] == "pj":
                        pj(b)

            for k in range(CHUNKS):
                img(0, k)
            turn(0, None)
            with pool.Fori(1, B - 1) as b:
                turn(b, b - 1)
            turn(B - 1, B - 2, False)
            turn(None, B - 1)

        @block.scalar
        def _(act):
            one_ahead(act, ACT_SIGNALS)
            act.wait_ge(c_in, 16)
            for i in range(len(preps)):
                v, hi, lo, scale = prep_view(i)
                act.wait_ge(prep_full, i + 1)
                nc.scalar.activation(hi, v, ACT.Copy, scale=scale).then_inc(prep_hi, 1)
            for i in range(len(stages)):
                v, hi, lo, scale = stage_views(i)
                act.wait_ge(stg_in[i % 4], 32 * (i // 4 + 1))
                nc.scalar.activation(hi, v, ACT.Copy, scale=scale).then_inc(stg_hi, 1)
            act.wait_ge(c_set, 1)

            def img(b, k):
                act.wait_ge(S[f"xin{k % 2}"], due(f"xin{k % 2}", b, (k // 2 + 1) * XIN))
                act.wait_ge(S["img_split"], due("img_split", b, k))
                nc.scalar.activation(xmask[0:96, :], ximg[0:96, k % 2, :], ACT.Identity,
                                     scale=m48[0:96, :]).then_inc(S["img_hi"], 1)

            def tr(b, i):
                dst = XM if i == 2 else XT
                act.wait_ge(S["tr_full"], due("tr_full", b, 2 * i + 1))
                nc.scalar.activation(dst[:, 0, :], bank("tr", 2 * i)[:, 0:T], ACT.Copy).then_inc(S["tr_hi"], 1)
                act.wait_ge(S["tr_full"], due("tr_full", b, 2 * i + 2))
                nc.scalar.activation(trm, bank("tr", 2 * i + 1)[:, 0:T], ACT.Identity,
                                     scale=m64).then_inc(S["tr_hi"], 1)

            def qk1(b, i):
                for j in range(2):
                    act.wait_ge(S["rope_sum"], due("rope_sum", b, 2 * i + j + 1))
                    nc.scalar.activation(QK1[:, 2 * i + j, 0, :], tmp[:, 4 * i + j, :],
                                         ACT.Copy).then_inc(S["rope_hi"], 1)

            def v1(b):
                for t in range(NT):
                    act.wait_ge(S["v1_full"], due("v1_full", b, t + 1))
                    nc.scalar.activation(V1[:, 0, t, :], bank("v1", t)[0:TP, 0:D], ACT.Copy).then_inc(S["v1_hi"], 1)

            def s1(b):
                act.wait_ge(S["m1_ready"], due("m1_ready", b, 1))
                for t in range(NT):
                    w = TP * (t + 1)
                    nc.scalar.activation(S1[:, t, 0:w], S1[:, t, 0:w], ACT.Exp, bias=nm1[:, 1, t:t + 1], scale=SCALE1,
                                         accum_out=nm1[:, 2, t:t + 1]).then_inc(S["p1_ready"], 1)

            def p1t(b):
                for kt in range(NT):
                    act.wait_ge(S["p1t_full"], due("p1t_full", b, kt + 1))
                    nc.scalar.activation(PT[:, 0, 0, kt, TP * kt:T], bank("p1t", kt)[0:TP, TP * kt:T],
                                         ACT.Copy).then_inc(S["p1t_hi"], 1)

            def qk2(b, i):
                for j in (2 * i, 2 * i + 1):
                    mask = mq if j < 6 else mk
                    act.wait_ge(S["qk2_full"], due("qk2_full", b, j + 1))
                    act.wait_ge(S["qk2_done"], due("qk2_done", b, j - 1))
                    nc.scalar.activation(qm[:, j % 2, :], bank("qk2", j)[:, 0:T], ACT.Identity, scale=mask,
                                         bias=qkmb[:, j:j + 1]).then_inc(S["qk2_m"], 1)

            def v2(b):
                for t in range(NT):
                    act.wait_ge(S["v2_full"], due("v2_full", b, t + 1))
                    nc.scalar.activation(Vp[:, 0, t, :, 0:HD],
                                         bank("v2", t)[0:TP, 0:D].rearrange("p (h d) -> p h d", h=HEADS),
                                         ACT.Copy).then_inc(S["v2_hi"], 1)

            def scale(b, g):
                act.wait_ge(S["pv_norm"], due("pv_norm", b, g + 1))
                nc.scalar.activation(Os[:, 0, g, :], rsq[:, :], ACT.Identity,
                                     bias=vb[:, g:g + 1]).then_inc(S["o_hi"], 1)

            def att2(b, h):
                for kt in range(3):
                    n = 3 * h + kt
                    act.wait_ge(S["st_full"], due("st_full", b, n + 1))
                    if kt == 0:
                        act.wait_ge(S["pt_lo2"], due("pt_lo2", b, h - 1))
                    else:
                        act.wait_ge(S["pt_lo"], due("pt_lo", b, 2 * (h - 1) + kt))
                    nc.scalar.activation(Pr[:, n % 4, :], bank("st", n)[0:TP, 0:T], ACT.Exp,
                                         scale=SCALE2).then_inc(S["st_exp"], 1)

            def gate(b):
                act.wait_ge(S["gate_tanh_in"], due("gate_tanh_in", b, 1))
                nc.scalar.activation(rs[:, 6, :], rs[:, 5, :], ACT.Tanh, scale=0.5).then_inc(S["gate_tanh"], 1)

            def w1_gelu(m, e, c):
                n = NC * e + c
                act.wait_ge(S["w1_full"], due("w1_full", m, n + 1))
                if n % 3 == 2:
                    act.wait_ge(S["h_lo2"], due("h_lo2", m, n // 3))
                else:
                    act.wait_ge(S["h_lo"], due("h_lo", m, dve_low(n - 2)))
                nc.scalar.activation(h32[:, n % 3, :], M[n % 2][:, 0:T], ACT.Gelu, bias=b1s[:, e, c:c + 1],
                                     scale=1.0 / WSC).then_inc(S["gelu"], 1)
                if c == 0:
                    act.wait_ge(S["o_full"], due("o_full", m, 3 * (e - 1)))
                act.wait_ge(S["gelu"], due("gelu", m, n + 1))
                nc.scalar.activation(Hs[:, e % 2, 0, c, :], h32[:, n % 3, :], ACT.Copy).then_inc(S["h_hi"], 1)

            def turn(b, m, ahead=True):
                for step in order(m is not None, b is not None, ahead):
                    kind = step[0]
                    if kind == "W1":
                        w1_gelu(m, step[1], step[2])
                    elif kind == "img":
                        img(b + 1, step[1])
                    elif kind == "tr":
                        tr(b, step[1])
                    elif kind == "qk1":
                        qk1(b, step[1])
                    elif kind == "v1":
                        v1(b)
                    elif kind == "s1":
                        s1(b)
                    elif kind == "p1t":
                        p1t(b)
                    elif kind == "qk2":
                        qk2(b, step[1])
                    elif kind == "v2":
                        v2(b)
                    elif kind == "att2":
                        att2(b, step[1])
                    elif kind == "scale":
                        scale(b, step[1])
                    elif kind == "gate":
                        gate(b)

            for k in range(CHUNKS):
                img(0, k)
            turn(0, None)
            with act.Fori(1, B - 1) as b:
                turn(b, b - 1)
            turn(B - 1, B - 2, False)
            turn(None, B - 1)

        @block.vector
        def _(dve):
            one_ahead(dve, DVE_SIGNALS)
            for i in range(len(preps)):
                v, hi, lo, scale = prep_view(i)
                dve.wait_ge(prep_hi, i + 1)
                if scale == 1.0:
                    nc.vector.tensor_tensor(lo, v, hi, ALU.subtract).then_inc(prep_lo, 1)
                else:
                    nc.vector.scalar_tensor_tensor(lo, v, scale, hi, ALU.mult, ALU.subtract).then_inc(prep_lo, 1)
            for i in range(len(stages)):
                v, hi, lo, scale = stage_views(i)
                dve.wait_ge(stg_hi, i + 1)
                nc.vector.scalar_tensor_tensor(lo, v, scale, hi, ALU.mult, ALU.subtract).then_inc(stg_lo, 1)
            dve.wait_ge(c_in, N_C[0])
            nc.vector.tensor_copy(identb[:, :], cst[0:4, 0:4])
            nc.vector.tensor_scalar(qkmb[:, 0:6], qkb[:, 0:6], mq, None, ALU.mult)
            nc.vector.tensor_scalar(qkmb[:, 6:12], qkb[:, 6:12], mk, None, ALU.mult).then_inc(c_set, 1)

            steps = [0]

            def step_done(b, ins):
                ins.then_inc(S["dve_step"], 1)
                steps[0] += 1

            def stats(b, src):
                for t in range(NT):
                    step_done(b, nc.vector.bn_stats(st6[:, t, :], src[:, t, :]))
                dve.wait_ge(S["dve_step"], due("dve_step", b, steps[0]))
                apart(dve)
                for t in range(NT):
                    last = nc.vector.bn_aggr(mv[:, t, :], st6[:, t, :])
                last.then_inc(S["ln_var"], 1)

            def norm_affine(b, src, w):
                for t in range(NT):
                    step_done(b, nc.vector.scalar_tensor_tensor(Nrm[:, t, :], src[:, t, :], mv[:, t, 0:1],
                                                                norms[:, w, :], ALU.subtract, ALU.mult))
                dve.wait_ge(S["dve_step"], due("dve_step", b, steps[0]))
                for t in range(NT):
                    last = nc.vector.scalar_tensor_tensor(Nrm[:, t, :], Nrm[:, t, :], rstd[:, t:t + 1],
                                                          norms[:, w + 1, :], ALU.mult, ALU.add)
                last.then_inc(S["n_ready"], 1)

            def emb(b):
                dve.wait_ge(S["r_sum"], due("r_sum", b - 1, 1))
                for t, rows in ((0, TP), (1, PT1)):
                    dve.wait_ge(S["emb_full"], due("emb_full", b, t + 1))
                    nc.vector.scalar_tensor_tensor(Hres[0:rows, t, :], bank("emb", t)[0:rows, 0:D], 1.0 / WSC,
                                                   tokb[0:rows, :], ALU.mult, ALU.add).then_inc(S["emb_evac"], 1)
                dve.wait_ge(S["emb_evac"], due("emb_evac", b, 2))
                dve.wait_ge(S["txt_in"], due("txt_in", b, 32))
                stats(b, Hres)

            def ln(b, i):
                dve.wait_ge(S["ln_rstd"], due("ln_rstd", b, i + 1))
                if i == 0:
                    dve.wait_ge(S["tr_full"], due("tr_full", b - 1, 6))
                    for t in range(NT):
                        last = nc.vector.tensor_scalar(Nrm[:, t, :], Hres[:, t, :], mv[:, t, 0:1], rstd[:, t:t + 1],
                                                       ALU.subtract, ALU.mult)
                    last.then_inc(S["n_ready"], 1)
                elif i == 1:
                    for t in range(NT):
                        last = nc.vector.tensor_scalar(XF[:, t, :], Hres[:, t, :], mv[:, t, 0:1], rstd[:, t:t + 1],
                                                       ALU.subtract, ALU.mult)
                    last.then_inc(S["xf_ready"], 1)
                    dve.wait_ge(S["xf_ready"], due("xf_ready", b, 1))
                    stats(b, XF)
                else:
                    norm_affine(b, XF, 2 * (i - 2))

            def tr(b, i):
                dst = XM if i == 2 else XT
                dve.wait_ge(S["tr_hi"], due("tr_hi", b, 2 * i + 1))
                nc.vector.tensor_tensor(dst[:, 1, :], bank("tr", 2 * i)[:, 0:T], dst[:, 0, :],
                                        ALU.subtract).then_inc(S["tr_lo"], 1)
                dve.wait_ge(S["tr_hi"], due("tr_hi", b, 2 * i + 2))
                nc.vector.tensor_tensor(dst[:, 2, :], bank("tr", 2 * i + 1)[:, 0:T], trm,
                                        ALU.subtract).then_inc(S["tr_lo"], 1)

            def qk1(b, i):
                re, im = bank("qk1", 2 * i)[0:RH, 0:T], bank("qk1", 2 * i + 1)[0:RH, 0:T]
                dve.wait_ge(S["qk1_full"], due("qk1_full", b, 2 * i + 1))
                nc.vector.tensor_tensor(tmp[:, 4 * i, :], re, cos, ALU.mult)
                nc.vector.tensor_tensor(tmp[:, 4 * i + 1, :], re, sin, ALU.mult).then_inc(S["rope_re"], 1)
                dve.wait_ge(S["qk1_full"], due("qk1_full", b, 2 * i + 2))
                nc.vector.tensor_tensor(tmp[:, 4 * i + 2, :], im, sin, ALU.mult)
                nc.vector.tensor_tensor(tmp[:, 4 * i + 3, :], im, cos, ALU.mult).then_inc(S["rope_mul"], 1)

            def v1(b):
                for t in range(NT):
                    dve.wait_ge(S["v1_hi"], due("v1_hi", b, t + 1))
                    nc.vector.tensor_tensor(V1[:, 1, t, :], bank("v1", t)[0:TP, 0:D], V1[:, 0, t, :],
                                            ALU.subtract).then_inc(S["v1_lo"], 1)

            def s1(b):
                for t in range(NT):
                    ps = bank("s1", t)
                    dve.wait_ge(S["s1_full"], due("s1_full", b, t + 1))
                    if t:
                        nc.vector.tensor_copy(S1[:, t, 0:TP * t], ps[0:TP, 0:TP * t])
                    nc.vector.tensor_tensor(S1[:, t, TP * t:TP * t + TP], ps[0:TP, TP * t:TP * t + TP], cap,
                                            ALU.min).then_inc(S["s1_evac"], 1)
                dve.wait_ge(S["s1_evac"], due("s1_evac", b, 3))
                for t in range(NT):
                    step_done(b, nc.vector.tensor_reduce(nm1[:, 0, t:t + 1], S1[:, t, 0:TP * (t + 1)], AX.X, ALU.max))
                dve.wait_ge(S["dve_step"], due("dve_step", b, steps[0]))
                nc.vector.tensor_scalar(nm1[:, 1, :], nm1[:, 0, :], -SCALE1, None, ALU.mult).then_inc(S["m1_ready"], 1)

            def p1t(b):
                for kt in range(NT):
                    dve.wait_ge(S["p1t_hi"], due("p1t_hi", b, kt + 1))
                    nc.vector.tensor_tensor(PT[:, 0, 1, kt, TP * kt:T], bank("p1t", kt)[0:TP, TP * kt:T],
                                            PT[:, 0, 0, kt, TP * kt:T], ALU.subtract).then_inc(S["p1t_lo"], 1)
                dve.wait_ge(S["p1_ready"], due("p1_ready", b, 3))
                step_done(b, nc.vector.reciprocal(nm1[:, 3, :], nm1[:, 2, :]))
                dve.wait_ge(S["dve_step"], due("dve_step", b, steps[0]))

            def pv1(b):
                for t in range(NT):
                    dve.wait_ge(S["pv1_full"], due("pv1_full", b, t + 1))
                    nc.vector.scalar_tensor_tensor(Hres[:, t, :], bank("pv1", t)[0:TP, 0:D], nm1[:, 3, t:t + 1],
                                                   Hres[:, t, :], ALU.mult, ALU.add).then_inc(S["pv1_evac"], 1)
                dve.wait_ge(S["pv1_evac"], due("pv1_evac", b, 3))
                stats(b, Hres)

            def qk2(b, i):
                for j in (2 * i, 2 * i + 1):
                    dve.wait_ge(S["qk2_m"], due("qk2_m", b, j + 1))
                    nc.vector.scalar_tensor_tensor(QK[:, j, :], bank("qk2", j)[:, 0:T], qkb[:, j:j + 1], qm[:, j % 2, :],
                                                   ALU.add, ALU.subtract).then_inc(S["qk2_done"], 1)

            def v2(b):
                for t in range(NT):
                    dve.wait_ge(S["v2_hi"], due("v2_hi", b, t + 1))
                    nc.vector.tensor_tensor(Vp[:, 1, t, :, 0:HD],
                                            bank("v2", t)[0:TP, 0:D].rearrange("p (h d) -> p h d", h=HEADS),
                                            Vp[:, 0, t, :, 0:HD], ALU.subtract).then_inc(S["v2_lo"], 1)

            def s(b, h):
                for qt in range(NT):
                    n = 3 * h + qt
                    dve.wait_ge(S["s_full"], due("s_full", b, n + 1))
                    nc.vector.tensor_reduce(mx[:, qt, h:h + 1], bank("s", n)[0:TP, 0:T], AX.X,
                                            ALU.max).then_inc(S["s_max"], 1)

            def mt(b, g):
                dve.wait_ge(S["mt_full"], due("mt_full", b, g + 1))
                dve.wait_ge(S["st_full"], due("st_full", b, 12 * g))
                nc.vector.tensor_scalar(nmT[:, :], bank("mt", g)[0:4, 0:T], -1.0, None,
                                        ALU.mult).then_inc(S["mt_done"], 1)

            def norm(b, g):
                ps = bank("pv", g)[:, 0:T]
                dve.wait_ge(S["pv_done"], due("pv_done", b, 4 * g + 4))
                apart(dve)
                nc.vector.stream_shuffle(rsi[:, :], ps, [16 + i % 16 for i in range(32)]).then_inc(S["sum_out"], 1)
                dve.wait_ge(S["sum_out"], due("sum_out", b, g + 1))
                nc.vector.reciprocal(rsi[:, :], rsi[:, :]).then_inc(S["sum_inv"], 1)

            def scale(b, g):
                dve.wait_ge(S["sum_inv"], due("sum_inv", b, g + 1))
                nc.vector.tensor_tensor(rsq[:, :], bank("pv", g)[:, 0:T], rsi[:, :], ALU.mult).then_inc(S["pv_norm"], 1)

            def o_split(b, g):
                dve.wait_ge(S["o_hi"], due("o_hi", b, g + 1))
                nc.vector.scalar_tensor_tensor(Os[:, 1, g, :], rsq[:, :], vb[:, g:g + 1], Os[:, 0, g, :],
                                               ALU.add, ALU.subtract).then_inc(S["o_lo"], 1)

            def att2(b, h):
                dve.wait_ge(S["pv_done"], due("pv_done", b, h - 1))
                for kt in range(3):
                    n = 3 * h + kt
                    dve.wait_ge(S["st_exp"], due("st_exp", b, n + 1))
                    nc.vector.tensor_copy(PT[:, h % 2, 0, kt, :], Pr[:, n % 4, :]).then_inc(S["pt_hi"], 1)
                for kt in range(2):
                    n = 3 * h + kt
                    dve.wait_ge(S["pt_hi"], due("pt_hi", b, n + 1))
                    nc.vector.tensor_tensor(PT[:, h % 2, 1, kt, :], Pr[:, n % 4, :], PT[:, h % 2, 0, kt, :],
                                            ALU.subtract).then_inc(S["pt_lo"], 1)

            def pj(b):
                dve.wait_ge(S["xfb_ready"], due("xfb_ready", b, 1))
                for t in range(NT):
                    dve.wait_ge(S["pj_full"], due("pj_full", b, t + 1))
                    nc.vector.scalar_tensor_tensor(XF[:, t, :], bank("pj", t)[0:TP, 0:D], 1.0 / WSC, R[:, t, :],
                                                   ALU.mult, ALU.add).then_inc(S["x1_done"], 1)
                dve.wait_ge(S["x1_done"], due("x1_done", b, 3))
                stats(b, XF)

            def gate(b):
                def wide(ap):
                    return ap.rearrange("p (t a) -> p t a", a=1).to_broadcast([TP, NT, E])

                L, eq, c1, one1, L2, one2 = (rt[:, i] for i in range(6))
                top1, first1, top2, first2 = (rs[:, i, :] for i in range(4))
                dve.wait_ge(S["gate_full"], due("gate_full", b, 1))
                nc.vector.tensor_scalar(L, bank("gate", 0)[0:TP, 0:NT * E].rearrange("p (t e) -> p t e", e=E),
                                        1.0 / WSC, None, ALU.mult).then_inc(S["gate_evac"], 1)
                dve.wait_ge(S["gate_evac"], due("gate_evac", b, 1))
                for src, top, first, one in ((L, top1, first1, one1), (L2, top2, first2, one2)):
                    step_done(b, nc.vector.tensor_reduce(top, src, AX.X, ALU.max))
                    dve.wait_ge(S["dve_step"], due("dve_step", b, steps[0]))
                    step_done(b, nc.vector.tensor_tensor(eq, src, wide(top), ALU.is_ge))
                    dve.wait_ge(S["dve_step"], due("dve_step", b, steps[0]))
                    step_done(b, nc.vector.tensor_tensor(c1, eq, rev, ALU.mult))
                    dve.wait_ge(S["dve_step"], due("dve_step", b, steps[0]))
                    step_done(b, nc.vector.tensor_reduce(first, c1, AX.X, ALU.max))
                    dve.wait_ge(S["dve_step"], due("dve_step", b, steps[0]))
                    step_done(b, nc.vector.tensor_tensor(one, c1, wide(first), ALU.is_equal))
                    dve.wait_ge(S["dve_step"], due("dve_step", b, steps[0]))
                    if one is one1:
                        step_done(b, nc.vector.scalar_tensor_tensor(L2, one1, -3.0e38, L, ALU.mult, ALU.add))
                        dve.wait_ge(S["dve_step"], due("dve_step", b, steps[0]))
                nc.vector.tensor_tensor(rs[:, 5, :], top1, top2, ALU.subtract).then_inc(S["gate_tanh_in"], 1)
                dve.wait_ge(S["gate_tanh"], due("gate_tanh", b, 1))
                step_done(b, nc.vector.tensor_scalar(rs[:, 4, :], rs[:, 6, :], 0.5, 0.5, ALU.mult, ALU.add))
                step_done(b, nc.vector.tensor_scalar(rs[:, 7, :], rs[:, 6, :], -0.5, 0.5, ALU.mult, ALU.add))
                dve.wait_ge(S["dve_step"], due("dve_step", b, steps[0]))
                step_done(b, nc.vector.tensor_tensor(eq, one1, wide(rs[:, 4, :]), ALU.mult))
                step_done(b, nc.vector.tensor_tensor(c1, one2, wide(rs[:, 7, :]), ALU.mult))
                dve.wait_ge(S["dve_step"], due("dve_step", b, steps[0]))
                nc.vector.tensor_tensor(G[:, :, :], eq, c1, ALU.add).then_inc(S["g_ready"], 1)

            def gt(b):
                dve.wait_ge(S["gt_full"], due("gt_full", b, 1))
                nc.vector.tensor_copy(GT, bank("gt", 0)[0:E, 0:T]).then_inc(S["gt_done"], 1)

            def b2_step(b):
                dve.wait_ge(S["g_ready"], due("g_ready", b, 1))
                dve.wait_ge(S["acc"], due("acc", b - 1, 24))
                nc.vector.tensor_scalar(Gs[:, :, :], G[:, :, :], 1.0 / WSC, None, ALU.mult)
                dve.wait_ge(S["r_sum"], due("r_sum", b, 1))
                for t in range(NT):
                    dve.wait_ge(S["b2_full"], due("b2_full", b, t + 1))
                    nc.vector.tensor_tensor(R[:, t, :], bank("b2", t)[0:TP, 0:D], R[:, t, :],
                                            ALU.add).then_inc(S["r_ready"], 1)

            def h_low(m, n):
                e, c = n // NC, n % NC
                dve.wait_ge(S["h_hi"], due("h_hi", m, n + 1))
                nc.vector.tensor_tensor(Hs[:, e % 2, 1, c, :], h32[:, n % 3, :], Hs[:, e % 2, 0, c, :],
                                        ALU.subtract).then_inc(S["h_lo"], 1)

            def w2_acc(m, e, t):
                if t == 0:
                    return
                if e == 0 and t == 1:
                    dve.wait_ge(S["out_done"], due("out_done", m, 0))
                    dve.wait_ge(S["r_ready"], due("r_ready", m, 3))
                else:
                    dve.wait_ge(S["acc"], due("acc", m, 3 * e - 3 + (2 if t == 1 else 3)))
                dve.wait_ge(S["o_full"], due("o_full", m, 3 * e + t + 1))
                for u in ((0, 1) if t == 1 else (2,)):
                    ps = O[0][0:TP, D * u:D * u + D] if u < 2 else O[1][0:TP, 0:D]
                    nc.vector.scalar_tensor_tensor(ACC[:, u, :], ps, Gs[:, u, e:e + 1],
                                                   (R if e == 0 else ACC)[:, u, :], ALU.mult,
                                                   ALU.add).then_inc(S["acc"], 1)

            def turn(b, m, ahead=True):
                steps[0] = 0
                for step in order(m is not None, b is not None, ahead):
                    kind = step[0]
                    if kind == "W1":
                        n = NC * step[1] + step[2]
                        if n and (n - 1) % 3 < 2:
                            h_low(m, n - 1)
                    elif kind == "W2":
                        w2_acc(m, step[1], step[2])
                    elif kind == "emb":
                        emb(b)
                    elif kind == "ln":
                        ln(b, step[1])
                    elif kind == "norm":
                        norm(b, step[1])
                    elif kind == "scale":
                        scale(b, step[1])
                    elif kind == "osplit":
                        o_split(b, step[1])
                    elif kind == "tr":
                        tr(b, step[1])
                    elif kind == "qk1":
                        qk1(b, step[1])
                    elif kind == "v1":
                        v1(b)
                    elif kind == "s1":
                        s1(b)
                    elif kind == "p1t":
                        p1t(b)
                    elif kind == "pv1":
                        pv1(b)
                    elif kind == "qk2":
                        qk2(b, step[1])
                    elif kind == "v2":
                        v2(b)
                    elif kind == "s":
                        s(b, step[1])
                    elif kind == "mt":
                        mt(b, step[1])
                    elif kind == "att2":
                        att2(b, step[1])
                    elif kind == "pj":
                        pj(b)
                    elif kind == "gate":
                        gate(b)
                    elif kind == "gt":
                        gt(b)
                    elif kind == "b2":
                        b2_step(b)
                assert b is None or steps[0] == DVE_STEPS, steps[0]

            turn(0, None)
            with dve.Fori(1, B - 1) as b:
                turn(b, b - 1)
            turn(B - 1, B - 2, False)
            turn(None, B - 1)

        @block.tensor
        def _(pe):
            one_ahead(pe, PE_SIGNALS)
            pe.wait_ge(c_in, 16)
            pe.wait_ge(big_in, 128)

            def turn_twice(ps, c0, src, n):
                nc.tensor.transpose(ps[:, c0:c0 + n], src[:, D - 128:D], ident[0:n, 0:n])
                return nc.tensor.transpose(ps[0:KB, c0:c0 + n], src[:, KA:D], ident[0:n, 0:n])

            for i, (kind, at, rows, cols, _hi, _lo, _sc) in enumerate(preps):
                ps = TB[i % 3]
                if i >= 3:
                    pe.wait_ge(prep_lo, i - 2)
                if kind == "tok":
                    pe.wait_ge(tok_dup, i + 1)
                    for n in range(4):
                        last = nc.tensor.transpose(ps[0:96, 96 * n:96 * n + 96], tokD[:, i % 2, n, :], ident[0:96, 0:96])
                elif kind == "qkva":
                    for a in range(2):
                        last = nc.tensor.transpose(ps[:, 96 * a:96 * a + 96], qkvS[:, 2 * at + a, 0:KA], ident[0:96, 0:96])
                elif kind == "qkvb":
                    for a in range(2):
                        last = turn_twice(ps, 96 * a, qkvS[:, 2 * at + a, :], 96)
                else:
                    for g in range(3):
                        last = nc.tensor.transpose(ps[:, 96 * g:96 * g + 96], projS[:, at, g, :], ident[0:96, 0:96])
                last.then_inc(prep_full, 1)
            pe.wait_ge(c_set, 1)
            pe.wait_ge(pad_set, 4)

            def five(out_ap, pairs):
                for i, (lhsT, rhs) in enumerate(pairs):
                    last = nc.tensor.matmul(out_ap, lhsT, rhs, start=(i == 0), stop=(i == len(pairs) - 1))
                return last

            def emb(b):
                pe.wait_ge(S["img_split"], due("img_split", b, CHUNKS))
                xv = XS[0:96, :].rearrange("p (t w) -> p w t", w=PATCH)
                for t, n in ((0, TP), (1, PT1)):
                    pe.wait_ge(*bank_read(b, "emb", t))
                    five(bank("emb", t)[0:n, 0:D],
                         [(xv[:, w, TP * t:TP * t + n], tokW[0:96, s, w, :]) for w in range(PATCH) for s in range(2)]
                         ).then_inc(S["emb_full"], 1)

            def tr(b, i):
                pe.wait_ge(S["n_ready"], due("n_ready", b, i + 1))
                pe.wait_ge(*bank_read(b, "tr", 2 * i))
                for t in range(NT):
                    last = nc.tensor.transpose(bank("tr", 2 * i)[:, TP * t:TP * t + TP], Nrm[:, t, 0:KA],
                                               ident[0:TP, 0:TP])
                last.then_inc(S["tr_full"], 1)
                pe.wait_ge(*bank_read(b, "tr", 2 * i + 1))
                for t in range(NT):
                    last = turn_twice(bank("tr", 2 * i + 1), TP * t, Nrm[:, t, :], TP)
                last.then_inc(S["tr_full"], 1)

            def by_weight(wa, wb, pick, X):
                return [(pick(wa, 0), X[:, 0, :]), (pick(wa, 1), X[:, 0, :]), (pick(wa, 0), X[:, 1, :]),
                        (pick(wb, 0), X[:, 2, :]), (pick(wb, 1), X[:, 2, :])]

            def by_token(wa, wb, pick, X, t):
                c = slice(TP * t, TP * t + TP)
                return [(X[:, 0, c], pick(wa, 0)), (X[:, 0, c], pick(wa, 1)), (X[:, 1, c], pick(wa, 0)),
                        (X[:, 2, c], pick(wb, 0)), (X[:, 2, c], pick(wb, 1))]

            def qk1(b, i):
                pe.wait_ge(S["tr_lo"], due("tr_lo", b, 2))
                for j in (2 * i, 2 * i + 1):
                    pe.wait_ge(*bank_read(b, "qk1", j))
                    five(bank("qk1", j)[0:RH, 0:T],
                         by_weight(attWa, attWb, lambda w, s: w[:, s, RH * j:RH * j + RH], XT)
                         ).then_inc(S["qk1_full"], 1)

            def v1(b):
                for t in range(NT):
                    pe.wait_ge(*bank_read(b, "v1", t))
                    five(bank("v1", t)[0:TP, 0:D], by_token(attWa, attWb, lambda w, s: w[:, s, 2 * D:3 * D], XT, t)
                         ).then_inc(S["v1_full"], 1)

            def s1(b):
                pe.wait_ge(S["rope_lo"], due("rope_lo", b, 4))
                for t in range(NT):
                    w = TP * (t + 1)
                    pe.wait_ge(*bank_read(b, "s1", t))
                    five(bank("s1", t)[0:TP, 0:w],
                         [(QK1[:, j, qs, TP * t:w], QK1[:, 2 + j, ks, 0:w])
                          for j in range(2) for qs, ks in ((0, 0), (0, 1), (1, 0))]).then_inc(S["s1_full"], 1)

            def p1t(b):
                pe.wait_ge(S["p1_ready"], due("p1_ready", b, 3))
                for kt in range(NT):
                    pe.wait_ge(*bank_read(b, "p1t", kt))
                    for qt in range(kt, NT):
                        last = nc.tensor.transpose(bank("p1t", kt)[0:TP, TP * qt:TP * qt + TP],
                                                   S1[:, qt, TP * kt:TP * kt + TP], ident[0:TP, 0:TP])
                    last.then_inc(S["p1t_full"], 1)

            def pv1(b):
                pe.wait_ge(S["p1t_lo"], due("p1t_lo", b, 3))
                pe.wait_ge(S["v1_lo"], due("v1_lo", b, 3))
                for t in range(NT):
                    pe.wait_ge(*bank_read(b, "pv1", t))
                    five(bank("pv1", t)[0:TP, 0:D],
                         [(PT[:, 0, ps, kt, TP * t:TP * t + TP], V1[:, vs, kt, :])
                          for kt in range(t + 1) for ps, vs in ((0, 0), (0, 1), (1, 0))]).then_inc(S["pv1_full"], 1)

            def qk2(b, i):
                pe.wait_ge(S["tr_lo"], due("tr_lo", b, 4))
                for j in (2 * i, 2 * i + 1):
                    pe.wait_ge(*bank_read(b, "qk2", j))
                    five(bank("qk2", j)[:, 0:T],
                         by_weight(qkvWa, qkvWb, lambda w, s: w[:, s, 128 * j:128 * j + 128], XT)
                         ).then_inc(S["qk2_full"], 1)

            def v2(b):
                for t in range(NT):
                    pe.wait_ge(*bank_read(b, "v2", t))
                    five(bank("v2", t)[0:TP, 0:D], by_token(qkvWa, qkvWb, lambda w, s: w[:, s, 1536:1536 + D], XT, t)
                         ).then_inc(S["v2_full"], 1)

            def s(b, h):
                pe.wait_ge(S["qk2_done"], due("qk2_done", b, 12))
                r = slice(64 * (h % 2), 64 * (h % 2) + 64)
                for qt in range(NT):
                    pe.wait_ge(*bank_read(b, "s", 3 * h + qt))
                    nc.tensor.matmul(bank("s", 3 * h + qt)[0:TP, 0:T], QK[r, h // 2, TP * qt:TP * qt + TP],
                                     QK[r, 6 + h // 2, :], start=True, stop=True).then_inc(S["s_full"], 1)

            def mt(b, g):
                pe.wait_ge(S["s_max"], due("s_max", b, 12 * g + 12))
                pe.wait_ge(*bank_read(b, "mt", g))
                for qt in range(NT):
                    last = nc.tensor.transpose(bank("mt", g)[0:4, TP * qt:TP * qt + TP], mx[:, qt, 4 * g:4 * g + 4],
                                               ident[0:TP, 0:TP])
                last.then_inc(S["mt_full"], 1)

            def st(b, h):
                if h % 4 == 0:
                    pe.wait_ge(S["mt_done"], due("mt_done", b, h // 4 + 1))
                r = slice(64 * (h % 2), 64 * (h % 2) + 64)
                for kt in range(3):
                    n = 3 * h + kt
                    pe.wait_ge(*bank_read(b, "st", n))
                    ps = bank("st", n)[0:TP, 0:T]
                    nc.tensor.matmul(ps, QK[r, 6 + h // 2, TP * kt:TP * kt + TP], QK[r, h // 2, :],
                                     start=True, stop=False)
                    nc.tensor.matmul(ps, identb[:, h % 4:h % 4 + 1].to_broadcast([4, TP]), nmT[:, :],
                                     start=False, stop=True).then_inc(S["st_full"], 1)

            def pv(b, h):
                j, g = h % 4, h // 4
                if h == 0:
                    pe.wait_ge(S["v2_lo"], due("v2_lo", b, 3))
                if j == 0:
                    pe.wait_ge(*bank_read(b, "pv", g))
                pe.wait_ge(S["pt_lo"], due("pt_lo", b, 2 * h + 2))
                pe.wait_ge(S["pt_lo2"], due("pt_lo2", b, h + 1))
                ps = bank("pv", g)[32 * j:32 * j + 32, 0:T]
                for kt in range(3):
                    for p_, v_ in ((0, 0), (0, 1), (1, 0)):
                        last = nc.tensor.matmul(ps, Vp[:, v_, kt, h, :], PT[:, h % 2, p_, kt, :],
                                                start=(kt == 0 and (p_, v_) == (0, 0)),
                                                stop=(kt == 2 and (p_, v_) == (1, 0)))
                last.then_inc(S["pv_done"], 1)

            def pj(b):
                pe.wait_ge(S["o_lo"], due("o_lo", b, 3))
                for t in range(NT):
                    c = slice(TP * t, TP * t + TP)
                    pe.wait_ge(*bank_read(b, "pj", t))
                    five(bank("pj", t)[0:TP, 0:D],
                         [(Os[:, s_, g, c], projW[:, w_, g, :]) for g in range(3) for s_, w_ in ((0, 0), (0, 1), (1, 0))]
                         ).then_inc(S["pj_full"], 1)

            def gate(b):
                pe.wait_ge(S["tr_lo"], due("tr_lo", b, 6))
                pe.wait_ge(*bank_read(b, "gate", 0))
                for t in range(NT):
                    last = five(bank("gate", 0)[0:TP, E * t:E * t + E],
                                by_token(gateWa, gateWb, lambda w, s: w[:, s, :], XM, t))
                last.then_inc(S["gate_full"], 1)

            def gt(b):
                pe.wait_ge(S["g_ready"], due("g_ready", b, 1))
                pe.wait_ge(*bank_read(b, "gt", 0))
                for t in range(NT):
                    last = nc.tensor.transpose(bank("gt", 0)[0:E, TP * t:TP * t + TP], G[:, t, :], ident[0:TP, 0:TP])
                last.then_inc(S["gt_full"], 1)

            def b2_step(b):
                pe.wait_ge(S["gt_done"], due("gt_done", b, 1))
                for t in range(NT):
                    pe.wait_ge(*bank_read(b, "b2", t))
                    nc.tensor.matmul(bank("b2", t)[0:TP, 0:D], GT[:, TP * t:TP * t + TP], b2s[:, :],
                                     start=True, stop=True).then_inc(S["b2_full"], 1)

            def w1_chunk(m, e, c):
                n = NC * e + c
                if n == 0:
                    pe.wait_ge(S["tr_lo"], due("tr_lo", m, 6))
                pe.wait_ge(S["gelu"], due("gelu", m, n - 1))
                cols = slice(128 * c, 128 * c + 128)
                five(M[n % 2][:, 0:T], by_weight(W1a[:, e], W1b[:, e], lambda w, s: w[:, s, cols], XM)
                     ).then_inc(S["w1_full"], 1)

            def w2_tile(m, e, t):
                if t == 0:
                    pe.wait_ge(S["h_lo"], due("h_lo", m, dve_low(NC * (e + 1))))
                    pe.wait_ge(S["h_lo2"], due("h_lo2", m, NC // 3 * (e + 1)))
                if t != 1:
                    pe.wait_ge(S["acc"], due("acc", m, 3 * (e - 1) + (2 if t == 0 else 3)))
                ps = O[0][0:TP, D * t:D * t + D] if t < 2 else O[1][0:TP, 0:D]
                rows = slice(TP * t, TP * t + TP)
                five(ps, [(Hs[:, e % 2, s_, c, rows], W2s[:, e, c, w_, :])
                          for c in range(NC) for s_, w_ in ((0, 0), (0, 1), (1, 0))]).then_inc(S["o_full"], 1)

            def turn(b, m, ahead=True):
                for step in order(m is not None, b is not None, ahead):
                    kind = step[0]
                    if kind == "W1":
                        w1_chunk(m, step[1], step[2])
                    elif kind == "W2":
                        w2_tile(m, step[1], step[2])
                    elif kind == "emb":
                        emb(b)
                    elif kind == "tr":
                        tr(b, step[1])
                    elif kind == "qk1":
                        qk1(b, step[1])
                    elif kind == "v1":
                        v1(b)
                    elif kind == "s1":
                        s1(b)
                    elif kind == "p1t":
                        p1t(b)
                    elif kind == "pv1":
                        pv1(b)
                    elif kind == "qk2":
                        qk2(b, step[1])
                    elif kind == "v2":
                        v2(b)
                    elif kind == "s":
                        s(b, step[1])
                    elif kind == "mt":
                        mt(b, step[1])
                    elif kind == "att2":
                        st(b, step[1])
                    elif kind == "pv":
                        pv(b, step[1])
                    elif kind == "pj":
                        pj(b)
                    elif kind == "gate":
                        gate(b)
                    elif kind == "gt":
                        gt(b)
                    elif kind == "b2":
                        b2_step(b)

            turn(0, None)
            with pe.Fori(1, B - 1) as b:
                turn(b, b - 1)
            turn(B - 1, B - 2, False)
            turn(None, B - 1)


_INS = ["x", "txt", "L0_tok_W", "L0_tok_b", "L0_attn_Wq", "L0_attn_Wk", "L0_attn_Wv", "L0_ffn_norm1_w",
        "L0_ffn_norm1_b", "L0_ffn_qkv_w", "L0_ffn_qkv_b", "L0_ffn_proj_w", "L0_ffn_proj_b", "L0_ffn_norm2_w",
        "L0_ffn_norm2_b", "L0_ffn_w_gate", "L0_ffn_W1", "L0_ffn_b1", "L0_ffn_W2", "L0_ffn_b2"]


def shape_constants():
    import numpy as np
    c = np.zeros((128, C_N), np.float32)
    p = np.arange(128)
    c[:, C_ID:C_ID + 128] = np.eye(128, dtype=np.float32)
    c[:, C_M64] = p >= 64
    c[:, C_MQ] = p % 64 >= 32
    c[:, C_MK] = p % 32 >= 16
    c[:, C_M48] = p >= IMROWS
    j = np.arange(RH, dtype=np.float32)
    theta = np.power(np.float32(10000.0), np.float32(-2.0) * j / np.float32(D), dtype=np.float32)
    ang = np.arange(T, dtype=np.float32)[None, :] * theta[:, None]
    c[0:RH, C_COS:C_COS + T] = np.cos(ang)
    c[0:RH, C_SIN:C_SIN + T] = np.sin(ang)
    q, k = np.arange(TP)[:, None], np.arange(TP)[None, :]
    c[0:TP, C_CAP:C_CAP + TP] = np.where(k <= q, 3.0e38, -3.0e38)
    c[:, C_EPS:C_N] = EPS
    c[:, C_POW:C_EPS] = -0.5
    c[:, C_REV:C_POW] = np.tile(np.arange(E, 0, -1, dtype=np.float32), NT)[None, :]
    return c


def kernel(**inputs):
    import numpy as np
    import concourse.bacc as bacc
    from concourse.bass_utils import run_bass_kernel_spmd as run

    nc = bacc.Bacc("TRN2", target_bir_lowering=False, num_devices=1)
    nc.disable_value_cache = True
    arrays, args = {}, []
    for name in _INS:
        a = np.ascontiguousarray(inputs[name])
        arrays[f"in_{name}"] = a
        args.append(nc.dram_tensor(f"in_{name}", a.shape, mybir.dt.from_np(a.dtype), kind="ExternalInput").ap())
    arrays["in_const"] = shape_constants()
    args.append(nc.dram_tensor("in_const", (128, C_N), F32, kind="ExternalInput").ap())
    out = nc.dram_tensor("out", (B, T, D), F32, kind="ExternalOutput").ap()
    build_program(nc, *args, out)
    return run(nc, [arrays], core_ids=[0]).results[0]["out"]
```

```python
from contextlib import ExitStack

import concourse.bass as bass
from concourse import mybir

ALU = mybir.AluOpType
ACT = mybir.ActivationFunctionType
F32 = mybir.dt.float32
F16 = mybir.dt.float16
AX = mybir.AxisListType

B, CH, IMG, PATCH = 32, 3, 224, 16
D, HID, E, HEADS = 192, 768, 8, 12
HD = D // HEADS
GRID = IMG // PATCH
NPATCH = GRID * GRID
NTEXT = 128
T = NPATCH + NTEXT
TP = 108
NT = T // TP
PT1 = NPATCH - TP
KA, KB = 128, D - 128
RH = D // 2
NC = HID // 128
IMROWS = CH * PATCH
CHUNKS = 7
CW = GRID * IMG // CHUNKS
BIG = 32768.0
WSC = 64.0
EPS = 1e-5
SCALE1 = float(D) ** -0.5
SCALE2 = float(HD) ** -0.5

C_ID, C_M64, C_MQ, C_MK = 0, 128, 129, 130
C_COS, C_SIN = 131, 131 + T
C_CAP = C_SIN + T
C_REV = C_CAP + TP
C_POW = C_REV + NT * E
C_EPS = C_POW + NT
C_BIG = C_EPS + NT
C_N = C_BIG + 1

XIN = 96
DVE_STEPS = 37
SP_SIGNALS = dict(nm_in=96, xin0=4 * XIN, xin1=3 * XIN, txt_in=32, out_done=16)
PE_SIGNALS = dict(emb_full=2, tr_full=6, qk1_full=4, v1_full=3, s1_full=3, p1t_full=3, pv1_full=3, qk2_full=12,
                  v2_full=3, s_full=36, mt_full=3, st_full=36, pv_done=12, pj_full=3, gate_full=1, gt_full=1,
                  b2_full=3, w1_full=48, o_full=24)
ACT_SIGNALS = dict(img_hi=7, tr_hi=6, rope_hi=4, v1_hi=3, p1_ready=3, p1t_hi=3, qk2_m=12, v2_hi=3, st_exp=36, pt_hi2=12, o_hi=3,
                   gate_tanh=1, gelu=48, h_hi=48)
DVE_SIGNALS = dict(emb_evac=2, n_ready=3, tr_lo=6, rope_re=2, rope_mul=2, v1_lo=3, s1_evac=3, m1_ready=1,
                   p1t_lo=3, pv1_evac=3, xf_ready=1, qk2_done=12, v2_lo=3, s_max=36, mt_done=3, pt_hi=24, pt_lo=24, sum_out=3, sum_inv=3,
                   pv_norm=3, o_lo=3, x1_done=3, gate_evac=1, gate_tanh_in=1, g_ready=1, gt_done=1, r_ready=3, h_lo=32, acc=24,
                   ln_var=4, dve_step=DVE_STEPS)
POOL_SIGNALS = dict(img_split=7, h_lo2=16, rope_sum=4, rope_lo=4, xfb_ready=1, pt_lo2=12, r_sum=1, ln_eps=4, ln_rstd=4)
PER = SP_SIGNALS | PE_SIGNALS | ACT_SIGNALS | DVE_SIGNALS | POOL_SIGNALS

SCHEDULE = [
    "W1", "W1", ("emb", 0), "W1", "W1", "W1", ("ln", 0), "W1", ("tr", 0), "W1", "W1", ("qk1", 0), "W1",
    ("qk1", 1), "W1", "W1", "W2", "W1", ("img", 0), ("s1", 0), "W2", ("v1", 0), ("p1t", 0), "W2", ("pv1", 0),
    "W1", "W1", "W2", ("img", 1), "W1", "W1", ("ln", 1), "W1", ("ln", 2), "W2", ("img", 2), "W1", "W2", ("tr", 1),
    "W1", "W1", ("qk2", 0), ("qk2", 1), ("img", 3), "W1", ("img", 4), ("qk2", 2), "W1", ("qk2", 3), "W2", "W1",
    "W2", ("qk2", 4), "W1", ("qk2", 5), "W2", ("s", 0), ("img", 5), "W1", ("img", 6), ("s", 1), ("v2", 0), "W1",
    ("s", 2), "W1", "W1", ("s", 3), "W1", ("mt", 0), "W1", "W2", ("att2", 0), "W2", ("att2", 1), ("pv", 0),
    ("att2", 2), ("att2", 3), "W2", ("pv", 1), ("s", 4), ("pv", 2), "W1", ("pv", 3), ("norm", 0), ("scale", 0),
    "W1", ("s", 5), "W1", ("s", 6), "W1", ("s", 7), "W1", ("osplit", 0), ("mt", 1), "W1", "W2", "W2", ("att2", 4),
    "W2", ("att2", 5), ("att2", 6), ("pv", 4), ("pv", 5), ("att2", 7), "W1", ("pv", 6), ("s", 8), ("pv", 7),
    ("norm", 1), ("scale", 1), "W2", "W1", ("s", 9), "W1", ("osplit", 1), "W1", ("s", 10), ("s", 11), ("mt", 2),
    "W1", "W2", ("att2", 8), "W2", ("att2", 9), ("att2", 10), ("pv", 8), ("att2", 11), ("pv", 9), "W1",
    ("pv", 10), ("pv", 11), ("norm", 2), "W1", "W1", ("scale", 2), "W1", "W2", ("osplit", 2), ("pj", 0), "W1",
    "W1", ("ln", 3), "W1", "W2", "W2", ("tr", 2), ("gate", 0), "W2", "W2", "W2", ("gt", 0), ("b2", 0),
]
LOADS = 4 * E


def order(experts, attention, image=True):
    out, units, chunks, tiles = [], 0, 0, 0
    for step in SCHEDULE:
        if step == "W1":
            if experts:
                out.append(("W1", chunks // NC, chunks % NC))
            chunks += 1
        elif step == "W2":
            if experts:
                out.append(("W2", tiles // NT, tiles % NT))
            tiles += 1
        elif attention and (image or step[0] != "img"):
            out.append(step)
        if isinstance(step, str):
            if not experts and units % 2 == 0 and units // 2 < LOADS:
                out.append(("stage", units // 2))
            units += 1
    assert (chunks, tiles) == (E * NC, E * NT)
    return out


USES = []


def plan_uses():
    turn, held = 0, None

    def use(step, i, sem, k):
        nonlocal turn
        if turn == held:
            turn = (turn + 1) % 4
        USES.append(((step, i), turn, sem, k))
        turn = (turn + 1) % 4

    plain = {"v1": (3, "v1_lo"), "s1": (3, "s1_evac"), "p1t": (3, "p1t_lo"), "pv1": (3, "pv1_evac"),
             "v2": (3, "v2_lo"), "emb": (2, "emb_evac"), "tr": (2, "tr_lo"), "qk2": (2, "qk2_done"),
             "s": (3, "s_max"), "mt": (1, "mt_done"), "pj": (3, "x1_done"), "gate": (1, "gate_evac"),
             "gt": (1, "gt_done"), "b2": (3, "r_ready")}
    for step in SCHEDULE:
        if isinstance(step, str):
            continue
        kind, at = step
        if kind in plain:
            n, sem = plain[kind]
            for i in range(n * at, n * at + n):
                use(kind, i, sem, i + 1)
        elif kind == "qk1":
            use("qk1", 2 * at, "rope_re", at + 1)
            use("qk1", 2 * at + 1, "rope_mul", at + 1)
        elif kind == "att2":
            use("st", 3 * at, "st_exp", 3 * at + 1)
            use("st", 3 * at + 1, "st_exp", 3 * at + 2)
            use("st", 3 * at + 2, "pt_hi2", at + 1)
        elif kind == "pv" and at % 4 == 0:
            use("pv", at // 4, "pv_norm", at // 4 + 1)
            held = USES[-1][1]
        elif kind == "scale":
            held = None


plan_uses()
BANK = {key: bank for key, bank, _, _ in USES}
LAST = {bank: (sem, k) for _, bank, sem, k in USES}
BEFORE = {}
_seen = {}
for _key, _bank, _sem, _k in USES:
    BEFORE[_key] = _seen.get(_bank)
    _seen[_bank] = (_sem, _k)


class Batch:

    def __init__(self, loop, plus=0):
        self.loop, self.plus = loop, plus

    def __add__(self, n):
        return Batch(self.loop, self.plus + n)

    def __sub__(self, n):
        return Batch(self.loop, self.plus - n)


def build_program(nc, x, txt, tok_w, tok_b, wq, wk, wv, n1w, n1b, qkv_w, qkv_b, proj_w, proj_b, n2w, n2b,
                  w_gate, w1, b1, w2, b2, const, out):
    with ExitStack() as ctx:
        def sb(name, shape, dt):
            return ctx.enter_context(nc.sbuf_tensor(name, shape, dt))

        def sem(name):
            return ctx.enter_context(nc.semaphore(name))

        W1a = sb("W1a", [128, E, 2, HID], F16)
        W1b = sb("W1b", [128, E, 2, HID], F16)
        W2s = sb("W2s", [128, E, NC, 2, D], F16)
        tokW = sb("tokW", [128, 2, PATCH // 2, D], F16)
        attWa = sb("attWa", [128, 2, 3 * D], F16)
        attWb = sb("attWb", [128, 2, 3 * D], F16)
        qkvWa = sb("qkvWa", [128, 2, 12 * 128 + D], F16)
        qkvWb = sb("qkvWb", [128, 2, 12 * 128 + D], F16)
        projW = sb("projW", [128, 2, 3, D], F16)
        gateWa = sb("gateWa", [128, 2, E], F16)
        gateWb = sb("gateWb", [128, 2, E], F16)
        b2s = sb("b2s", [E, D], F32)
        b1s = sb("b1s", [128, E, NC], F32)
        tokb = sb("tokb", [TP, D], F32)
        projb = sb("projb", [TP, D], F32)
        norms = sb("norms", [TP, 4, D], F32)
        qkb = sb("qkb", [128, 12], F32)
        qkmb = sb("qkmb", [128, 12], F32)
        vb = sb("vb", [128, 3], F32)
        cst = sb("cst", [128, C_N], F32)
        ident = cst[:, C_ID:C_ID + 128]
        m64, mq, mk = (cst[:, c:c + 1] for c in (C_M64, C_MQ, C_MK))
        cos, sin = cst[0:RH, C_COS:C_COS + T], cst[0:RH, C_SIN:C_SIN + T]
        cap = cst[0:TP, C_CAP:C_CAP + TP]
        rev = cst[0:TP, C_REV:C_REV + NT * E].rearrange("p (t e) -> p t e", t=NT)

        ximg = sb("ximg", [128, 2, CW], F32)
        XS = sb("XS", [128, 2, CHUNKS * CW // 2], F16)
        Hres = sb("Hres", [TP, NT, D], F32)
        Nrm = sb("Nrm", [TP, NT, D], F32)
        XF = sb("XF", [TP, NT, D], F32)
        R = sb("R", [TP, NT, D], F32)
        ACC = sb("ACC", [TP, NT, D], F32)
        XT = sb("XT", [128, 3, T], F16)
        XM = sb("XM", [128, 3, T], F16)
        QK = sb("QK", [128, 12, T], F16)
        QK1 = QK[0:RH, 0:8, :].rearrange("p (i s) t -> p i s t", s=2)
        V1 = sb("V1", [TP, 2, NT, D], F16)
        WS = sb("WS", [128, 6 * T + 9 * T], F32)
        tmp = WS[0:RH, 0:8 * T].rearrange("p (i t) -> p i t", t=T)
        S1 = WS[0:TP, 0:3 * T].rearrange("p (i t) -> p i t", t=T)
        Pr = WS[0:TP, 0:6 * T].rearrange("p (i t) -> p i t", t=T)
        PT = WS[0:TP, 6 * T:15 * T].bitcast(F16).rearrange("p (a s k t) -> p a s k t", a=3, s=2, k=3)
        one = sb("one", [1, 8], F32)
        qm = sb("qm", [128, 2, T], F16)
        trm = qm[:, 0, :]
        Vp = sb("Vp", [TP, 2, NT, HEADS, 32], F16)
        mx = sb("mx", [TP, NT, HEADS], F32)
        nmT = sb("nmT", [4, T], F16)
        rsq = sb("rsq", [128, T], F32)
        rsi = sb("rsi", [128, T], F32)
        Os = sb("Os", [128, 2, 3, T], F16)
        st6 = sb("st6", [TP, NT, 6], F32)
        mv = sb("mv", [TP, NT, 2], F32)
        rstd = sb("rstd", [TP, NT], F32)
        veps = sb("veps", [TP, NT], F32)
        nm1 = sb("nm1", [TP, 4, NT], F32)
        rt = sb("rt", [TP, 8, NT, E], F32)
        rs = sb("rs", [TP, 8, NT], F32)
        G = sb("G", [TP, NT, E], F32)
        Gs = sb("Gs", [TP, NT, E], F32)
        GT = rsi[0:E, :]

        h32 = sb("h32", [128, 3, T], F32)
        Hs = sb("Hs", [128, 2, 2, NC, T], F16)

        M = [ctx.enter_context(nc.psum_tensor(f"M{i}", [128, 512], F32)) for i in range(2)]
        O = [ctx.enter_context(nc.psum_tensor(f"O{i}", [128, 512], F32)) for i in range(2)]
        TB = [ctx.enter_context(nc.psum_tensor(f"TB{i}", [128, 512], F32)) for i in range(4)]

        S = {name: sem(name) for name in PER}
        c_in, c_set = sem("c_in"), sem("c_set")
        stg_in = [sem(f"stg_in{i}") for i in range(4)]
        stg_hi, stg_lo = sem("stg_hi"), sem("stg_lo")
        big_in, prep_full, prep_hi, prep_lo = sem("big_in"), sem("prep_full"), sem("prep_hi"), sem("prep_lo")
        passed = sem("passed")
        pad_set, tok_dup, bias_set = sem("pad_set"), sem("tok_dup"), sem("bias_set")

        def due(name, b, k):
            if isinstance(b, Batch):
                return b.loop * PER[name] + ((b.plus + 1) * PER[name] + k)
            return (b + 1) * PER[name] + k

        def number(b):
            return b.loop + b.plus if isinstance(b, Batch) else b

        def one_ahead(eng, signals):
            for name, count in signals.items():
                eng.sem_inc(S[name], count)

        def dve_low(n):
            return 2 * (n // 3) + n % 3

        def apart(eng):
            eng.sem_inc(passed, 1)

        def bank_read(b, step, i):
            before = BEFORE[(step, i)]
            if before:
                return S[before[0]], due(before[0], b, before[1])
            last, k = LAST[BANK[(step, i)]]
            return S[last], due(last, b - 1, k)

        def bank(step, i):
            return TB[BANK[(step, i)]]

        big = Hs[:, :, :, :, :].rearrange("p a s c t -> p (a s c t)").bitcast(F32)
        tokS = big[0:96, 0:2 * 768].rearrange("p (a n) -> p a n", a=2)
        qkvS = big[0:96, 1536:1536 + 6 * D].rearrange("p (a n) -> p a n", a=6)
        projS = big[0:96, 2688:2688 + 768].rearrange("p (a g n) -> p a g n", a=2, g=3)
        tokD = XS[:, :, :].rearrange("p s n -> p (s n)").bitcast(F32)[0:96, 0:768].rearrange(
            "p (s n m) -> p s n m", s=2, n=4)
        slot = [WS[:, 768 * i:768 * (i + 1)] for i in range(4)] + [big[:, 768 * i:768 * (i + 1)] for i in range(4)]
        stages = []

        for name, w, c0 in (("q", wq, 0), ("k", wk, D)):
            for half in range(2):
                for dst, rows in ((attWa, None), (attWb, 64)):
                    stages.append((w, rows, D, dst, c0 + half * RH, half, 1.0))
        for dst, rows in ((attWa, None), (attWb, 64)):
            stages.append((wv, rows, D, dst, 2 * D, None, 1.0))
        for dst, rows in ((gateWa, None), (gateWb, 64)):
            stages.append((w_gate, rows, E, dst, 0, None, WSC))
        EARLY = len(stages)
        for e in range(E):
            stages.append((w1[e], None, HID, W1a[:, e], 0, None, WSC))
            stages.append((w1[e], 64, HID, W1b[:, e], 0, None, WSC))
            for c in range(0, NC, 3):
                stages.append((w2[e], ("w2", c), 3 * D, W2s[:, e, c:c + 3], 0, "w2", WSC))

        def stage_slot(i):
            return slot[i % 4 + (4 if i >= EARLY else 0)]

        def stage_views(i):
            src, rows, cols, dst, c0, pick, scale = stages[i]
            s = stage_slot(i)
            if pick == "w2":
                v = s[:, 0:cols].rearrange("p (c n) -> p c n", c=3)
                return v, dst[:, :, 0, :], dst[:, :, 1, :], scale
            if pick is None:
                return s[:, 0:cols], dst[:, 0, c0:c0 + cols], dst[:, 1, c0:c0 + cols], scale
            v = s[:, 0:cols].rearrange("p (j r) -> p j r", r=2)[:, :, pick]
            return v, dst[:, 0, c0:c0 + RH], dst[:, 1, c0:c0 + RH], scale

        preps = []
        for pw in range(0, PATCH // 2, 2):
            preps.append(("tok", pw, 96, 2 * D, tokW[0:96, 0, pw:pw + 2, :], tokW[0:96, 1, pw:pw + 2, :], WSC))
        def four(w, sel, i):
            return w[:, sel, 768 * i:768 * i + 768].rearrange("p (h a d) -> p h a d", h=HEADS, a=4)[:, :, 0:3, :]

        for part, dst in (("a", qkvWa), ("b", qkvWb)):
            for i in range(2):
                preps.append(("qkv" + part, i, 128, D, four(dst, 0, i), four(dst, 1, i), 1.0))
            preps.append(("qkv" + part, 2, 128, D, dst[:, 0, 1536:], dst[:, 1, 1536:], 1.0))
        for half in range(2):
            cols = slice(96 * half, 96 * half + 96)
            preps.append(("proj", half, 128, 288, projW[:, 0, :, cols], projW[:, 1, :, cols], WSC))

        def prep_view(i):
            kind, at, rows, cols, hi, lo, scale = preps[i]
            v = TB[i % 3][0:rows, 0:cols]
            if kind == "tok":
                v = v.rearrange("p (w n) -> p w n", w=2)
            if kind == "proj":
                v = v.rearrange("p (g n) -> p g n", g=3)
            if kind[:3] == "qkv" and at < 2:
                v = v.rearrange("p (h a d) -> p h a d", h=HEADS, a=1).to_broadcast([128, HEADS, 3, HD])
            return v, hi, lo, scale

        N_C = [0]
        block = ctx.enter_context(nc.Block())

        @block.sync
        def _(sp):
            def const_in(dst, src):
                sp.dma_start(dst, src, allow_slow_non_contiguous=True).then_inc(c_in, 16)
                N_C[0] += 16

            const_in(cst[:, :], const)
            sp.wait_ge(pad_set, 3)
            sp.dma_start(tokS, tok_w.rearrange("(a p) n -> p a n", p=96)).then_inc(big_in, 16)
            sp.dma_start(qkvS, qkv_w.rearrange("(a p) n -> p a n", p=96)).then_inc(big_in, 16)
            for a in range(2):
                for g in range(3):
                    sp.dma_start(projS[:, a, g, :].rearrange("p (j r) -> p j r", r=32)[:, :, 0:HD],
                                 proj_w[96 * a:96 * a + 96, 64 * g:64 * g + 64].rearrange("p (j r) -> p j r", r=HD)
                                 ).then_inc(big_in, 16)
            const_in(tokb[:, :], tok_b.rearrange("(a n) -> a n", a=1).to_broadcast([TP, D]))
            const_in(projb[:, :], proj_b.rearrange("(a n) -> a n", a=1).to_broadcast([TP, D]))
            for i, v in enumerate((n1w, n1b, n2w, n2b)):
                const_in(norms[:, i, :], v.rearrange("(a n) -> a n", a=1).to_broadcast([TP, D]))
            for hh in range(2):
                for c in range(3):
                    const_in(qkb[64 * hh + 16 * c:64 * hh + 16 * c + 16, :],
                             qkv_b[0:2 * D].rearrange("(i h d) -> h d i", h=2, d=HD)[hh])
            for j in range(4):
                const_in(vb[32 * j:32 * j + HD, :], qkv_b[2 * D:3 * D].rearrange("(g j d) -> j d g", j=4, d=HD)[j])
            const_in(b2s[:, :], b2)
            for e in range(E):
                const_in(b1s[:, e, :], b1[e].rearrange("(c p) -> p c", p=128))
            def stage(i):
                src, rows, cols, dst, c0, pick, scale = stages[i]
                if i >= 4:
                    sp.wait_ge(stg_lo, i - 3)
                if i == EARLY:
                    sp.wait_ge(prep_full, len(preps))
                s = stage_slot(i)
                if pick == "w2":
                    c = rows[1]
                    sp.dma_start(s[:, 0:cols].rearrange("p (c n) -> p c n", c=3),
                                 src[128 * c:128 * (c + 3), :].rearrange("(c p) n -> p c n", p=128)
                                 ).then_inc(stg_in[i % 4], 32)
                elif rows is None:
                    sp.dma_start(s[:, 0:cols], src[0:128, :]).then_inc(stg_in[i % 4], 32)
                else:
                    for r in range(2):
                        sp.dma_start(s[64 * r:64 * r + 64, 0:cols], src[128:D, :]).then_inc(stg_in[i % 4], 16)

            def image(b, k):
                name = f"xin{k % 2}"
                sp.wait_ge(S["img_split"], due("img_split", b, k - 1 if k >= 2 else 0))
                rows = x[number(b)].rearrange("c (h r) w -> c r h w", r=PATCH)
                for odd in range(2):
                    for c in range(CH):
                        p = IMROWS * odd + PATCH * c
                        sp.dma_start(ximg[p:p + PATCH, k % 2, :].rearrange("r (h w) -> r h w", h=2)[:, :, 0:IMG - odd],
                                     rows[c, :, 2 * k:2 * k + 2, odd:IMG]).then_inc(S[name], 16)

            def text(b):
                sp.wait_ge(S["r_sum"], due("r_sum", b - 1, 1))
                sp.dma_start(Hres[PT1:TP, 1, :], txt[number(b), 0:TP - PT1, :]).then_inc(S["txt_in"], 16)
                sp.dma_start(Hres[:, 2, :], txt[number(b), TP - PT1:NTEXT, :]).then_inc(S["txt_in"], 16)

            def maxima(b, g):
                sp.wait_ge(S["mt_done"], due("mt_done", b, g + 1))
                for odd in range(2):
                    sp.dma_start(QK[64 * odd + 3 * HD:64 * odd + 3 * HD + 1, 2 * g:2 * g + 2, :],
                                 nmT[2 * odd:2 * odd + 2, :]).then_inc(S["nm_in"], 16)

            def store(m):
                sp.wait_ge(S["acc"], due("acc", m, 24))
                sp.dma_start(out[number(m)].rearrange("(t p) d -> p t d", p=TP), ACC[:, :, :]).then_inc(S["out_done"], 16)

            def turn(b, m, ahead=True):
                text(b)
                if ahead:
                    for k in range(CHUNKS):
                        image(b + 1, k)
                for g in range(HEADS // 4):
                    maxima(b, g)
                if m is not None:
                    store(m)

            one_ahead(sp, SP_SIGNALS)
            image(0, 0)
            image(0, 1)
            for i in range(EARLY):
                stage(i)
            text(0)
            for k in range(2, CHUNKS):
                image(0, k)
            for step in order(False, True):
                if step[0] == "stage":
                    stage(EARLY + step[1])
                elif step[0] == "img":
                    image(1, step[1])
                elif step[0] == "mt":
                    maxima(0, step[1])
            with sp.Fori(1, B - 1) as b:
                turn(Batch(b), Batch(b) - 1)
            turn(B - 1, B - 2, False)
            store(B - 1)
            sp.wait_ge(S["out_done"], due("out_done", B - 1, 16))

        @block.gpsimd
        def _(pool):
            nc.gpsimd.memset(big[0:96, 2688:3456], 0.0).then_inc(pad_set, 1)
            nc.gpsimd.memset(vb[:, :], 0.0).then_inc(pad_set, 1)
            nc.gpsimd.memset(qkb[:, :], 0.0).then_inc(pad_set, 1)
            for w in (qkvWa, qkvWb):
                for part in range(2):
                    zeros = w[:, part, 0:1536].rearrange("p (h a d) -> p h a d", a=4, d=HD)[:, :, 3, :]
                    nc.gpsimd.memset(zeros, 0.0).then_inc(pad_set, 1)
            nc.gpsimd.memset(Vp[:, 0, :, :, :], 1.0).then_inc(pad_set, 1)
            nc.gpsimd.memset(Vp[:, 1, :, :, :], 0.0).then_inc(pad_set, 1)
            one_ahead(pool, POOL_SIGNALS)
            pool.wait_ge(big_in, 128)
            for i in range(PATCH // 4):
                if i >= 2:
                    pool.wait_ge(prep_full, i - 1)
                for w in range(2):
                    for a in range(2):
                        src = tokS[:, a, :].rearrange("p (r w c) -> p w c r", r=PATCH, w=PATCH)
                        for odd in range(2):
                            last = nc.gpsimd.tensor_copy(
                                tokD[:, i % 2, 2 * w + a, IMROWS * odd:IMROWS * (odd + 1)].rearrange(
                                    "p (c r) -> p c r", c=CH), src[:, 4 * i + 2 * w + odd])
                last.then_inc(tok_dup, 1)

            def qk1(b, i):
                pool.wait_ge(S["rope_mul"], due("rope_mul", b, i + 1))
                t0, t1, t2, t3 = (tmp[:, 4 * i + j, :] for j in range(4))
                nc.gpsimd.tensor_tensor(t0, t0, t2, ALU.subtract).then_inc(S["rope_sum"], 1)
                nc.gpsimd.tensor_tensor(t1, t1, t3, ALU.add).then_inc(S["rope_sum"], 1)
                for j, t in enumerate((t0, t1)):
                    pool.wait_ge(S["rope_hi"], due("rope_hi", b, 2 * i + j + 1))
                    nc.gpsimd.tensor_tensor(QK1[:, 2 * i + j, 1, :], t, QK1[:, 2 * i + j, 0, :],
                                            ALU.subtract).then_inc(S["rope_lo"], 1)

            def img(b, k):
                if k == 0:
                    pool.wait_ge(S["emb_full"], due("emb_full", b - 1, 2))
                pool.wait_ge(S["img_hi"], due("img_hi", b, k + 1))
                cols = slice(CW // 2 * k, CW // 2 * (k + 1))
                nc.gpsimd.tensor_tensor(XS[0:96, 1, cols], ximg[0:96, k % 2, 0:CW:2], XS[0:96, 0, cols],
                                        ALU.subtract).then_inc(S["img_split"], 1)

            def h_low(m, n):
                e, c = n // NC, n % NC
                pool.wait_ge(S["h_hi"], due("h_hi", m, n + 1))
                nc.gpsimd.tensor_tensor(Hs[:, e % 2, 1, c, :], h32[:, n % 3, :], Hs[:, e % 2, 0, c, :],
                                        ALU.subtract).then_inc(S["h_lo2"], 1)

            def inv_std(b, i):
                pool.wait_ge(S["ln_var"], due("ln_var", b, i + 1))
                nc.gpsimd.tensor_tensor(veps[:, :], mv[:, :, 1], cst[0:TP, C_EPS:C_EPS + NT],
                                        ALU.add).then_inc(S["ln_eps"], 1)
                pool.wait_ge(S["ln_eps"], due("ln_eps", b, i + 1))
                nc.gpsimd.tensor_tensor(rstd[:, :], veps[:, :], cst[0:TP, C_POW:C_POW + NT],
                                        ALU.pow).then_inc(S["ln_rstd"], 1)

            def pv1(b):
                inv_std(b, 1)
                pool.wait_ge(S["xf_ready"], due("xf_ready", b, 1))
                nc.gpsimd.tensor_tensor(R[:, :, :], XF[:, :, :],
                                        projb[:, :].rearrange("p (a n) -> p a n", a=1).to_broadcast([TP, NT, D]),
                                        ALU.add).then_inc(S["xfb_ready"], 1)
                inv_std(b, 2)

            def att2(b, h):
                pool.wait_ge(S["pt_hi2"], due("pt_hi2", b, h + 1))
                nc.gpsimd.tensor_tensor(PT[:, h % 3, 1, 2, :], Pr[:, (3 * h + 2) % 6, :], PT[:, h % 3, 0, 2, :],
                                        ALU.subtract).then_inc(S["pt_lo2"], 1)

            def pj(b):
                inv_std(b, 3)
                pool.wait_ge(S["x1_done"], due("x1_done", b, 3))
                nc.gpsimd.tensor_tensor(R[:, :, :], Hres[:, :, :], XF[:, :, :], ALU.add).then_inc(S["r_sum"], 1)

            def turn(b, m, ahead=True):
                chunk = None
                for step in order(m is not None, b is not None, ahead):
                    if step[0] in ("W1", "W2"):
                        if chunk is not None and chunk % 3 == 2:
                            h_low(m, chunk)
                        chunk = NC * step[1] + step[2] if step[0] == "W1" else None
                    elif step[0] == "img":
                        img(b + 1, step[1])
                    elif step[0] == "emb":
                        inv_std(b, 0)
                    elif step[0] == "qk1":
                        qk1(b, step[1])
                    elif step[0] == "pv1":
                        pv1(b)
                    elif step[0] == "att2":
                        att2(b, step[1])
                    elif step[0] == "pj":
                        pj(b)

            for k in range(CHUNKS):
                img(0, k)
            turn(0, None)
            with pool.Fori(1, B - 1) as b:
                turn(Batch(b), Batch(b) - 1)
            turn(B - 1, B - 2, False)
            turn(None, B - 1)

        @block.scalar
        def _(act):
            one_ahead(act, ACT_SIGNALS)
            act.wait_ge(c_in, 16)

            def load_table(func, i):
                nc.scalar.activation(one[:, i:i + 1], cst[0:1, C_ID:C_ID + 1], func)

            for i in range(len(preps)):
                v, hi, lo, scale = prep_view(i)
                act.wait_ge(prep_full, i + 1)
                nc.scalar.activation(hi, v, ACT.Copy, scale=scale).then_inc(prep_hi, 1)

            def img(b, k):
                act.wait_ge(S[f"xin{k % 2}"], due(f"xin{k % 2}", b, (k // 2 + 1) * XIN))
                if k == 0:
                    act.wait_ge(S["emb_full"], due("emb_full", b - 1, 2))
                nc.scalar.activation(XS[0:96, 0, CW // 2 * k:CW // 2 * (k + 1)], ximg[0:96, k % 2, 0:CW:2],
                                     ACT.Copy).then_inc(S["img_hi"], 1)

            def stage(i):
                v, hi, lo, scale = stage_views(i)
                act.wait_ge(stg_in[i % 4], 32 * (i // 4 + 1))
                nc.scalar.activation(hi, v, ACT.Copy, scale=scale).then_inc(stg_hi, 1)

            img(0, 0)
            img(0, 1)
            for i in range(EARLY):
                stage(i)
            act.wait_ge(c_set, 1)

            def tr(b, i):
                dst = XM if i == 2 else XT
                act.wait_ge(S["tr_full"], due("tr_full", b, 2 * i + 1))
                nc.scalar.activation(dst[:, 0, :], bank("tr", 2 * i)[:, 0:T], ACT.Copy).then_inc(S["tr_hi"], 1)
                act.wait_ge(S["tr_full"], due("tr_full", b, 2 * i + 2))
                nc.scalar.activation(trm, bank("tr", 2 * i + 1)[:, 0:T], ACT.Identity,
                                     scale=m64).then_inc(S["tr_hi"], 1)

            def qk1(b, i):
                for j in range(2):
                    act.wait_ge(S["rope_sum"], due("rope_sum", b, 2 * i + j + 1))
                    nc.scalar.activation(QK1[:, 2 * i + j, 0, :], tmp[:, 4 * i + j, :],
                                         ACT.Copy).then_inc(S["rope_hi"], 1)

            def v1(b):
                for t in range(NT):
                    act.wait_ge(S["v1_full"], due("v1_full", b, t + 1))
                    nc.scalar.activation(V1[:, 0, t, :], bank("v1", t)[0:TP, 0:D], ACT.Copy).then_inc(S["v1_hi"], 1)

            def s1(b):
                load_table(ACT.Exp, 3)
                act.wait_ge(S["m1_ready"], due("m1_ready", b, 1))
                for t in range(NT):
                    w = TP * (t + 1)
                    nc.scalar.activation(S1[:, t, 0:w], S1[:, t, 0:w], ACT.Exp, bias=nm1[:, 1, t:t + 1], scale=SCALE1,
                                         accum_out=nm1[:, 2, t:t + 1]).then_inc(S["p1_ready"], 1)

            def p1t(b):
                for kt in range(NT):
                    act.wait_ge(S["p1t_full"], due("p1t_full", b, kt + 1))
                    nc.scalar.activation(PT[:, 0, 0, kt, TP * kt:T], bank("p1t", kt)[0:TP, TP * kt:T],
                                         ACT.Copy).then_inc(S["p1t_hi"], 1)

            def qk2(b, i):
                for j in (2 * i, 2 * i + 1):
                    mask = mq if j < 6 else mk
                    act.wait_ge(S["qk2_full"], due("qk2_full", b, j + 1))
                    act.wait_ge(S["qk2_done"], due("qk2_done", b, j - 1))
                    nc.scalar.activation(qm[:, j % 2, :], bank("qk2", j)[:, 0:T], ACT.Identity, scale=mask,
                                         bias=qkmb[:, j:j + 1]).then_inc(S["qk2_m"], 1)

            def v2(b):
                for t in range(NT):
                    act.wait_ge(S["v2_full"], due("v2_full", b, t + 1))
                    nc.scalar.activation(Vp[:, 0, t, :, 0:HD],
                                         bank("v2", t)[0:TP, 0:D].rearrange("p (h d) -> p h d", h=HEADS),
                                         ACT.Copy).then_inc(S["v2_hi"], 1)

            def scale(b, g):
                act.wait_ge(S["pv_norm"], due("pv_norm", b, g + 1))
                nc.scalar.activation(Os[:, 0, g, :], rsq[:, :], ACT.Identity,
                                     bias=vb[:, g:g + 1]).then_inc(S["o_hi"], 1)

            def att2(b, h):
                if h % 4 == 0:
                    load_table(ACT.Exp, h // 4)
                for kt in range(3):
                    n = 3 * h + kt
                    act.wait_ge(S["st_full"], due("st_full", b, n + 1))
                    if kt == 2:
                        act.wait_ge(S["pt_lo2"], due("pt_lo2", b, h - 1))
                    else:
                        act.wait_ge(S["pt_lo"], due("pt_lo", b, 2 * (h - 2) + kt + 1))
                    nc.scalar.activation(Pr[:, n % 6, :], bank("st", n)[0:TP, 0:T], ACT.Exp,
                                         scale=SCALE2).then_inc(S["st_exp"], 1)
                act.wait_ge(S["pv_done"], due("pv_done", b, h - 2))
                nc.scalar.activation(PT[:, h % 3, 0, 2, :], bank("st", n)[0:TP, 0:T], ACT.Exp,
                                     scale=SCALE2).then_inc(S["pt_hi2"], 1)

            def gate(b):
                act.wait_ge(S["gate_tanh_in"], due("gate_tanh_in", b, 1))
                nc.scalar.activation(rs[:, 6, :], rs[:, 5, :], ACT.Tanh, scale=0.5).then_inc(S["gate_tanh"], 1)

            def w1_gelu(m, e, c, after_exp):
                n = NC * e + c
                if after_exp:
                    load_table(ACT.Gelu, 4 + c % 4)
                act.wait_ge(S["w1_full"], due("w1_full", m, n + 1))
                if n % 3 == 2:
                    act.wait_ge(S["h_lo2"], due("h_lo2", m, n // 3))
                else:
                    act.wait_ge(S["h_lo"], due("h_lo", m, dve_low(n - 2)))
                nc.scalar.activation(h32[:, n % 3, :], M[n % 2][:, 0:T], ACT.Gelu, bias=b1s[:, e, c:c + 1],
                                     scale=1.0 / WSC).then_inc(S["gelu"], 1)
                if c == 0:
                    act.wait_ge(S["o_full"], due("o_full", m, 3 * (e - 1)))
                act.wait_ge(S["gelu"], due("gelu", m, n + 1))
                nc.scalar.activation(Hs[:, e % 2, 0, c, :], h32[:, n % 3, :], ACT.Copy).then_inc(S["h_hi"], 1)

            def turn(b, m, ahead=True):
                after_exp = False
                for step in order(m is not None, b is not None, ahead):
                    kind = step[0]
                    if kind == "W1":
                        w1_gelu(m, step[1], step[2], after_exp)
                        after_exp = False
                    elif kind == "img":
                        img(b + 1, step[1])
                    elif kind == "stage":
                        stage(EARLY + step[1])
                    elif kind == "tr":
                        tr(b, step[1])
                    elif kind == "qk1":
                        qk1(b, step[1])
                    elif kind == "v1":
                        v1(b)
                    elif kind == "s1":
                        s1(b)
                        after_exp = True
                    elif kind == "p1t":
                        p1t(b)
                    elif kind == "qk2":
                        qk2(b, step[1])
                    elif kind == "v2":
                        v2(b)
                    elif kind == "att2":
                        att2(b, step[1])
                        after_exp = True
                    elif kind == "scale":
                        scale(b, step[1])
                    elif kind == "gate":
                        gate(b)

            for k in range(2, CHUNKS):
                img(0, k)
            turn(0, None)
            with act.Fori(1, B - 1) as b:
                turn(Batch(b), Batch(b) - 1)
            turn(B - 1, B - 2, False)
            turn(None, B - 1)

        @block.vector
        def _(dve):
            one_ahead(dve, DVE_SIGNALS)
            for i in range(len(preps)):
                v, hi, lo, scale = prep_view(i)
                dve.wait_ge(prep_hi, i + 1)
                if scale == 1.0:
                    nc.vector.tensor_tensor(lo, v, hi, ALU.subtract).then_inc(prep_lo, 1)
                else:
                    nc.vector.scalar_tensor_tensor(lo, v, scale, hi, ALU.mult, ALU.subtract).then_inc(prep_lo, 1)

            def stage(i):
                v, hi, lo, scale = stage_views(i)
                dve.wait_ge(stg_hi, i + 1)
                nc.vector.scalar_tensor_tensor(lo, v, scale, hi, ALU.mult, ALU.subtract).then_inc(stg_lo, 1)

            for i in range(EARLY):
                stage(i)
            dve.wait_ge(c_in, N_C[0])
            nc.vector.tensor_scalar(qkb[:, 6:12], qkb[:, 6:12], cst[:, C_BIG:C_BIG + 1], None,
                                    ALU.add).then_inc(bias_set, 1)
            dve.wait_ge(bias_set, 1)
            nc.vector.tensor_scalar(qkmb[:, 0:6], qkb[:, 0:6], mq, None, ALU.mult)
            nc.vector.tensor_scalar(qkmb[:, 6:12], qkb[:, 6:12], mk, None, ALU.mult).then_inc(c_set, 1)

            steps = [0]

            def step_done(b, ins):
                ins.then_inc(S["dve_step"], 1)
                steps[0] += 1

            def stats(b, src):
                for t in range(NT):
                    step_done(b, nc.vector.bn_stats(st6[:, t, :], src[:, t, :]))
                dve.wait_ge(S["dve_step"], due("dve_step", b, steps[0]))
                apart(dve)
                for t in range(NT):
                    last = nc.vector.bn_aggr(mv[:, t, :], st6[:, t, :])
                last.then_inc(S["ln_var"], 1)

            def norm_affine(b, src, w):
                for t in range(NT):
                    step_done(b, nc.vector.scalar_tensor_tensor(Nrm[:, t, :], src[:, t, :], mv[:, t, 0:1],
                                                                norms[:, w, :], ALU.subtract, ALU.mult))
                dve.wait_ge(S["dve_step"], due("dve_step", b, steps[0]))
                for t in range(NT):
                    last = nc.vector.scalar_tensor_tensor(Nrm[:, t, :], Nrm[:, t, :], rstd[:, t:t + 1],
                                                          norms[:, w + 1, :], ALU.mult, ALU.add)
                last.then_inc(S["n_ready"], 1)

            def emb(b):
                dve.wait_ge(S["r_sum"], due("r_sum", b - 1, 1))
                for t, rows in ((0, TP), (1, PT1)):
                    dve.wait_ge(S["emb_full"], due("emb_full", b, t + 1))
                    nc.vector.scalar_tensor_tensor(Hres[0:rows, t, :], bank("emb", t)[0:rows, 0:D], 1.0 / WSC,
                                                   tokb[0:rows, :], ALU.mult, ALU.add).then_inc(S["emb_evac"], 1)
                dve.wait_ge(S["emb_evac"], due("emb_evac", b, 2))
                dve.wait_ge(S["txt_in"], due("txt_in", b, 32))
                stats(b, Hres)

            def ln(b, i):
                dve.wait_ge(S["ln_rstd"], due("ln_rstd", b, i + 1))
                if i == 0:
                    dve.wait_ge(S["tr_full"], due("tr_full", b - 1, 6))
                    for t in range(NT):
                        last = nc.vector.tensor_scalar(Nrm[:, t, :], Hres[:, t, :], mv[:, t, 0:1], rstd[:, t:t + 1],
                                                       ALU.subtract, ALU.mult)
                    last.then_inc(S["n_ready"], 1)
                elif i == 1:
                    for t in range(NT):
                        last = nc.vector.tensor_scalar(XF[:, t, :], Hres[:, t, :], mv[:, t, 0:1], rstd[:, t:t + 1],
                                                       ALU.subtract, ALU.mult)
                    last.then_inc(S["xf_ready"], 1)
                    dve.wait_ge(S["xf_ready"], due("xf_ready", b, 1))
                    stats(b, XF)
                else:
                    norm_affine(b, XF, 2 * (i - 2))

            def tr(b, i):
                dst = XM if i == 2 else XT
                dve.wait_ge(S["tr_hi"], due("tr_hi", b, 2 * i + 1))
                nc.vector.tensor_tensor(dst[:, 1, :], bank("tr", 2 * i)[:, 0:T], dst[:, 0, :],
                                        ALU.subtract).then_inc(S["tr_lo"], 1)
                dve.wait_ge(S["tr_hi"], due("tr_hi", b, 2 * i + 2))
                nc.vector.tensor_tensor(dst[:, 2, :], bank("tr", 2 * i + 1)[:, 0:T], trm,
                                        ALU.subtract).then_inc(S["tr_lo"], 1)

            def qk1(b, i):
                re, im = bank("qk1", 2 * i)[0:RH, 0:T], bank("qk1", 2 * i + 1)[0:RH, 0:T]
                dve.wait_ge(S["qk1_full"], due("qk1_full", b, 2 * i + 1))
                nc.vector.tensor_tensor(tmp[:, 4 * i, :], re, cos, ALU.mult)
                nc.vector.tensor_tensor(tmp[:, 4 * i + 1, :], re, sin, ALU.mult).then_inc(S["rope_re"], 1)
                dve.wait_ge(S["qk1_full"], due("qk1_full", b, 2 * i + 2))
                nc.vector.tensor_tensor(tmp[:, 4 * i + 2, :], im, sin, ALU.mult)
                nc.vector.tensor_tensor(tmp[:, 4 * i + 3, :], im, cos, ALU.mult).then_inc(S["rope_mul"], 1)

            def v1(b):
                for t in range(NT):
                    dve.wait_ge(S["v1_hi"], due("v1_hi", b, t + 1))
                    nc.vector.tensor_tensor(V1[:, 1, t, :], bank("v1", t)[0:TP, 0:D], V1[:, 0, t, :],
                                            ALU.subtract).then_inc(S["v1_lo"], 1)

            def s1(b):
                for t in range(NT):
                    ps = bank("s1", t)
                    dve.wait_ge(S["s1_full"], due("s1_full", b, t + 1))
                    if t:
                        nc.vector.tensor_copy(S1[:, t, 0:TP * t], ps[0:TP, 0:TP * t])
                    nc.vector.tensor_tensor(S1[:, t, TP * t:TP * t + TP], ps[0:TP, TP * t:TP * t + TP], cap,
                                            ALU.min).then_inc(S["s1_evac"], 1)
                dve.wait_ge(S["s1_evac"], due("s1_evac", b, 3))
                for t in range(NT):
                    step_done(b, nc.vector.tensor_reduce(nm1[:, 0, t:t + 1], S1[:, t, 0:TP * (t + 1)], AX.X, ALU.max))
                dve.wait_ge(S["dve_step"], due("dve_step", b, steps[0]))
                nc.vector.tensor_scalar(nm1[:, 1, :], nm1[:, 0, :], -SCALE1, None, ALU.mult).then_inc(S["m1_ready"], 1)

            def p1t(b):
                for kt in range(NT):
                    dve.wait_ge(S["p1t_hi"], due("p1t_hi", b, kt + 1))
                    nc.vector.tensor_tensor(PT[:, 0, 1, kt, TP * kt:T], bank("p1t", kt)[0:TP, TP * kt:T],
                                            PT[:, 0, 0, kt, TP * kt:T], ALU.subtract).then_inc(S["p1t_lo"], 1)
                dve.wait_ge(S["p1_ready"], due("p1_ready", b, 3))
                step_done(b, nc.vector.reciprocal(nm1[:, 3, :], nm1[:, 2, :]))
                dve.wait_ge(S["dve_step"], due("dve_step", b, steps[0]))

            def pv1(b):
                for t in range(NT):
                    dve.wait_ge(S["pv1_full"], due("pv1_full", b, t + 1))
                    nc.vector.scalar_tensor_tensor(Hres[:, t, :], bank("pv1", t)[0:TP, 0:D], nm1[:, 3, t:t + 1],
                                                   Hres[:, t, :], ALU.mult, ALU.add).then_inc(S["pv1_evac"], 1)
                dve.wait_ge(S["pv1_evac"], due("pv1_evac", b, 3))
                stats(b, Hres)

            def qk2(b, i):
                for j in (2 * i, 2 * i + 1):
                    dve.wait_ge(S["qk2_m"], due("qk2_m", b, j + 1))
                    nc.vector.scalar_tensor_tensor(QK[:, j, :], bank("qk2", j)[:, 0:T], qkb[:, j:j + 1], qm[:, j % 2, :],
                                                   ALU.add, ALU.subtract).then_inc(S["qk2_done"], 1)

            def v2(b):
                for t in range(NT):
                    dve.wait_ge(S["v2_hi"], due("v2_hi", b, t + 1))
                    nc.vector.tensor_tensor(Vp[:, 1, t, :, 0:HD],
                                            bank("v2", t)[0:TP, 0:D].rearrange("p (h d) -> p h d", h=HEADS),
                                            Vp[:, 0, t, :, 0:HD], ALU.subtract).then_inc(S["v2_lo"], 1)

            def s(b, h):
                at = h // 4 * 4 + h % 2 * 2 + h // 2 % 2
                for qt in range(NT):
                    n = 3 * h + qt
                    dve.wait_ge(S["s_full"], due("s_full", b, n + 1))
                    nc.vector.tensor_reduce(mx[:, qt, at:at + 1], bank("s", n)[0:TP, 0:T], AX.X,
                                            ALU.max).then_inc(S["s_max"], 1)

            def mt(b, g):
                dve.wait_ge(S["mt_full"], due("mt_full", b, g + 1))
                dve.wait_ge(S["nm_in"], due("nm_in", b, 32 * g))
                nc.vector.tensor_scalar(nmT[:, :], bank("mt", g)[0:4, 0:T], -1.0 / BIG, None,
                                        ALU.mult).then_inc(S["mt_done"], 1)

            def norm(b, g):
                ps = bank("pv", g)[:, 0:T]
                dve.wait_ge(S["pv_done"], due("pv_done", b, 4 * g + 4))
                apart(dve)
                nc.vector.stream_shuffle(rsi[:, :], ps, [16 + i % 16 for i in range(32)]).then_inc(S["sum_out"], 1)
                dve.wait_ge(S["sum_out"], due("sum_out", b, g + 1))
                nc.vector.reciprocal(rsi[:, :], rsi[:, :]).then_inc(S["sum_inv"], 1)

            def scale(b, g):
                dve.wait_ge(S["sum_inv"], due("sum_inv", b, g + 1))
                nc.vector.tensor_tensor(rsq[:, :], bank("pv", g)[:, 0:T], rsi[:, :], ALU.mult).then_inc(S["pv_norm"], 1)

            def o_split(b, g):
                dve.wait_ge(S["o_hi"], due("o_hi", b, g + 1))
                nc.vector.scalar_tensor_tensor(Os[:, 1, g, :], rsq[:, :], vb[:, g:g + 1], Os[:, 0, g, :],
                                               ALU.add, ALU.subtract).then_inc(S["o_lo"], 1)

            def att2(b, h):
                dve.wait_ge(S["pv_done"], due("pv_done", b, h - 2))
                for kt in range(2):
                    n = 3 * h + kt
                    dve.wait_ge(S["st_exp"], due("st_exp", b, n + 1))
                    nc.vector.tensor_copy(PT[:, h % 3, 0, kt, :], Pr[:, n % 6, :]).then_inc(S["pt_hi"], 1)
                dve.wait_ge(S["pt_hi"], due("pt_hi", b, 2 * h + 2))
                for kt in range(2):
                    n = 3 * h + kt
                    nc.vector.tensor_tensor(PT[:, h % 3, 1, kt, :], Pr[:, n % 6, :], PT[:, h % 3, 0, kt, :],
                                            ALU.subtract).then_inc(S["pt_lo"], 1)

            def pj(b):
                dve.wait_ge(S["xfb_ready"], due("xfb_ready", b, 1))
                for t in range(NT):
                    dve.wait_ge(S["pj_full"], due("pj_full", b, t + 1))
                    nc.vector.scalar_tensor_tensor(XF[:, t, :], bank("pj", t)[0:TP, 0:D], 1.0 / WSC, R[:, t, :],
                                                   ALU.mult, ALU.add).then_inc(S["x1_done"], 1)
                dve.wait_ge(S["x1_done"], due("x1_done", b, 3))
                stats(b, XF)

            def gate(b):
                def wide(ap):
                    return ap.rearrange("p (t a) -> p t a", a=1).to_broadcast([TP, NT, E])

                L, eq, c1, one1, L2, one2 = (rt[:, i] for i in range(6))
                top1, first1, top2, first2 = (rs[:, i, :] for i in range(4))
                dve.wait_ge(S["gate_full"], due("gate_full", b, 1))
                nc.vector.tensor_scalar(L, bank("gate", 0)[0:TP, 0:NT * E].rearrange("p (t e) -> p t e", e=E),
                                        1.0 / WSC, None, ALU.mult).then_inc(S["gate_evac"], 1)
                dve.wait_ge(S["gate_evac"], due("gate_evac", b, 1))
                for src, top, first, one in ((L, top1, first1, one1), (L2, top2, first2, one2)):
                    step_done(b, nc.vector.tensor_reduce(top, src, AX.X, ALU.max))
                    dve.wait_ge(S["dve_step"], due("dve_step", b, steps[0]))
                    step_done(b, nc.vector.tensor_tensor(eq, src, wide(top), ALU.is_ge))
                    dve.wait_ge(S["dve_step"], due("dve_step", b, steps[0]))
                    step_done(b, nc.vector.tensor_tensor(c1, eq, rev, ALU.mult))
                    dve.wait_ge(S["dve_step"], due("dve_step", b, steps[0]))
                    step_done(b, nc.vector.tensor_reduce(first, c1, AX.X, ALU.max))
                    dve.wait_ge(S["dve_step"], due("dve_step", b, steps[0]))
                    step_done(b, nc.vector.tensor_tensor(one, c1, wide(first), ALU.is_equal))
                    dve.wait_ge(S["dve_step"], due("dve_step", b, steps[0]))
                    if one is one1:
                        step_done(b, nc.vector.scalar_tensor_tensor(L2, one1, -3.0e38, L, ALU.mult, ALU.add))
                        dve.wait_ge(S["dve_step"], due("dve_step", b, steps[0]))
                nc.vector.tensor_tensor(rs[:, 5, :], top1, top2, ALU.subtract).then_inc(S["gate_tanh_in"], 1)
                dve.wait_ge(S["gate_tanh"], due("gate_tanh", b, 1))
                step_done(b, nc.vector.tensor_scalar(rs[:, 4, :], rs[:, 6, :], 0.5, 0.5, ALU.mult, ALU.add))
                step_done(b, nc.vector.tensor_scalar(rs[:, 7, :], rs[:, 6, :], -0.5, 0.5, ALU.mult, ALU.add))
                dve.wait_ge(S["dve_step"], due("dve_step", b, steps[0]))
                step_done(b, nc.vector.tensor_tensor(eq, one1, wide(rs[:, 4, :]), ALU.mult))
                step_done(b, nc.vector.tensor_tensor(c1, one2, wide(rs[:, 7, :]), ALU.mult))
                dve.wait_ge(S["dve_step"], due("dve_step", b, steps[0]))
                nc.vector.tensor_tensor(G[:, :, :], eq, c1, ALU.add).then_inc(S["g_ready"], 1)

            def gt(b):
                dve.wait_ge(S["gt_full"], due("gt_full", b, 1))
                nc.vector.tensor_copy(GT, bank("gt", 0)[0:E, 0:T]).then_inc(S["gt_done"], 1)

            def b2_step(b):
                dve.wait_ge(S["g_ready"], due("g_ready", b, 1))
                dve.wait_ge(S["acc"], due("acc", b - 1, 24))
                nc.vector.tensor_scalar(Gs[:, :, :], G[:, :, :], 1.0 / WSC, None, ALU.mult)
                dve.wait_ge(S["r_sum"], due("r_sum", b, 1))
                for t in range(NT):
                    dve.wait_ge(S["b2_full"], due("b2_full", b, t + 1))
                    nc.vector.tensor_tensor(R[:, t, :], bank("b2", t)[0:TP, 0:D], R[:, t, :],
                                            ALU.add).then_inc(S["r_ready"], 1)

            def h_low(m, n):
                e, c = n // NC, n % NC
                dve.wait_ge(S["h_hi"], due("h_hi", m, n + 1))
                nc.vector.tensor_tensor(Hs[:, e % 2, 1, c, :], h32[:, n % 3, :], Hs[:, e % 2, 0, c, :],
                                        ALU.subtract).then_inc(S["h_lo"], 1)

            def w2_acc(m, e, t):
                if t == 0:
                    return
                if e == 0 and t == 1:
                    dve.wait_ge(S["out_done"], due("out_done", m, 0))
                    dve.wait_ge(S["r_ready"], due("r_ready", m, 3))
                else:
                    dve.wait_ge(S["acc"], due("acc", m, 3 * e - 3 + (2 if t == 1 else 3)))
                dve.wait_ge(S["o_full"], due("o_full", m, 3 * e + t + 1))
                for u in ((0, 1) if t == 1 else (2,)):
                    ps = O[0][0:TP, D * u:D * u + D] if u < 2 else O[1][0:TP, 0:D]
                    nc.vector.scalar_tensor_tensor(ACC[:, u, :], ps, Gs[:, u, e:e + 1],
                                                   (R if e == 0 else ACC)[:, u, :], ALU.mult,
                                                   ALU.add).then_inc(S["acc"], 1)

            def turn(b, m, ahead=True):
                steps[0] = 0
                chunk = None
                for step in order(m is not None, b is not None, ahead):
                    kind = step[0]
                    if kind in ("W1", "W2"):
                        if chunk is not None and chunk % 3 < 2:
                            h_low(m, chunk)
                        chunk = NC * step[1] + step[2] if kind == "W1" else None
                    if kind == "W2":
                        w2_acc(m, step[1], step[2])
                    elif kind == "emb":
                        emb(b)
                    elif kind == "ln":
                        ln(b, step[1])
                    elif kind == "norm":
                        norm(b, step[1])
                    elif kind == "scale":
                        scale(b, step[1])
                    elif kind == "osplit":
                        o_split(b, step[1])
                    elif kind == "stage":
                        stage(EARLY + step[1])
                    elif kind == "tr":
                        tr(b, step[1])
                    elif kind == "qk1":
                        qk1(b, step[1])
                    elif kind == "v1":
                        v1(b)
                    elif kind == "s1":
                        s1(b)
                    elif kind == "p1t":
                        p1t(b)
                    elif kind == "pv1":
                        pv1(b)
                    elif kind == "qk2":
                        qk2(b, step[1])
                    elif kind == "v2":
                        v2(b)
                    elif kind == "s":
                        s(b, step[1])
                    elif kind == "mt":
                        mt(b, step[1])
                    elif kind == "att2":
                        att2(b, step[1])
                    elif kind == "pj":
                        pj(b)
                    elif kind == "gate":
                        gate(b)
                    elif kind == "gt":
                        gt(b)
                    elif kind == "b2":
                        b2_step(b)
                assert b is None or steps[0] == DVE_STEPS, steps[0]

            turn(0, None)
            with dve.Fori(1, B - 1) as b:
                turn(Batch(b), Batch(b) - 1)
            turn(B - 1, B - 2, False)
            turn(None, B - 1)

        @block.tensor
        def _(pe):
            one_ahead(pe, PE_SIGNALS)
            pe.wait_ge(c_in, 16)
            pe.wait_ge(big_in, 128)

            def turn_twice(ps, c0, src, n):
                nc.tensor.transpose(ps[:, c0:c0 + n], src[:, D - 128:D], ident[0:n, 0:n])
                return nc.tensor.transpose(ps[0:KB, c0:c0 + n], src[:, KA:D], ident[0:n, 0:n])

            for i, (kind, at, rows, cols, _hi, _lo, _sc) in enumerate(preps):
                ps = TB[i % 3]
                if i >= 3:
                    pe.wait_ge(prep_lo, i - 2)
                if kind == "tok":
                    pe.wait_ge(tok_dup, i + 1)
                    for n in range(4):
                        last = nc.tensor.transpose(ps[0:96, 96 * n:96 * n + 96], tokD[:, i % 2, n, :], ident[0:96, 0:96])
                elif kind == "qkva":
                    for a in range(2):
                        last = nc.tensor.transpose(ps[:, 96 * a:96 * a + 96], qkvS[:, 2 * at + a, 0:KA], ident[0:96, 0:96])
                elif kind == "qkvb":
                    for a in range(2):
                        last = turn_twice(ps, 96 * a, qkvS[:, 2 * at + a, :], 96)
                else:
                    for g in range(3):
                        last = nc.tensor.transpose(ps[:, 96 * g:96 * g + 96], projS[:, at, g, :], ident[0:96, 0:96])
                last.then_inc(prep_full, 1)
            pe.wait_ge(c_set, 1)
            pe.wait_ge(stg_lo, EARLY)
            pe.wait_ge(pad_set, 9)

            def five(out_ap, pairs):
                for i, (lhsT, rhs) in enumerate(pairs):
                    last = nc.tensor.matmul(out_ap, lhsT, rhs, start=(i == 0), stop=(i == len(pairs) - 1))
                return last

            def emb(b):
                pe.wait_ge(S["img_split"], due("img_split", b, CHUNKS))
                xv = XS[0:96, :, :].rearrange("p s (t w) -> p s w t", w=PATCH // 2)
                for t, n in ((0, TP), (1, PT1)):
                    pe.wait_ge(*bank_read(b, "emb", t))
                    five(bank("emb", t)[0:n, 0:D],
                         [(xv[:, xs, w, TP * t:TP * t + n], tokW[0:96, ws, w, :])
                          for w in range(PATCH // 2) for xs, ws in ((0, 0), (0, 1), (1, 0))]
                         ).then_inc(S["emb_full"], 1)

            def tr(b, i):
                pe.wait_ge(S["n_ready"], due("n_ready", b, i + 1))
                pe.wait_ge(*bank_read(b, "tr", 2 * i))
                for t in range(NT):
                    last = nc.tensor.transpose(bank("tr", 2 * i)[:, TP * t:TP * t + TP], Nrm[:, t, 0:KA],
                                               ident[0:TP, 0:TP])
                last.then_inc(S["tr_full"], 1)
                pe.wait_ge(*bank_read(b, "tr", 2 * i + 1))
                for t in range(NT):
                    last = turn_twice(bank("tr", 2 * i + 1), TP * t, Nrm[:, t, :], TP)
                last.then_inc(S["tr_full"], 1)

            def by_weight(wa, wb, pick, X):
                return [(pick(wa, 0), X[:, 0, :]), (pick(wa, 1), X[:, 0, :]), (pick(wa, 0), X[:, 1, :]),
                        (pick(wb, 0), X[:, 2, :]), (pick(wb, 1), X[:, 2, :])]

            def by_token(wa, wb, pick, X, t):
                c = slice(TP * t, TP * t + TP)
                return [(X[:, 0, c], pick(wa, 0)), (X[:, 0, c], pick(wa, 1)), (X[:, 1, c], pick(wa, 0)),
                        (X[:, 2, c], pick(wb, 0)), (X[:, 2, c], pick(wb, 1))]

            def qk1(b, i):
                if i == 0:
                    pe.wait_ge(S["tr_lo"], due("tr_lo", b, 2))
                for j in (2 * i, 2 * i + 1):
                    pe.wait_ge(*bank_read(b, "qk1", j))
                    five(bank("qk1", j)[0:RH, 0:T],
                         by_weight(attWa, attWb, lambda w, s: w[:, s, RH * j:RH * j + RH], XT)
                         ).then_inc(S["qk1_full"], 1)

            def v1(b):
                for t in range(NT):
                    pe.wait_ge(*bank_read(b, "v1", t))
                    five(bank("v1", t)[0:TP, 0:D], by_token(attWa, attWb, lambda w, s: w[:, s, 2 * D:3 * D], XT, t)
                         ).then_inc(S["v1_full"], 1)

            def s1(b):
                pe.wait_ge(S["rope_lo"], due("rope_lo", b, 4))
                for t in range(NT):
                    w = TP * (t + 1)
                    pe.wait_ge(*bank_read(b, "s1", t))
                    five(bank("s1", t)[0:TP, 0:w],
                         [(QK1[:, j, qs, TP * t:w], QK1[:, 2 + j, ks, 0:w])
                          for j in range(2) for qs, ks in ((0, 0), (0, 1), (1, 0))]).then_inc(S["s1_full"], 1)

            def p1t(b):
                pe.wait_ge(S["p1_ready"], due("p1_ready", b, 3))
                for kt in range(NT):
                    pe.wait_ge(*bank_read(b, "p1t", kt))
                    for qt in range(kt, NT):
                        last = nc.tensor.transpose(bank("p1t", kt)[0:TP, TP * qt:TP * qt + TP],
                                                   S1[:, qt, TP * kt:TP * kt + TP], ident[0:TP, 0:TP])
                    last.then_inc(S["p1t_full"], 1)

            def pv1(b):
                pe.wait_ge(S["p1t_lo"], due("p1t_lo", b, 3))
                pe.wait_ge(S["v1_lo"], due("v1_lo", b, 3))
                for t in range(NT):
                    pe.wait_ge(*bank_read(b, "pv1", t))
                    five(bank("pv1", t)[0:TP, 0:D],
                         [(PT[:, 0, ps, kt, TP * t:TP * t + TP], V1[:, vs, kt, :])
                          for kt in range(t + 1) for ps, vs in ((0, 0), (0, 1), (1, 0))]).then_inc(S["pv1_full"], 1)

            def qk2(b, i):
                if i == 0:
                    pe.wait_ge(S["tr_lo"], due("tr_lo", b, 4))
                for j in (2 * i, 2 * i + 1):
                    pe.wait_ge(*bank_read(b, "qk2", j))
                    five(bank("qk2", j)[:, 0:T],
                         by_weight(qkvWa, qkvWb, lambda w, s: w[:, s, 128 * j:128 * j + 128], XT)
                         ).then_inc(S["qk2_full"], 1)

            def v2(b):
                for t in range(NT):
                    pe.wait_ge(*bank_read(b, "v2", t))
                    five(bank("v2", t)[0:TP, 0:D], by_token(qkvWa, qkvWb, lambda w, s: w[:, s, 1536:1536 + D], XT, t)
                         ).then_inc(S["v2_full"], 1)

            def s(b, h):
                if h == 0:
                    pe.wait_ge(S["qk2_done"], due("qk2_done", b, 12))
                r = slice(64 * (h % 2), 64 * (h % 2) + 64)
                for qt in range(NT):
                    pe.wait_ge(*bank_read(b, "s", 3 * h + qt))
                    nc.tensor.matmul(bank("s", 3 * h + qt)[0:TP, 0:T], QK[r, h // 2, TP * qt:TP * qt + TP],
                                     QK[r, 6 + h // 2, :], start=True, stop=True).then_inc(S["s_full"], 1)

            def mt(b, g):
                pe.wait_ge(S["s_max"], due("s_max", b, 12 * g + 12))
                pe.wait_ge(*bank_read(b, "mt", g))
                for qt in range(NT):
                    last = nc.tensor.transpose(bank("mt", g)[0:4, TP * qt:TP * qt + TP], mx[:, qt, 4 * g:4 * g + 4],
                                               ident[0:TP, 0:TP])
                last.then_inc(S["mt_full"], 1)

            def st(b, h):
                if h % 4 == 0:
                    pe.wait_ge(S["nm_in"], due("nm_in", b, 32 * (h // 4 + 1)))
                r = slice(64 * (h % 2), 64 * (h % 2) + 64)
                for kt in range(3):
                    n = 3 * h + kt
                    pe.wait_ge(*bank_read(b, "st", n))
                    ps = bank("st", n)[0:TP, 0:T]
                    nc.tensor.matmul(ps, QK[r, 6 + h // 2, TP * kt:TP * kt + TP], QK[r, h // 2, :],
                                     start=True, stop=True).then_inc(S["st_full"], 1)

            def pv(b, h):
                j, g = h % 4, h // 4
                if h == 0:
                    pe.wait_ge(S["v2_lo"], due("v2_lo", b, 3))
                if j == 0:
                    pe.wait_ge(*bank_read(b, "pv", g))
                pe.wait_ge(S["pt_lo"], due("pt_lo", b, 2 * h + 2))
                pe.wait_ge(S["pt_lo2"], due("pt_lo2", b, h + 1))
                ps = bank("pv", g)[32 * j:32 * j + 32, 0:T]
                for kt in range(3):
                    for p_, v_ in ((0, 0), (0, 1), (1, 0)):
                        last = nc.tensor.matmul(ps, Vp[:, v_, kt, h, :], PT[:, h % 3, p_, kt, :],
                                                start=(kt == 0 and (p_, v_) == (0, 0)),
                                                stop=(kt == 2 and (p_, v_) == (1, 0)))
                last.then_inc(S["pv_done"], 1)

            def pj(b):
                pe.wait_ge(S["o_lo"], due("o_lo", b, 3))
                for t in range(NT):
                    c = slice(TP * t, TP * t + TP)
                    pe.wait_ge(*bank_read(b, "pj", t))
                    five(bank("pj", t)[0:TP, 0:D],
                         [(Os[:, s_, g, c], projW[:, w_, g, :]) for g in range(3) for s_, w_ in ((0, 0), (0, 1), (1, 0))]
                         ).then_inc(S["pj_full"], 1)

            def gate(b):
                pe.wait_ge(S["tr_lo"], due("tr_lo", b, 6))
                pe.wait_ge(*bank_read(b, "gate", 0))
                for t in range(NT):
                    last = five(bank("gate", 0)[0:TP, E * t:E * t + E],
                                by_token(gateWa, gateWb, lambda w, s: w[:, s, :], XM, t))
                last.then_inc(S["gate_full"], 1)

            def gt(b):
                pe.wait_ge(S["g_ready"], due("g_ready", b, 1))
                pe.wait_ge(*bank_read(b, "gt", 0))
                for t in range(NT):
                    last = nc.tensor.transpose(bank("gt", 0)[0:E, TP * t:TP * t + TP], G[:, t, :], ident[0:TP, 0:TP])
                last.then_inc(S["gt_full"], 1)

            def b2_step(b):
                pe.wait_ge(S["gt_done"], due("gt_done", b, 1))
                for t in range(NT):
                    pe.wait_ge(*bank_read(b, "b2", t))
                    nc.tensor.matmul(bank("b2", t)[0:TP, 0:D], GT[:, TP * t:TP * t + TP], b2s[:, :],
                                     start=True, stop=True).then_inc(S["b2_full"], 1)

            def w1_chunk(m, e, c):
                n = NC * e + c
                if n == 0:
                    pe.wait_ge(S["tr_lo"], due("tr_lo", m, 6))
                pe.wait_ge(S["gelu"], due("gelu", m, n - 1))
                cols = slice(128 * c, 128 * c + 128)
                five(M[n % 2][:, 0:T], by_weight(W1a[:, e], W1b[:, e], lambda w, s: w[:, s, cols], XM)
                     ).then_inc(S["w1_full"], 1)

            def w2_tile(m, e, t):
                if t == 0:
                    pe.wait_ge(S["h_lo"], due("h_lo", m, dve_low(NC * (e + 1))))
                    pe.wait_ge(S["h_lo2"], due("h_lo2", m, NC // 3 * (e + 1)))
                if t != 1:
                    pe.wait_ge(S["acc"], due("acc", m, 3 * (e - 1) + (2 if t == 0 else 3)))
                ps = O[0][0:TP, D * t:D * t + D] if t < 2 else O[1][0:TP, 0:D]
                rows = slice(TP * t, TP * t + TP)
                five(ps, [(Hs[:, e % 2, s_, c, rows], W2s[:, e, c, w_, :])
                          for c in range(NC) for s_, w_ in ((0, 0), (0, 1), (1, 0))]).then_inc(S["o_full"], 1)

            def turn(b, m, ahead=True):
                for step in order(m is not None, b is not None, ahead):
                    kind = step[0]
                    if kind == "W1":
                        w1_chunk(m, step[1], step[2])
                    elif kind == "W2":
                        w2_tile(m, step[1], step[2])
                    elif kind == "emb":
                        emb(b)
                    elif kind == "tr":
                        tr(b, step[1])
                    elif kind == "qk1":
                        qk1(b, step[1])
                    elif kind == "v1":
                        v1(b)
                    elif kind == "s1":
                        s1(b)
                    elif kind == "p1t":
                        p1t(b)
                    elif kind == "pv1":
                        pv1(b)
                    elif kind == "qk2":
                        qk2(b, step[1])
                    elif kind == "v2":
                        v2(b)
                    elif kind == "s":
                        s(b, step[1])
                    elif kind == "mt":
                        mt(b, step[1])
                    elif kind == "att2":
                        st(b, step[1])
                    elif kind == "pv":
                        pv(b, step[1])
                    elif kind == "pj":
                        pj(b)
                    elif kind == "gate":
                        gate(b)
                    elif kind == "gt":
                        gt(b)
                    elif kind == "b2":
                        b2_step(b)

            turn(0, None)
            pe.wait_ge(stg_lo, len(stages))
            with pe.Fori(1, B - 1) as b:
                turn(Batch(b), Batch(b) - 1)
            turn(B - 1, B - 2, False)
            turn(None, B - 1)


_INS = ["x", "txt", "L0_tok_W", "L0_tok_b", "L0_attn_Wq", "L0_attn_Wk", "L0_attn_Wv", "L0_ffn_norm1_w",
        "L0_ffn_norm1_b", "L0_ffn_qkv_w", "L0_ffn_qkv_b", "L0_ffn_proj_w", "L0_ffn_proj_b", "L0_ffn_norm2_w",
        "L0_ffn_norm2_b", "L0_ffn_w_gate", "L0_ffn_W1", "L0_ffn_b1", "L0_ffn_W2", "L0_ffn_b2"]


def shape_constants():
    import numpy as np
    c = np.zeros((128, C_N), np.float32)
    p = np.arange(128)
    c[:, C_ID:C_ID + 128] = np.eye(128, dtype=np.float32)
    c[:, C_M64] = p >= 64
    c[:, C_MQ] = p % 64 >= 32
    c[:, C_MK] = (p % 64 >= HD) & (p % 64 < 2 * HD)
    j = np.arange(RH, dtype=np.float32)
    theta = np.power(np.float32(10000.0), np.float32(-2.0) * j / np.float32(D), dtype=np.float32)
    ang = np.arange(T, dtype=np.float32)[None, :] * theta[:, None]
    c[0:RH, C_COS:C_COS + T] = np.cos(ang)
    c[0:RH, C_SIN:C_SIN + T] = np.sin(ang)
    q, k = np.arange(TP)[:, None], np.arange(TP)[None, :]
    c[0:TP, C_CAP:C_CAP + TP] = np.where(k <= q, 3.0e38, -3.0e38)
    c[:, C_EPS:C_BIG] = EPS
    c[:, C_BIG] = np.where(p % 64 == 3 * HD, BIG, 0.0)
    c[:, C_POW:C_EPS] = -0.5
    c[:, C_REV:C_POW] = np.tile(np.arange(E, 0, -1, dtype=np.float32), NT)[None, :]
    return c


def kernel(**inputs):
    import numpy as np
    import concourse.bacc as bacc
    from concourse.bass_utils import run_bass_kernel_spmd as run

    nc = bacc.Bacc("TRN2", target_bir_lowering=False, num_devices=1)
    nc.disable_value_cache = True
    arrays, args = {}, []
    for name in _INS:
        a = np.ascontiguousarray(inputs[name])
        arrays[f"in_{name}"] = a
        args.append(nc.dram_tensor(f"in_{name}", a.shape, mybir.dt.from_np(a.dtype), kind="ExternalInput").ap())
    arrays["in_const"] = shape_constants()
    args.append(nc.dram_tensor("in_const", (128, C_N), F32, kind="ExternalInput").ap())
    out = nc.dram_tensor("out", (B, T, D), F32, kind="ExternalOutput").ap()
    build_program(nc, *args, out)
    return run(nc, [arrays], core_ids=[0]).results[0]["out"]
```
